# Optimizing a Trainium2 kernel written in Bass

```python
import numpy as np
import jax
import jax.numpy as jnp

def _softmax(x, axis=-1):
    return jax.nn.softmax(x, axis=axis)

def _gelu(x):
    return jax.nn.gelu(x, approximate=True)

def _silu(x):
    return jax.nn.silu(x)

def _sigmoid(x):
    return jax.nn.sigmoid(x)

def _layernorm(x, axis=-1, eps=1e-05):
    m = jnp.mean(x, axis=axis, keepdims=True)
    v = jnp.var(x, axis=axis, keepdims=True)
    return (x - m) / jnp.sqrt(v + eps)

def _scatter_add(tgt, idx, src, axis=0):
    return tgt.at[idx].add(src)

def _segment_sum(src, seg, n):
    return jax.ops.segment_sum(src, seg, n)
kernel_name = 'mk_hybrid_d1_jaxref_r8_ab27fc'

def setup_inputs(seed: int=0):
    np.random.seed(seed)
    _w = jnp.asarray

    def _L0_attn_a_setup():
        import jax, jax.numpy as jnp
        import numpy as np
        from jax import lax
        D_MODEL, D_STATE, EXPAND, K = (128, 16, 2, 4)
        D_INNER = D_MODEL * EXPAND
        B, L = (2, 256)

        def _selective_ssm(x, A_log, D_skip, W_delta, b_delta, W_B, W_C):
            A = -jnp.exp(A_log)
            delta = jax.nn.softplus(x @ W_delta + b_delta)
            Bm = x @ W_B
            Cm = x @ W_C
            h0 = jnp.zeros((x.shape[0], A.shape[0], A.shape[1]), x.dtype)

            def step(h, inp):
                d_t, x_t, B_t, C_t = inp
                dA = jnp.exp(d_t[..., None] * A)
                h = dA * h + (d_t * x_t)[..., None] * B_t[:, None, :]
                y_t = jnp.einsum('bdn,bn->bd', h, C_t)
                return (h, y_t)
            xs = (delta.transpose(1, 0, 2), x.transpose(1, 0, 2), Bm.transpose(1, 0, 2), Cm.transpose(1, 0, 2))
            _, ys = lax.scan(step, h0, xs)
            return ys.transpose(1, 0, 2) + x * D_skip
        key = jax.random.key(seed)
        ks = jax.random.split(key, 16)
        s = lambda fan_in: 1.0 / np.sqrt(fan_in)
        inp = {'x': jax.random.normal(ks[0], (B, L, D_MODEL), jnp.float32), 'W_in': jax.random.normal(ks[1], (D_MODEL, D_INNER), jnp.float32) * s(D_MODEL), 'b_in': jnp.zeros((D_INNER,), jnp.float32), 'W_gate': jax.random.normal(ks[2], (D_MODEL, D_INNER), jnp.float32) * s(D_MODEL), 'b_gate': jnp.zeros((D_INNER,), jnp.float32), 'conv_w': jax.random.normal(ks[3], (D_INNER, 1, K), jnp.float32) * s(K), 'conv_b': jnp.zeros((D_INNER,), jnp.float32), 'A_log': jnp.log(jnp.broadcast_to(jnp.arange(1, D_STATE + 1, dtype=jnp.float32), (D_INNER, D_STATE))), 'D_skip': jnp.ones((D_INNER,), jnp.float32), 'W_delta': jax.random.normal(ks[4], (D_INNER, D_INNER), jnp.float32) * s(D_INNER), 'b_delta': jnp.zeros((D_INNER,), jnp.float32), 'W_B': jax.random.normal(ks[5], (D_INNER, D_STATE), jnp.float32) * s(D_INNER), 'W_C': jax.random.normal(ks[6], (D_INNER, D_STATE), jnp.float32) * s(D_INNER), 'W_out': jax.random.normal(ks[7], (D_INNER, D_MODEL), jnp.float32) * s(D_INNER), 'b_out': jnp.zeros((D_MODEL,), jnp.float32)}
        return inp
    _L0_attn_a_in = _L0_attn_a_setup()

    def _L0_attn_b_setup():
        import jax, jax.numpy as jnp
        import numpy as np
        NUM_HEADS = 16
        STRIDE = 32
        WINDOW = 64

        def _sparse_mask(n: int) -> jnp.ndarray:
            i = jnp.arange(n)[:, None]
            j = jnp.arange(n)[None, :]
            return (j % STRIDE == 0) | (jnp.abs(i - j) <= WINDOW)
        key = jax.random.key(seed)
        k0, k1, k2 = jax.random.split(key, 3)
        d = 128
        return {'x': jax.random.normal(k0, (1, 256, d), dtype=jnp.float32), 'w_qkv': jax.random.normal(k1, (d, 3 * d), dtype=jnp.float32) / np.sqrt(d), 'b_qkv': jnp.zeros((3 * d,), dtype=jnp.float32), 'w_out': jax.random.normal(k2, (d, d), dtype=jnp.float32) / np.sqrt(d), 'b_out': jnp.zeros((d,), dtype=jnp.float32)}
    _L0_attn_b_in = _L0_attn_b_setup()

    def _L0_ffn_setup():
        import jax, jax.numpy as jnp
        import numpy as np
        NUM_EXPERTS = 8
        TOP_K = 2
        DIM = 128
        HIDDEN = 512
        B, S = (4, 256)
        key = jax.random.key(seed)
        ks = jax.random.split(key, 6)
        scale = 0.02
        x = jax.random.normal(ks[0], (B, S, DIM), dtype=jnp.float32)
        wg = jax.random.normal(ks[1], (NUM_EXPERTS, DIM), dtype=jnp.float32) * scale
        bg = jnp.zeros((NUM_EXPERTS,), dtype=jnp.float32)
        Wgate = jax.random.normal(ks[2], (NUM_EXPERTS, HIDDEN, DIM), dtype=jnp.float32) * scale
        Wup = jax.random.normal(ks[3], (NUM_EXPERTS, HIDDEN, DIM), dtype=jnp.float32) * scale
        Wdown = jax.random.normal(ks[4], (NUM_EXPERTS, DIM, HIDDEN), dtype=jnp.float32) * scale
        return {'x': x, 'wg': wg, 'bg': bg, 'Wgate': Wgate, 'Wup': Wup, 'Wdown': Wdown}
    _L0_ffn_in = _L0_ffn_setup()
    _d = {'L0_attn_a_x': _L0_attn_a_in['x'], 'L0_attn_a_W_in': _L0_attn_a_in['W_in'], 'L0_attn_a_b_in': _L0_attn_a_in['b_in'], 'L0_attn_a_W_gate': _L0_attn_a_in['W_gate'], 'L0_attn_a_b_gate': _L0_attn_a_in['b_gate'], 'L0_attn_a_conv_w': _L0_attn_a_in['conv_w'], 'L0_attn_a_conv_b': _L0_attn_a_in['conv_b'], 'L0_attn_a_A_log': _L0_attn_a_in['A_log'], 'L0_attn_a_D_skip': _L0_attn_a_in['D_skip'], 'L0_attn_a_W_delta': _L0_attn_a_in['W_delta'], 'L0_attn_a_b_delta': _L0_attn_a_in['b_delta'], 'L0_attn_a_W_B': _L0_attn_a_in['W_B'], 'L0_attn_a_W_C': _L0_attn_a_in['W_C'], 'L0_attn_a_W_out': _L0_attn_a_in['W_out'], 'L0_attn_a_b_out': _L0_attn_a_in['b_out'], 'L0_attn_b_w_qkv': _L0_attn_b_in['w_qkv'], 'L0_attn_b_b_qkv': _L0_attn_b_in['b_qkv'], 'L0_attn_b_w_out': _L0_attn_b_in['w_out'], 'L0_attn_b_b_out': _L0_attn_b_in['b_out'], 'L0_ffn_wg': _L0_ffn_in['wg'], 'L0_ffn_bg': _L0_ffn_in['bg'], 'L0_ffn_Wgate': _L0_ffn_in['Wgate'], 'L0_ffn_Wup': _L0_ffn_in['Wup'], 'L0_ffn_Wdown': _L0_ffn_in['Wdown']}
    _x0 = _d['L0_attn_a_x']
    _d['L0_attn_a_x'] = jax.random.normal(jax.random.fold_in(jax.random.key(seed), 1), (8, 512, 128), dtype=_x0.dtype)
    del _x0
    return _d

def reference(L0_attn_a_x, L0_attn_a_W_in, L0_attn_a_b_in, L0_attn_a_W_gate, L0_attn_a_b_gate, L0_attn_a_conv_w, L0_attn_a_conv_b, L0_attn_a_A_log, L0_attn_a_D_skip, L0_attn_a_W_delta, L0_attn_a_b_delta, L0_attn_a_W_B, L0_attn_a_W_C, L0_attn_a_W_out, L0_attn_a_b_out, L0_attn_b_w_qkv, L0_attn_b_b_qkv, L0_attn_b_w_out, L0_attn_b_b_out, L0_ffn_wg, L0_ffn_bg, L0_ffn_Wgate, L0_ffn_Wup, L0_ffn_Wdown):

    def _L0_attn_a_ref(x, W_in, b_in, W_gate, b_gate, conv_w, conv_b, A_log, D_skip, W_delta, b_delta, W_B, W_C, W_out, b_out):
        import jax, jax.numpy as jnp
        import numpy as np
        from jax import lax
        D_MODEL, D_STATE, EXPAND, K = (128, 16, 2, 4)
        D_INNER = D_MODEL * EXPAND
        B, L = (2, 256)

        def _selective_ssm(x, A_log, D_skip, W_delta, b_delta, W_B, W_C):
            A = -jnp.exp(A_log)
            delta = jax.nn.softplus(x @ W_delta + b_delta)
            Bm = x @ W_B
            Cm = x @ W_C
            h0 = jnp.zeros((x.shape[0], A.shape[0], A.shape[1]), x.dtype)

            def step(h, inp):
                d_t, x_t, B_t, C_t = inp
                dA = jnp.exp(d_t[..., None] * A)
                h = dA * h + (d_t * x_t)[..., None] * B_t[:, None, :]
                y_t = jnp.einsum('bdn,bn->bd', h, C_t)
                return (h, y_t)
            xs = (delta.transpose(1, 0, 2), x.transpose(1, 0, 2), Bm.transpose(1, 0, 2), Cm.transpose(1, 0, 2))
            _, ys = lax.scan(step, h0, xs)
            return ys.transpose(1, 0, 2) + x * D_skip
        xz = x @ W_in + b_in
        x_gate = x @ W_gate + b_gate
        x_conv = lax.conv_general_dilated(xz.transpose(0, 2, 1), conv_w, window_strides=(1,), padding=[(K - 1, 0)], dimension_numbers=('NCH', 'OIH', 'NCH'), feature_group_count=D_INNER)
        x_conv = x_conv.transpose(0, 2, 1) + conv_b
        act = jax.nn.silu(x_conv)
        ssm_out = _selective_ssm(act, A_log, D_skip, W_delta, b_delta, W_B, W_C)
        gated = ssm_out * jax.nn.silu(x_gate)
        return gated @ W_out + b_out

    def _L0_attn_b_ref(x, w_qkv, b_qkv, w_out, b_out):
        import jax, jax.numpy as jnp
        import numpy as np
        NUM_HEADS = 16
        STRIDE = 32
        WINDOW = 64

        def _sparse_mask(n: int) -> jnp.ndarray:
            i = jnp.arange(n)[:, None]
            j = jnp.arange(n)[None, :]
            return (j % STRIDE == 0) | (jnp.abs(i - j) <= WINDOW)
        b, n, d = x.shape
        h = NUM_HEADS
        dh = d // h
        scale = dh ** (-0.5)
        qkv = x @ w_qkv + b_qkv
        q, k, v = jnp.split(qkv, 3, axis=-1)
        q = q.reshape(b, n, h, dh).transpose(0, 2, 1, 3)
        k = k.reshape(b, n, h, dh).transpose(0, 2, 1, 3)
        v = v.reshape(b, n, h, dh).transpose(0, 2, 1, 3)
        scores = jnp.einsum('bhid,bhjd->bhij', q, k) * scale
        mask = _sparse_mask(n)
        scores = jnp.where(mask, scores, -jnp.inf)
        attn = jax.nn.softmax(scores, axis=-1)
        out = jnp.einsum('bhij,bhjd->bhid', attn, v)
        out = out.transpose(0, 2, 1, 3).reshape(b, n, d)
        return out @ w_out + b_out

    def _L0_ffn_ref(x, wg, bg, Wgate, Wup, Wdown):
        import jax, jax.numpy as jnp
        import numpy as np
        NUM_EXPERTS = 8
        TOP_K = 2
        DIM = 128
        HIDDEN = 512
        B, S = (4, 256)
        b, s, d = x.shape
        xf = x.reshape(-1, d)
        T = xf.shape[0]
        logits = xf @ wg.T + bg
        vals, idx = jax.lax.top_k(logits, TOP_K)
        masked = jnp.full_like(logits, -jnp.inf)
        rows = jnp.arange(T)[:, None]
        masked = masked.at[rows, idx].set(vals)
        weights = jax.nn.softmax(masked, axis=-1)
        out = jnp.zeros_like(xf)
        for e in range(NUM_EXPERTS):
            g = xf @ Wgate[e].T
            u = xf @ Wup[e].T
            h = g * jax.nn.sigmoid(g) * u
            out = out + h @ Wdown[e].T * weights[:, e:e + 1]
        return out.reshape(b, s, d)
    x = L0_attn_a_x
    x = x + _L0_attn_a_ref(_layernorm(x, axis=-1), L0_attn_a_W_in, L0_attn_a_b_in, L0_attn_a_W_gate, L0_attn_a_b_gate, L0_attn_a_conv_w, L0_attn_a_conv_b, L0_attn_a_A_log, L0_attn_a_D_skip, L0_attn_a_W_delta, L0_attn_a_b_delta, L0_attn_a_W_B, L0_attn_a_W_C, L0_attn_a_W_out, L0_attn_a_b_out)
    x = x + _L0_ffn_ref(_layernorm(x, axis=-1), L0_ffn_wg, L0_ffn_bg, L0_ffn_Wgate, L0_ffn_Wup, L0_ffn_Wdown)
    x = x + _L0_attn_b_ref(_layernorm(x, axis=-1), L0_attn_b_w_qkv, L0_attn_b_b_qkv, L0_attn_b_w_out, L0_attn_b_b_out)
    x = x + _L0_ffn_ref(_layernorm(x, axis=-1), L0_ffn_wg, L0_ffn_bg, L0_ffn_Wgate, L0_ffn_Wup, L0_ffn_Wdown)
    return x

_drawn_inputs = setup_inputs


def setup_inputs(seed=0):
    import zlib

    import numpy as np

    out = dict(_drawn_inputs(seed))
    spreads = {'L0_attn_a_b_in': (0.0, 0.1),
     'L0_attn_a_b_gate': (0.0, 0.1),
     'L0_attn_a_conv_b': (0.0, 0.1),
     'L0_attn_a_D_skip': (1.0, 0.2),
     'L0_attn_a_b_delta': (0.0, 0.351),
     'L0_attn_a_b_out': (0.0, 0.1),
     'L0_attn_b_b_qkv': (0.0, 0.1),
     'L0_attn_b_b_out': (0.0, 0.1),
     'L0_ffn_bg': (0.0, 0.8)}
    factors = {'L0_ffn_wg': 4.984, 'L0_ffn_Wgate': 4.108, 'L0_ffn_Wup': 4.101, 'L0_ffn_Wdown': 4.09}
    for name, (base, spread) in spreads.items():
        noise = np.random.default_rng([zlib.crc32(name.encode()), seed]).standard_normal(out[name].shape)
        drawn = base * np.exp(spread * noise) if base else spread * noise
        out[name] = jnp.asarray(drawn.astype(out[name].dtype))
    for name, factor in factors.items():
        out[name] = (out[name] * factor).astype(out[name].dtype)
    return out
```

```python
import concourse.bass as bass
from concourse import mybir
from contextlib import ExitStack


def hybrid_layer_kernel(nc, x, w_in, b_in, w_gate, b_gate, conv_w, conv_b, a_log, d_skip, w_delta,
                        b_delta, w_b, w_c, ssm_w_out, ssm_b_out, w_qkv, b_qkv, att_w_out, att_b_out,
                        router_w, router_b, ffn_gate, ffn_up, ffn_down, att_consts, out, stages=None):
    fp32 = mybir.dt.float32
    bf16 = mybir.dt.bfloat16
    ALU = mybir.AluOpType
    ACT = mybir.ActivationFunctionType
    AX = mybir.AxisListType
    if stages is None:
        stages = ("ssm", "moe", "att", "moe")

    B, L, D = x.shape
    P = 128
    T = B * L // P
    TB = L // P
    DI = w_in.shape[1]
    J = DI // P
    NS = w_b.shape[1]
    KC = conv_w.shape[2]
    PAD = KC - 1
    E = router_w.shape[0]
    HID = ffn_gate.shape[2]
    HC = HID // P
    EPS = 1e-5
    AHEAD = 4

    NH = 16
    DH = D // NH
    G = 4
    R = NH // G
    STRIDE, WINDOW = 32, 64
    KS_N = L // STRIDE
    BAND = P + 2 * WINDOW
    reach = [(WINDOW if t == 0 else 0, BAND - (WINDOW if t == TB - 1 else 0)) for t in range(TB)]
    TERMS_Q = (0, 0, 0, 1, 1, 2)
    TERMS_K = (0, 1, 2, 0, 1, 0)
    TR = len(TERMS_Q) * DH

    ctx = ExitStack()
    with ctx:
        def sb(name, shape, dt=fp32):
            return ctx.enter_context(nc.sbuf_tensor(name, shape, dt))

        def sem(name):
            return ctx.enter_context(nc.semaphore(name))

        ts, ds = bass.ts, bass.ds
        bank = [ctx.enter_context(nc.psum_tensor(f"bank{i}", [P, 512], fp32)) for i in range(2)]
        score = [ctx.enter_context(nc.psum_tensor(f"score{i}", [P, 4, BAND], fp32)) for i in range(2)]
        bank += [score[i // 2][:, 2 * (i % 2):2 * (i % 2) + 2, :].rearrange("p a b -> p (a b)") for i in range(4)]
        bank += [ctx.enter_context(nc.psum_tensor(f"bank{i}", [P, 512], fp32)) for i in range(6, 8)]

        X = sb("X", [P, T, D])
        xnT = sb("xnT", [P, T * P])
        ident = sb("ident", [P, P])
        ones_row = sb("ones_row", [1, P])
        stats = sb("stats", [P, T, 6])
        mv = sb("mv", [P, T, 2])
        std = sb("std", [P, T])
        rstd = sb("rstd", [P, T])
        eps_col = sb("eps_col", [P, 1])
        fall = sb("fall", [P, E])
        xn = sb("xn", [P, 2, TB, D])

        identb = sb("identb", [P, P], bf16)
        rw_sb = sb("rw_sb", [P, E])
        rb_sb = sb("rb_sb", [P, E])
        wg_sb = sb("wg_sb", [P, E, HID])
        wu_sb = sb("wu_sb", [P, E, HID])
        wd_sb = sb("wd_sb", [P, E, HC, D])

        scr = ExitStack()

        def tmp(name, shape, dt=fp32):
            return scr.enter_context(nc.sbuf_tensor(name, shape, dt))

        w_in_sb = tmp("w_in_sb", [P, DI])
        w_gate_sb = tmp("w_gate_sb", [P, DI])
        w_delta_sb = tmp("w_delta_sb", [P, J, DI])
        w_bc_sb = tmp("w_bc_sb", [P, J, 3, 2 * NS])
        w_out_sb = tmp("w_out_sb", [P, J, D])
        b_out_row = tmp("b_out_row", [1, D])
        b_in_sb = tmp("b_in_sb", [P, J])
        b_gate_sb = tmp("b_gate_sb", [P, J])
        conv_w_sb = tmp("conv_w_sb", [P, J, KC])
        conv_b_sb = tmp("conv_b_sb", [P, J])
        b_delta_sb = tmp("b_delta_sb", [P, J])
        d_skip_sb = tmp("d_skip_sb", [P, J])
        a_log_sb = tmp("a_log_sb", [P, J, NS])
        a_exp = tmp("a_exp", [P, J, NS])
        a_neg = tmp("a_neg", [P, J, NS])
        conv_diag = tmp("conv_diag", [P, J, KC, P])
        pick = tmp("pick", [3 * 2 * NS, 2 * NS, P], bf16)
        xz = tmp("xz", [P, 2, J, PAD + L])
        lin = tmp("lin", [P, 2 * J, L])
        gact = tmp("gact", [P, 2, 2 * J, L])
        act_x = gact[:, :, J:, :]
        gate = gact[:, :, 0:J, :]
        pre_dt = tmp("pre_dt", [P, J, L])
        soft = tmp("soft", [P, J, L])
        dt = tmp("dt", [P, 2, J, L])
        u = tmp("u", [P, 2, J, L])
        bc_f = tmp("bc_f", [3 * 2 * NS, L])
        bc_r = tmp("bc_r", [3 * 2 * NS, L])
        bc_p2 = tmp("bc_p2", [3 * 2 * NS, L], bf16)
        bc_r2 = tmp("bc_r2", [3 * 2 * NS, L])
        bc3 = tmp("bc3", [3 * 2 * NS, 2, L], bf16)
        b_sb = tmp("b_sb", [P, AHEAD, L])
        dbu = tmp("dbu", [P, 2, J, L])
        h = tmp("h", [P, 2, J, L])
        hc = tmp("hc", [P, 2, J, L])
        gated = tmp("gated", [P, J, L])

        bank_b, bank_c = bank[0], bank[1]
        bank_da = [bank[2], bank[3]]
        bank_y = [bank[4], bank[5]]
        bank_pre = [bank[6], bank[7]]
        scr.close()

        scr = ExitStack()
        logits = tmp("logits", [P, T, E])
        lrank = tmp("lrank", [P, T, E])
        rest = tmp("rest", [P, T, E])
        one1 = tmp("one1", [P, T, E])
        one2 = tmp("one2", [P, T, E])
        wts = tmp("wts", [P, T, E])
        top = tmp("top", [P, 8, T])
        sg = tmp("sg", [P, 2, L])
        ht = tmp("ht", [P, 2, HC, L])
        scr.close()

        scr = ExitStack()
        xt = tmp("xt", [P, 2, L])
        wqkv_sb = tmp("wqkv_sb", [P, 3 * D])
        wo_sb = tmp("wo_sb", [P, G, D])
        bo_row = tmp("bo_row", [1, D])
        bqk_sb = tmp("bqk_sb", [P, 2])
        bv_all = tmp("bv_all", [P, NH, DH])
        bv_str = tmp("bv_str", [P, G, DH])
        consts_f = tmp("consts_f", [P, 2 * BAND + L + P])
        consts_b = tmp("consts_b", [P, 2 * BAND + L], bf16)
        qk_f = tmp("qk_f", [P, 2, L])
        qk_r = tmp("qk_r", [P, 2, L])
        qk_p = tmp("qk_p", [P, 2, 3, L], bf16)
        qs = tmp("qs", [P, 2, NH // 2, L], bf16)
        ks = tmp("ks", [P, 2, NH // 2, L], bf16)
        va = tmp("va", [P, 2, TB, NH, 32])
        vs_ = tmp("vs_", [P, 2, G, 32])
        mxw = tmp("mxw", [P, TB, 2, NH // 2])
        mxs = tmp("mxs", [P, TB, 2, NH // 2])
        mxn = tmp("mxn", [P, TB, 2, NH // 2])
        m_f = tmp("m_f", [NH, L])
        m_r = tmp("m_r", [NH, L])
        m_p = tmp("m_p", [NH, 3, L], bf16)
        pt = tmp("pt", [P, 2, TB * BAND])
        pts = tmp("pts", [P, 2, L])
        ots = tmp("ots", [P, 2, L])
        otn = tmp("otn", [P, G, L])
        rden = tmp("rden", [P, L])
        scr.close()
        band_q = consts_b[:, 0:BAND]
        band_k = consts_b[:, BAND:2 * BAND]
        far_k = consts_b[:, 2 * BAND:]
        den_pick = consts_f[:, 2 * BAND + L:]
        qk_dram = nc.dram_tensor("qk_parts", (2, 2, 3, P, L), bf16).ap()

        s_x = [sem(f"s_x{c}") for c in range(4)]
        s_cst = sem("s_cst")
        s_lnst = sem("s_lnst")
        s_var = sem("s_var")
        s_std = sem("s_std")
        s_rstd = sem("s_rstd")
        s_xn = sem("s_xn")
        s_xt = sem("s_xt")
        s_xnT = sem("s_xnT")
        s_w = sem("s_w")
        s_aneg = sem("s_aneg")
        s_diag = sem("s_diag")
        s_unit = sem("s_unit")
        s_unita = sem("s_unita")
        s_silu = sem("s_silu")
        s_soft = sem("s_soft")
        s_bc = sem("s_bc")
        s_dt = sem("s_dt")
        s_u = sem("s_u")
        s_bcs = sem("s_bcs")
        s_bc3 = sem("s_bc3")
        s_bb = sem("s_bb")
        s_cb = sem("s_cb")
        s_bcp = sem("s_bcp")
        s_da = sem("s_da")
        s_dbu = sem("s_dbu")
        s_h = sem("s_h")
        s_hc = sem("s_hc")
        s_y = sem("s_y")
        s_yd = sem("s_yd")
        s_gt = sem("s_gt")
        s_op = sem("s_op")
        s_res = sem("s_res")
        s_wf = sem("s_wf")
        s_lg = sem("s_lg")
        s_rt = sem("s_rt")
        s_re2 = sem("s_re2")
        s_re = sem("s_re")
        s_g = sem("s_g")
        s_up = sem("s_up")
        s_sg = sem("s_sg")
        s_ht = sem("s_ht")
        s_dn = sem("s_dn")
        s_mx = sem("s_mx")
        s_out = sem("s_out")
        a_w = sem("a_w")
        a_cst = sem("a_cst")
        a_wo = sem("a_wo")
        a_xt = sem("a_xt")
        a_qk = sem("a_qk")
        a_qf = sem("a_qf")
        a_sa = sem("a_sa")
        a_sp = sem("a_sp")
        a_st = sem("a_st")
        a_ld = [sem(f"a_ld{p}") for p in range(2)]
        a_v = sem("a_v")
        a_va = sem("a_va")
        a_s = sem("a_s")
        a_ss = sem("a_ss")
        a_mx = sem("a_mx")
        a_ms = sem("a_ms")
        a_mm = sem("a_mm")
        a_mn = sem("a_mn")
        a_mt = sem("a_mt")
        a_ma = sem("a_ma")
        a_mp = sem("a_mp")
        a_ml = [sem(f"a_ml{p}") for p in range(2)]
        a_t = sem("a_t")
        a_tf = sem("a_tf")
        a_e = sem("a_e")
        a_ef = sem("a_ef")
        a_pv = sem("a_pv")
        a_ot = sem("a_ot")
        a_dn = sem("a_dn")
        a_rd = sem("a_rd")
        a_on = sem("a_on")
        a_op = sem("a_op")
        a_res = sem("a_res")

        block = ctx.enter_context(nc.Block())
        n_ln = len(stages)
        ssm_loads = 0

        @block.sync
        def _(sp):
            xv = x.rearrange("b (t p) d -> p (b t) d", p=P)
            for c in range(4):
                sp.dma_start(X[:, ts(c, T // 4), :], xv[:, ts(c, T // 4), :]).then_inc(s_x[c], 16)
            nc_allow = ctx.enter_context(nc.allow_non_contiguous_dma(reason="small per-channel vectors"))
            if "ssm" in stages:
                col = lambda v: v.rearrange("(j p) -> p j", p=P)
                loads = [
                    (w_in_sb[:, :], w_in), (w_gate_sb[:, :], w_gate),
                    (w_delta_sb[:, :, :], w_delta.rearrange("(j p) n -> p j n", p=P)),
                    (w_out_sb[:, :, :], ssm_w_out.rearrange("(j p) n -> p j n", p=P)),
                    (b_out_row[:, :], ssm_b_out.rearrange("(a n) -> a n", a=1)),
                    (b_in_sb[:, :], col(b_in)), (b_gate_sb[:, :], col(b_gate)),
                    (conv_w_sb[:, :, :], conv_w.rearrange("(j p) a k -> p j (a k)", p=P)),
                    (conv_b_sb[:, :], col(conv_b)), (b_delta_sb[:, :], col(b_delta)),
                    (d_skip_sb[:, :], col(d_skip)),
                    (a_log_sb[:, :, :], a_log.rearrange("(j p) n -> p j n", p=P)),
                ]
                for r in range(3):
                    loads.append((w_bc_sb[:, :, r, 0:NS], w_b.rearrange("(j p) n -> p j n", p=P)))
                    loads.append((w_bc_sb[:, :, r, NS:2 * NS], w_c.rearrange("(j p) n -> p j n", p=P)))
                assert len(loads) == 18
                for dst, src in loads:
                    sp.dma_start(dst, src).then_inc(s_w, 16)
            if "moe" in stages:
                for dst, src in [
                    (rw_sb[:, :], router_w.rearrange("e d -> d e")),
                    (rb_sb[:, :], router_b.rearrange("(a e) -> a e", a=1).to_broadcast([P, E])),
                    (wg_sb[:, :, :], ffn_gate), (wu_sb[:, :, :], ffn_up), (wd_sb[:, :, :, :], ffn_down),
                ]:
                    sp.dma_start(dst, src).then_inc(s_wf, 16)
            if "att" in stages:
                if "ssm" in stages:
                    sp.wait_ge(s_res, B)
                if "moe" in stages:
                    sp.wait_ge(s_mx, B * E)
                sp.wait_ge(s_cst, 7)
                bv = b_qkv[2 * D:]
                loads = [(wqkv_sb[:, :], w_qkv), (bo_row[:, :], att_b_out.rearrange("(a n) -> a n", a=1)),
                         (bqk_sb[:, :], b_qkv[0:2 * D].rearrange("(c p) -> p c", p=P)),
                         (bv_all[:, :, :], bv.rearrange("(a h d) -> a h d", a=1, h=NH).to_broadcast([P, NH, DH])),
                         (consts_f[:, :], att_consts)]
                for r in range(R):
                    loads.append((bv_str[ts(r, 32), :, :],
                                  bv.rearrange("(g r d) -> r g d", g=G, r=R)[r:r + 1].to_broadcast([32, G, DH])))
                for dst, src in loads:
                    sp.dma_start(dst, src).then_inc(a_w, 16)
                sp.wait_ge(a_cst, 1)
                for r in range(R):
                    sp.dma_start(wo_sb[32 * r:32 * r + DH, :, :],
                                 att_w_out.rearrange("(g r d) n -> r d g n", g=G, r=R)[r]).then_inc(a_wo, 16)

                def stack(b, p):
                    sp.wait_ge(a_sp, 2 * b + 2)
                    if not (isinstance(b, int) and b < 2):
                        sp.wait_ge(a_pv, NH * (b - 1))
                    sp.dma_start(qk_dram[p].rearrange("c t p n -> p c t n"), qk_p[:, :, :, :]).then_inc(a_st, 16)
                    sp.wait_ge(a_st, 16 * b + 16)
                    for c, (dst, terms) in enumerate(((qs, TERMS_Q), (ks, TERMS_K))):
                        for z in range(2):
                            for i, t in enumerate(terms):
                                src = qk_dram[p, c, t].rearrange("(m z d) n -> z d m n", z=2, d=DH)[z]
                                at = 64 * z + DH * i
                                sp.dma_start(dst[at:at + DH, p, :, :], src).then_inc(a_ld[p], 16)

                def stack_max(b, p):
                    sp.wait_ge(a_mp, 2 * b + 2)
                    for z in range(2):
                        for t in range(3):
                            at = 64 * z + TR + t
                            sp.dma_start(qs[at:at + 1, p, :, :], m_p[ts(z, NH // 2), t, :]).then_inc(a_ml[p], 16)

                for b in range(2):
                    stack(b, b)
                    stack_max(b, b)
                with sp.Fori(0, (B - 2) // 2) as i:
                    for p in range(2):
                        stack(2 * i + 2 + p, p)
                        stack_max(2 * i + 2 + p, p)
            last = stages[-1]
            n_moe = stages.count("moe")
            if last == "moe":
                sp.wait_ge(s_mx, n_moe * B * E)
            elif last == "ssm":
                sp.wait_ge(s_res, B)
            else:
                sp.wait_ge(a_res, B)
            ov = out.rearrange("b (t p) d -> p (b t) d", p=P)
            for c in range(4):
                sp.dma_start(ov[:, ts(c, T // 4), :], X[:, ts(c, T // 4), :]).then_inc(s_out, 16)
            sp.wait_ge(s_out, 64)

        @block.gpsimd
        def _(pool):
            nc.gpsimd.memset(ident[:, :], 0.0).then_inc(s_cst, 1)
            nc.gpsimd.memset(ones_row[:, :], 1.0)
            nc.gpsimd.memset(eps_col[:, :], EPS)
            for e in range(E):
                nc.gpsimd.memset(fall[:, e:e + 1], float(E - e))
            nc.gpsimd.memset(xz[:, :, :, 0:PAD], 0.0)
            nc.gpsimd.memset(pick[:, :, :], 0.0).then_inc(s_cst, 1)
            pool.wait_ge(s_cst, 2)
            nc.gpsimd.affine_select(out=ident[:, :], in_=ident[:, :], compare_op=ALU.not_equal, fill=1.0,
                                    base=0, pattern=[[-1, P]], channel_multiplier=1).then_inc(s_cst, 1)
            for k in range(3):
                if k:
                    pool.wait_ge(s_cst, 3 + k)
                nc.gpsimd.affine_select(out=pick[:, :, :], in_=pick[:, :, :], compare_op=ALU.not_equal,
                                        fill=1.0, base=-2 * NS * k, pattern=[[-1, 2 * NS], [0, P]],
                                        channel_multiplier=1).then_inc(s_cst, 1)

            pool.wait_ge(s_cst, 6)
            nc.gpsimd.tensor_copy(identb[:, :], ident[:, :]).then_inc(s_cst, 1)

            def ssm_split_bc(b, p, k):
                if k == 0:
                    pool.wait_ge(s_bc, b + 1)
                    nc.gpsimd.tensor_tensor(bc_r[:, :], bc_f[:, :], bc3[:, p, :], ALU.subtract).then_inc(s_bcs, 1)
                elif k == 1:
                    if not (isinstance(b, int) and b == 0):
                        pool.wait_ge(s_bc3, b)
                    nc.gpsimd.tensor_tensor(bc_p2[:, :], bc_f[:, :], bc3[:, p, :], ALU.subtract).then_inc(s_bcs, 1)
                else:
                    pool.wait_ge(s_bcs, 3 * b + 2)
                    nc.gpsimd.tensor_tensor(bc_r2[:, :], bc_r[:, :], bc_p2[:, :], ALU.subtract).then_inc(s_bcs, 1)

            def ssm_u(b, p):
                pool.wait_ge(s_dt, b + 1)
                nc.gpsimd.tensor_tensor(u[:, p, :, :], dt[:, p, :, :], act_x[:, p, :, :], ALU.mult).then_inc(s_u, 1)

            def ssm_batch(b, p, last):
                for n in range(NS):
                    if n == 0:
                        pool.wait_ge(s_u, b + 1)
                    pool.wait_ge(s_bcp, NS * b + n + 1)
                    if not (isinstance(b, int) and b == 0 and n < 2):
                        pool.wait_ge(s_h, 2 * (NS * b + n - 1))
                    nc.gpsimd.tensor_tensor(dbu[:, n % 2, :, :], u[:, p, :, :],
                                            b_sb[:, n % AHEAD, None, :].to_broadcast([P, J, L]),
                                            ALU.mult).then_inc(s_dbu, 1)
                    if not last and n in (8, 9, 10):
                        ssm_split_bc(b + 1, 1 - p, n - 8)
                    if not last and n == 13:
                        ssm_u(b + 1, 1 - p)

            if "ssm" in stages:
                for k in range(3):
                    ssm_split_bc(0, 0, k)
                ssm_u(0, 0)
                ssm_batch(0, 0, False)
                with pool.Fori(0, (B - 2) // 2) as i:
                    ssm_batch(2 * i + 1, 1, False)
                    ssm_batch(2 * i + 2, 0, False)
                ssm_batch(B - 1, 1, True)

            if "att" in stages:
                if "ssm" in stages:
                    pool.wait_ge(s_res, B)
                if "moe" in stages:
                    pool.wait_ge(s_mx, B * E)
                nc.gpsimd.memset(wo_sb[:, :, :], 0.0).then_inc(a_cst, 1)
                nc.gpsimd.memset(va[:, :, :, :, :], 0.0).then_inc(a_cst, 1)
                nc.gpsimd.memset(vs_[:, :, :, :], 0.0).then_inc(a_cst, 1)
                nc.gpsimd.memset(ks[:, :, :, :], 1.0).then_inc(a_cst, 1)
                pool.wait_ge(a_cst, 4)
                nc.gpsimd.memset(va[:, :, :, :, DH:DH + 1], 1.0).then_inc(a_cst, 1)
                for r in range(R):
                    nc.gpsimd.memset(vs_[32 * r:32 * r + KS_N, :, :, DH:DH + 1], 1.0).then_inc(a_cst, 1)
                    pool.wait_ge(a_cst, 6 + r)
                pool.wait_ge(a_w, 16 * 9)
                nc.gpsimd.tensor_copy(consts_b[:, :], consts_f[:, 0:2 * BAND + L]).then_inc(a_cst, 1)
                k_att = stages.index("att")

                def att_xt(b, p):
                    if not (isinstance(b, int) and b < 2):
                        pool.wait_ge(a_v, b - 1)
                    pool.wait_ge(s_xnT, B * (k_att + 1))
                    nc.gpsimd.tensor_copy(xt[:, p, :], xnT[:, ts(b, L)]).then_inc(a_xt, 1)

                def att_split(b, p):
                    pool.wait_ge(a_sa, 2 * b + 1)
                    nc.gpsimd.tensor_tensor(qk_r[:, :, :], qk_f[:, :, :], qk_p[:, :, 0, :], ALU.subtract).then_inc(a_sp, 1)
                    pool.wait_ge(a_sa, 2 * b + 2)
                    pool.wait_ge(a_sp, 2 * b + 1)
                    nc.gpsimd.tensor_tensor(qk_p[:, :, 2, :], qk_r[:, :, :], qk_p[:, :, 1, :], ALU.subtract).then_inc(a_sp, 1)

                def att_split_max(b, p):
                    pool.wait_ge(a_ma, 3 * b + 2)
                    nc.gpsimd.tensor_tensor(m_r[:, :], m_f[:, :], m_p[:, 0, :], ALU.subtract).then_inc(a_mp, 1)
                    pool.wait_ge(a_ma, 3 * b + 3)
                    pool.wait_ge(a_mp, 2 * b + 1)
                    nc.gpsimd.tensor_tensor(m_p[:, 2, :], m_r[:, :], m_p[:, 1, :], ALU.subtract).then_inc(a_mp, 1)

                def att_next(b, p):
                    att_xt(b, p)
                    att_split(b, p)
                    att_split_max(b, p)

                att_next(0, 0)
                att_next(1, 1)
                with pool.Fori(0, (B - 2) // 2) as i:
                    att_next(2 * i + 2, 0)
                    att_next(2 * i + 3, 1)

        @block.scalar
        def _(act):
            def layer_norm(k):
                act.wait_ge(s_var, k + 1)
                if k == 0:
                    act.wait_ge(s_cst, 2 if stages[0] == "ssm" else 7)
                nc.scalar.activation(std[:, :], mv[:, :, 1], ACT.Sqrt, bias=eps_col[:, :]).then_inc(s_std, 1)
                with act.Fori(0, B // 2) as i:
                    for p in range(2):
                        b = 2 * i + p
                        act.wait_ge(s_xt, B * k + b + 1)
                        nc.scalar.activation(xnT[:, ts(b, L)], bank[p][:, :], ACT.Copy).then_inc(s_xnT, 1)

            def ssm_read(b, p, k):
                act.wait_ge(s_unit, 9 * b + k + 1)
                ps = bank_pre[(k + (k > 5)) % 2]
                if k in (0, 2):
                    nc.scalar.activation(xz[:, p, k // 2, PAD:], ps[:, :], ACT.Identity,
                                         bias=b_in_sb[:, k // 2:k // 2 + 1]).then_inc(s_unita, 1)
                elif k in (1, 3):
                    if k == 1 and not (isinstance(b, int) and b == 0):
                        act.wait_ge(s_silu, b)
                    nc.scalar.activation(lin[:, k // 2, :], ps[:, :], ACT.Identity,
                                         bias=b_gate_sb[:, k // 2:k // 2 + 1]).then_inc(s_unita, 1)
                elif k in (4, 5):
                    nc.scalar.activation(lin[:, J + k - 4, :], ps[:, :], ACT.Identity,
                                         bias=conv_b_sb[:, k - 4:k - 3]).then_inc(s_unita, 1)
                elif k == 6:
                    if not (isinstance(b, int) and b == 0):
                        act.wait_ge(s_bcs, 3 * b)
                    nc.scalar.activation(bc_f[:, :], ps[0:96, :], ACT.Copy).then_inc(s_unita, 1)
                    act.wait_ge(s_unita, 9 * b + 7)
                    nc.scalar.activation(bc3[:, p, :], bc_f[:, :], ACT.Copy).then_inc(s_bc, 1)
                else:
                    if k == 7 and not (isinstance(b, int) and b == 0):
                        act.wait_ge(s_dt, b)
                    nc.scalar.activation(pre_dt[:, k - 7, :], ps[:, :], ACT.Identity,
                                         bias=b_delta_sb[:, k - 7:k - 6]).then_inc(s_unita, 1)

            def ssm_silu(b, p):
                act.wait_ge(s_unita, 9 * b + 6)
                if not (isinstance(b, int) and b < 2):
                    act.wait_ge(s_gt, b - 1)
                nc.scalar.activation(gact[:, p, :, :], lin[:, :, :], ACT.Silu).then_inc(s_silu, 1)

            def ssm_soft(b):
                act.wait_ge(s_unita, 9 * b + 9)
                nc.scalar.activation(soft[:, :, :], pre_dt[:, :, :], ACT.Abs).then_inc(s_soft, 1)
                act.wait_ge(s_soft, 3 * b + 1)
                nc.scalar.activation(soft[:, :, :], soft[:, :, :], ACT.Exp, scale=-1.0).then_inc(s_soft, 1)
                act.wait_ge(s_soft, 3 * b + 2)
                nc.scalar.activation(soft[:, :, :], soft[:, :, :], ACT.Ln, bias=1.0).then_inc(s_soft, 1)

            def ssm_prepare(b, p, n):
                for k in {0: (0, 1), 1: (2, 3), 3: (4,), 5: (5,), 6: (6,), 7: (7,), 8: (8,)}.get(n, ()):
                    ssm_read(b, p, k)
                if n == 5:
                    ssm_silu(b, p)
                if n == 9:
                    ssm_soft(b)

            def ssm_row_b(b, n):
                act.wait_ge(s_bb, NS * b + n + 1)
                if not (isinstance(b, int) and b == 0 and n < AHEAD):
                    act.wait_ge(s_dbu, NS * b + n + 1 - AHEAD)
                nc.scalar.activation(b_sb[:, n % AHEAD, :], bank_b[:, :], ACT.Copy).then_inc(s_bcp, 1)

            def ssm_batch(b, p, first, last):
                if first:
                    for n in range(AHEAD - 1):
                        ssm_row_b(b, n)
                for n in range(NS):
                    for j in range(J):
                        if n == 0 and j == 0:
                            act.wait_ge(s_dt, b + 1)
                        if not (first and n == 0):
                            act.wait_ge(s_h, 2 * (NS * b + n) + j - 1)
                        nc.scalar.activation(bank_da[j][:, :], dt[:, p, j, :], ACT.Exp,
                                             scale=a_neg[:, j, n:n + 1]).then_inc(s_da, 1)
                    if n + AHEAD - 1 < NS:
                        ssm_row_b(b, n + AHEAD - 1)
                    elif not last:
                        ssm_row_b(b + 1, n + AHEAD - 1 - NS)
                    if not last:
                        ssm_prepare(b + 1, 1 - p, n)

            def moe_silu(b, m):
                for e in range(E):
                    for c in range(HC):
                        n = (m * B + b) * E * HC + e * HC + c
                        act.wait_ge(s_g, n + 1)
                        if not (isinstance(n, int) and n < 2):
                            act.wait_ge(s_ht, n - 1)
                        nc.scalar.activation(sg[:, c % 2, :], bank[c % 2][:, :], ACT.Silu).then_inc(s_sg, 1)

            def att_split(b, p):
                act.wait_ge(a_qf, b + 1)
                if not (isinstance(b, int) and b == 0):
                    act.wait_ge(a_st, 16 * b)
                nc.scalar.activation(qk_p[:, :, 0, :], qk_f[:, :, :], ACT.Copy).then_inc(a_sa, 1)
                act.wait_ge(a_sp, 2 * b + 1)
                nc.scalar.activation(qk_p[:, :, 1, :], qk_r[:, :, :], ACT.Copy).then_inc(a_sa, 1)

            def att_split_max(b, p, k):
                act.wait_ge(a_mt, b + 1)
                if not (isinstance(b, int) and b == 0):
                    act.wait_ge(a_ml[1 - p], 96 * (k + p))
                nc.scalar.activation(m_f[:, :], bank[0][0:NH, :], ACT.Copy).then_inc(a_ma, 1)
                act.wait_ge(a_ma, 3 * b + 1)
                nc.scalar.activation(m_p[:, 0, :], m_f[:, :], ACT.Copy).then_inc(a_ma, 1)
                act.wait_ge(a_mp, 2 * b + 1)
                nc.scalar.activation(m_p[:, 1, :], m_r[:, :], ACT.Copy).then_inc(a_ma, 1)

            def att_exps(b, p):
                def sums(g):
                    act.wait_ge(a_pv, NH * b + R * (g + 1))
                    if not (isinstance(b, int) and b == 0 and g < 2):
                        act.wait_ge(a_on, G * b + g - 1)
                    nc.scalar.activation(ots[:, g % 2, :], bank[6 + g % 2][:, :], ACT.Copy).then_inc(a_ot, 1)

                for h_ in range(NH):
                    g = h_ // R
                    if h_ % R == 0:
                        act.wait_ge(a_tf, G * b + g + 1)
                        if not (isinstance(b, int) and b == 0 and g < 2):
                            act.wait_ge(a_pv, NH * b + R * (g - 1))
                        nc.scalar.activation(pts[:, g % 2, :], bank[1][:, :], ACT.Exp).then_inc(a_ef, 1)
                    act.wait_ge(a_t, NH * b + h_ + 1)
                    if not (isinstance(b, int) and b == 0 and h_ < 2):
                        act.wait_ge(a_pv, NH * b + h_ - 1)
                    nc.scalar.activation(pt[:, h_ % 2, WINDOW:TB * BAND - WINDOW],
                                         score[h_ % 2][:, :, :].rearrange("p a b -> p (a b)")[:, WINDOW:TB * BAND - WINDOW],
                                         ACT.Exp).then_inc(a_e, 1)
                    if h_ >= R + 1 and (h_ - R - 1) % R == 0:
                        sums((h_ - R - 1) // R)
                sums(G - 1)

            for k, stage in enumerate(stages):
                layer_norm(k)
                if stage == "ssm":
                    act.wait_ge(s_w, 16 * 18)
                    nc.scalar.activation(a_exp[:, :, :], a_log_sb[:, :, :], ACT.Exp).then_inc(s_aneg, 1)
                    act.wait_ge(s_aneg, 1)
                    nc.scalar.mul(a_neg[:, :, :], a_exp[:, :, :], -1.0).then_inc(s_aneg, 1)
                    act.wait_ge(s_aneg, 2)
                    for n in range(NS):
                        ssm_prepare(0, 0, n)
                    ssm_batch(0, 0, True, False)
                    with act.Fori(0, (B - 2) // 2) as i:
                        ssm_batch(2 * i + 1, 1, False, False)
                        ssm_batch(2 * i + 2, 0, False, False)
                    ssm_batch(B - 1, 1, False, True)
                elif stage == "moe":
                    m = stages[:k].count("moe")
                    act.wait_ge(s_rt, 12 * m + 9)
                    nc.scalar.activation(top[:, 3, :], top[:, 2, :], ACT.Exp).then_inc(s_re, 1)
                    moe_silu(0, m)
                    with act.Fori(1, B) as b:
                        moe_silu(b, m)
                else:
                    att_split(0, 0)
                    att_split_max(0, 0, 0)
                    att_split(1, 1)
                    att_exps(0, 0)
                    att_split_max(1, 1, 0)
                    with act.Fori(0, (B - 2) // 2) as i:
                        for p in range(2):
                            b = 2 * i + 1 + p
                            att_split(b + 1, p)
                            att_exps(b, 1 - p)
                            att_split_max(b + 1, p, i + 1)
                    att_exps(B - 1, 1)

        @block.tensor
        def _(pe):
            def layer_norm(k):
                if k == 0:
                    pe.wait_ge(s_cst, 3)
                def transpose(b, p):
                    pe.wait_ge(s_xn, B * k + b + 1)
                    if not (isinstance(b, int) and B * k + b < 2):
                        pe.wait_ge(s_xnT, B * k + b - 1)
                    for t in range(TB):
                        mm = nc.tensor.transpose(bank[p][:, ts(t, P)], xn[:, p, t, :], ident[:, :])
                    mm.then_inc(s_xt, 1)

                for p in range(2):
                    transpose(p, p)
                with pe.Fori(1, B // 2) as i:
                    for p in range(2):
                        transpose(2 * i + p, p)

            def ssm_unit(b, p, k, part=None):
                if k == 0:
                    if not (isinstance(b, int) and b == 0):
                        pe.wait_ge(s_unita, 9 * b - 1)
                elif k == 1:
                    if not (isinstance(b, int) and b == 0):
                        pe.wait_ge(s_unita, 9 * b)
                elif k == 7:
                    if not (isinstance(b, int) and b < 2):
                        pe.wait_ge(s_res, b - 1)
                elif not part:
                    pe.wait_ge(s_unita, 9 * b + (k - 1 if k < 6 else k if k == 6 else 7))
                ps = bank_pre[(k + (k > 5)) % 2]
                xs = xnT[:, ts(b, L)]
                if k < 4:
                    w = w_gate_sb if k % 2 else w_in_sb
                    mm = nc.tensor.matmul(ps[:, :], w[:, ts(k // 2, P)], xs, start=True, stop=True)
                elif k < 6:
                    for t in (0, 1) if part == 0 else (2, 3):
                        mm = nc.tensor.matmul(ps[:, :], conv_diag[:, k - 4, t, :], xz[:, p, k - 4, t:t + L],
                                              start=(t == 0), stop=(t == KC - 1))
                    if part == 0:
                        return
                else:
                    pe.wait_ge(s_silu, b + 1)
                    for c in range(J):
                        w = w_bc_sb[:, c, :, :] if k == 6 else w_delta_sb[:, c, ts(k - 7, P)]
                        mm = nc.tensor.matmul(ps[0:96, :] if k == 6 else ps[:, :], w, act_x[:, p, c, :],
                                              start=(c == 0), stop=(c == J - 1))
                mm.then_inc(s_unit, 1)

            def ssm_prepare(b, p, n):
                for k, part in {0: ((0, None), (1, None)), 1: ((2, None), (3, None)), 2: ((4, 0),), 3: ((4, 1),),
                                4: ((5, 0),), 5: ((5, 1),), 6: ((6, None),), 7: ((7, None),), 8: ((8, None),)}.get(n, ()):
                    ssm_unit(b, p, k, part)

            def ssm_row_b(b, p, n):
                if n == 0:
                    pe.wait_ge(s_bc3, b + 1)
                if not (isinstance(b, int) and b == 0 and n == 0):
                    pe.wait_ge(s_bcp, NS * b + n)
                nc.tensor.matmul(bank_b[:, :], pick[:, n, :], bc3[:, p, :], start=True, stop=True).then_inc(s_bb, 1)

            def ssm_accumulate(b, n, q):
                pe.wait_ge(s_hc, NS * b + n + 1)
                if n == 0 and not (isinstance(b, int) and b == 0):
                    pe.wait_ge(s_yd, b)
                for j in range(J):
                    mm = nc.tensor.matmul(bank_y[j][:, :], ident[:, :], hc[:, q, j, :],
                                          start=(n == 0), stop=(n == NS - 1))
                mm.then_inc(s_y, 1)

            def ssm_out(b, p, last):
                pe.wait_ge(s_gt, b + 1)
                if not last:
                    pe.wait_ge(s_unita, 9 * B - 1 if isinstance(b, int) and b == B - 2 else 9 * (b + 2) + 5)
                else:
                    pe.wait_ge(s_res, b)
                for t in range(TB):
                    nc.tensor.matmul(bank_pre[0][:, ts(t, P)], ones_row[:, :], b_out_row[:, :], start=True, stop=False,
                                     skip_group_check=True)
                    for j in range(J):
                        mm = nc.tensor.matmul(bank_pre[0][:, ts(t, P)], gated[:, j, ts(t, P)], w_out_sb[:, j, :],
                                              start=False, stop=(j == J - 1), skip_group_check=True)
                mm.then_inc(s_op, 1)

            def ssm_batch(b, p, first, last):
                if first:
                    for n in range(AHEAD):
                        ssm_row_b(b, p, n)
                for n in range(NS):
                    if n + AHEAD < NS:
                        ssm_row_b(b, p, n + AHEAD)
                    elif not last:
                        ssm_row_b(b + 1, 1 - p, n + AHEAD - NS)
                    if not (first and n == 0):
                        pe.wait_ge(s_hc, NS * b + n)
                    nc.tensor.matmul(bank_c[:, :], pick[:, NS + n, :], bc3[:, p, :], start=True, stop=True).then_inc(s_cb, 1)
                    if n:
                        ssm_accumulate(b, n - 1, (n - 1) % 2)
                    elif not first:
                        ssm_accumulate(b - 1, NS - 1, 1)
                    if not last:
                        ssm_prepare(b + 1, 1 - p, n)
                    if not first and n == 5:
                        ssm_out(b - 1, 1 - p, False)
                if last:
                    ssm_accumulate(b, NS - 1, 1)
                    ssm_out(b, p, True)

            def moe_experts(b, m):
                xs = xnT[:, ts(b, L)]

                def down(e):
                    g = (m * B + b) * E + e
                    pe.wait_ge(s_ht, HC * (g + 1))
                    if not (isinstance(g, int) and g < 2):
                        pe.wait_ge(s_mx, g - 1)
                    for t in range(TB):
                        for c in range(HC):
                            mm = nc.tensor.matmul(bank[6 + e % 2][:, ts(t, P)], ht[:, e % 2, c, ts(t, P)],
                                                  wd_sb[:, e, c, :], start=(c == 0), stop=(c == HC - 1),
                                                  skip_group_check=True)
                    mm.then_inc(s_dn, 1)

                for e in range(E):
                    for c in range(HC):
                        n = (m * B + b) * E * HC + e * HC + c
                        if not (isinstance(n, int) and n < 2):
                            pe.wait_ge(s_sg, n - 1)
                        nc.tensor.matmul(bank[c % 2][:, :], wg_sb[:, e, ts(c, P)], xs, start=True, stop=True).then_inc(s_g, 1)
                        if not (isinstance(n, int) and n < 2):
                            pe.wait_ge(s_ht, n - 1)
                        nc.tensor.matmul(bank[2 + c % 2][:, :], wu_sb[:, e, ts(c, P)], xs, start=True, stop=True).then_inc(s_up, 1)
                    if e:
                        down(e - 1)
                down(E - 1)

            def att_project(b, p):
                pe.wait_ge(a_xt, b + 1)
                if not (isinstance(b, int) and b == 0):
                    if isinstance(b, int) and b == 1:
                        pe.wait_ge(a_ma, 1)
                    else:
                        pe.wait_ge(a_res, b - 1)
                    pe.wait_ge(a_ms, 2 * b)
                for c in range(2):
                    mm = nc.tensor.matmul(bank[c][:, :], wqkv_sb[:, ts(c, D)], xt[:, p, :], start=True, stop=True)
                mm.then_inc(a_qk, 1)
                pe.wait_ge(a_qf, b + 1)
                for t in range(TB):
                    nc.tensor.matmul(bank[0][:, ts(t, P)], xt[:, p, ts(t, P)], wqkv_sb[:, 2 * D:], start=True, stop=True,
                                     skip_group_check=True)
                wv = wqkv_sb[:, 2 * D:].rearrange("p (g r d) -> p r g d", g=G, r=R)
                for r in range(R):
                    mm = nc.tensor.matmul(bank[1][32 * r:32 * r + KS_N, 0:G * DH], xt[:, p, 0:L:STRIDE], wv[:, r, :, :],
                                          start=True, stop=True)
                mm.then_inc(a_v, 1)

            def att_scores(b, p, k):
                pe.wait_ge(a_ld[p], 384 * (k + 1))
                if isinstance(b, int) and b == 0:
                    pe.wait_ge(a_va, 1)
                else:
                    pe.wait_ge(a_ef, G * b)
                    pe.wait_ge(a_rd, G * b - 1)
                for z in range(2):
                    for qt in range(TB):
                        for m in range(NH // 2):
                            mm = nc.tensor.matmul(bank[z][:, ds(P * qt + KS_N * m, KS_N)],
                                                  qs[64 * z:64 * z + TR, p, m, ts(qt, P)],
                                                  ks[64 * z:64 * z + TR, p, m, 0:L:STRIDE], start=True, stop=True,
                                                  skip_group_check=True)
                    mm.then_inc(a_ss, 1)
                for qt in range(TB):
                    lo, hi = reach[qt]
                    for g in range(G):
                        u_ = G * qt + g
                        if u_ >= 2:
                            pe.wait_ge(a_mx, NH * b + u_ - 1)
                        elif not (isinstance(b, int) and b == 0):
                            pe.wait_ge(a_e, NH * b)
                        sc = score[u_ % 2]
                        for c in range(2):
                            nc.tensor.matmul(sc[:, 2 * c:2 * c + 2, :], identb[:, :],
                                             band_q[:, None, :].to_broadcast([P, 2, BAND]), start=True, stop=False,
                                             skip_group_check=True)
                        for r in range(R):
                            z, m = r // 2, 2 * g + r % 2
                            k0 = P * qt - WINDOW
                            mm = nc.tensor.matmul(sc[:, r, lo:hi], qs[64 * z:64 * z + TR, p, m, ts(qt, P)],
                                                  ks[64 * z:64 * z + TR, p, m, k0 + lo:k0 + hi], start=False, stop=True,
                                                  skip_group_check=True)
                        mm.then_inc(a_s, 1)

            def att_max(b, p):
                pe.wait_ge(a_mn, b + 1)
                for qt in range(TB):
                    mm = nc.tensor.transpose(bank[0][0:NH, ts(qt, P)], mxn[:, qt, :, :].rearrange("p z m -> p (z m)"), ident[:, :])
                mm.then_inc(a_mt, 1)

            def att_heads(b, p, k, last):
                TM = TR + 3

                def far(g):
                    if g == 0:
                        pe.wait_ge(a_va, b + 1 if last else b + 2)
                    else:
                        pe.wait_ge(a_ef, G * b + g)
                    nc.tensor.matmul(bank[1][:, :], identb[:, :], far_k, start=True, stop=False, skip_group_check=True)
                    for r in range(R):
                        h_ = R * g + r
                        at = 64 * (h_ % 2)
                        mm = nc.tensor.matmul(bank[1][32 * r:32 * r + KS_N, :], ks[at:at + TM, p, h_ // 2, 0:L:STRIDE],
                                              qs[at:at + TM, p, h_ // 2, :], start=False, stop=True, skip_group_check=True)
                    mm.then_inc(a_tf, 1)

                def near(h_):
                    if h_ >= 2:
                        pe.wait_ge(a_e, NH * b + h_ - 1)
                    else:
                        pe.wait_ge(a_mx, NH * (b + 1))
                    sc = score[h_ % 2]
                    for c in range(2):
                        nc.tensor.matmul(sc[:, 2 * c:2 * c + 2, :], identb[:, :],
                                         band_k[:, None, :].to_broadcast([P, 2, BAND]), start=True, stop=False,
                                         skip_group_check=True)
                    at = 64 * (h_ % 2)
                    for kt in range(TB):
                        lo, hi = reach[kt]
                        q0 = P * kt - WINDOW
                        mm = nc.tensor.matmul(sc[:, kt, lo:hi], ks[at:at + TM, p, h_ // 2, ts(kt, P)],
                                              qs[at:at + TM, p, h_ // 2, q0 + lo:q0 + hi], start=False, stop=True,
                                              skip_group_check=True)
                    mm.then_inc(a_t, 1)

                def sums(h_):
                    g, r = h_ // R, h_ % R
                    acc = bank[6 + g % 2]
                    if r == 0:
                        pe.wait_ge(a_ef, G * b + g + 1)
                        if not (isinstance(b, int) and b == 0 and g < 2):
                            pe.wait_ge(a_ot, G * b + g - 1)
                    pe.wait_ge(a_e, NH * b + h_ + 1)
                    for kt in range(TB):
                        lo, hi = reach[kt]
                        q0 = P * kt - WINDOW
                        nc.tensor.matmul(acc[ts(r, 32), q0 + lo:q0 + hi], va[:, p, kt, h_, :],
                                         pt[:, h_ % 2, BAND * kt + lo:BAND * kt + hi], start=(kt == 0), stop=False,
                                         skip_group_check=True)
                    nc.tensor.matmul(acc[ts(r, 32), :], vs_[ts(r, 32), p, g, :], pts[ts(r, 32), g % 2, :],
                                     start=False, stop=True, skip_group_check=True).then_inc(a_pv, 1)

                pe.wait_ge(a_ml[p], 96 * (k + 1))
                for h_ in range(NH):
                    if h_ % R == 0:
                        far(h_ // R)
                    near(h_)
                    if h_:
                        sums(h_ - 1)
                    if h_ >= R + 2 and (h_ - R - 2) % R == 0:
                        att_spread(b, (h_ - R - 2) // R, last)
                sums(NH - 1)

            def att_spread(b, g, last):
                pe.wait_ge(a_ot, G * b + g + 1)
                if g == 0 and last:
                    pe.wait_ge(a_res, b)
                elif g == 0:
                    pe.wait_ge(a_va, b + 2)
                elif g == G - 1 and not last:
                    pe.wait_ge(a_ma, 3 * (b + 1) + 1)
                else:
                    pe.wait_ge(a_rd, G * b + g)
                nc.tensor.matmul(bank[0][:, :], den_pick, ots[:, g % 2, :], start=True, stop=True).then_inc(a_dn, 1)

            def att_out(b):
                pe.wait_ge(a_on, G * (b + 1))
                for t in range(TB):
                    nc.tensor.matmul(bank[0][:, ts(t, P)], ones_row[:, :], bo_row[:, :], start=True, stop=False,
                                     skip_group_check=True)
                    for g in range(G):
                        mm = nc.tensor.matmul(bank[0][:, ts(t, P)], otn[:, g, ts(t, P)], wo_sb[:, g, :], start=False,
                                              stop=(g == G - 1), skip_group_check=True)
                mm.then_inc(a_op, 1)

            def att_step(b, p, k):
                kn = k + p
                att_project(b + 1, 1 - p)
                att_heads(b, p, k, False)
                att_scores(b + 1, 1 - p, kn)
                att_max(b + 1, 1 - p)
                att_spread(b, G - 1, False)
                att_out(b)

            for k, stage in enumerate(stages):
                layer_norm(k)
                if stage == "ssm":
                    pe.wait_ge(s_xnT, B * (k + 1))
                    pe.wait_ge(s_w, 16 * 18)
                    pe.wait_ge(s_diag, J * KC)
                    pe.wait_ge(s_cst, 6)
                    for n in range(NS):
                        ssm_prepare(0, 0, n)
                    ssm_batch(0, 0, True, False)
                    with pe.Fori(0, (B - 2) // 2) as i:
                        ssm_batch(2 * i + 1, 1, False, False)
                        ssm_batch(2 * i + 2, 0, False, False)
                    ssm_batch(B - 1, 1, False, True)
                elif stage == "moe":
                    m = stages[:k].count("moe")
                    pe.wait_ge(s_xnT, B * (k + 1))
                    pe.wait_ge(s_wf, 16 * 5)
                    for t in range(T):
                        mm = nc.tensor.matmul(bank[7][:, ts(t, E)], xnT[:, ts(t, P)], rw_sb[:, :], start=True, stop=True,
                                              skip_group_check=True)
                    mm.then_inc(s_lg, 1)
                    moe_experts(0, m)
                    with pe.Fori(1, B) as b:
                        moe_experts(b, m)
                else:
                    pe.wait_ge(a_w, 16 * 9)
                    pe.wait_ge(a_wo, 16 * R)
                    pe.wait_ge(a_cst, 10)
                    pe.wait_ge(s_cst, 7)
                    att_project(0, 0)
                    att_scores(0, 0, 0)
                    att_max(0, 0)
                    att_step(0, 0, 0)
                    with pe.Fori(0, (B - 2) // 2) as i:
                        att_step(2 * i + 1, 1, i)
                        att_step(2 * i + 2, 0, i + 1)
                    att_heads(B - 1, 1, B // 2 - 1, True)
                    att_spread(B - 1, G - 1, True)
                    att_out(B - 1)

        @block.vector
        def _(dve):
            vec = nc.vector

            def layer_norm(k):
                if k and stages[k - 1] == "ssm":
                    dve.wait_ge(s_res, B)
                elif k and stages[k - 1] == "moe":
                    dve.wait_ge(s_mx, stages[:k].count("moe") * B * E)
                elif k:
                    dve.wait_ge(a_res, B)
                for c in range(4):
                    if k == 0:
                        dve.wait_ge(s_x[c], 16)
                    for t in range(T // 4):
                        vec.bn_stats(stats[:, c * T // 4 + t, :], X[:, c * T // 4 + t, :]).then_inc(s_lnst, 1)
                dve.wait_ge(s_lnst, T * (k + 1))
                for t in range(T):
                    vs = vec.bn_aggr(mv[:, t, :], stats[:, t, :])
                vs.then_inc(s_var, 1)
                dve.wait_ge(s_std, k + 1)
                vec.reciprocal(rstd[:, :], std[:, :]).then_inc(s_rstd, 1)
                dve.wait_ge(s_rstd, k + 1)

                def normalise(b, p):
                    if not (isinstance(b, int) and B * k + b < 2):
                        dve.wait_ge(s_xt, B * k + b - 1)
                    for t in range(TB):
                        g = b * TB + t
                        vs = vec.tensor_scalar(xn[:, p, t:t + 1, :], X[:, ds(g, 1), :], mv[:, ds(g, 1), 0], rstd[:, ds(g, 1)],
                                               ALU.subtract, ALU.mult)
                    vs.then_inc(s_xn, 1)

                for p in range(2):
                    normalise(p, p)
                with dve.Fori(1, B // 2) as i:
                    for p in range(2):
                        normalise(2 * i + p, p)

            def ssm_dt(b, p):
                dve.wait_ge(s_soft, 3 * b + 3)
                if not (isinstance(b, int) and b < 2):
                    dve.wait_ge(s_da, 2 * NS * (b - 1))
                vec.scalar_tensor_tensor(out=dt[:, p, :, :], in0=pre_dt[:, :, :], scalar=0.0, in1=soft[:, :, :],
                                         op0=ALU.max, op1=ALU.add).then_inc(s_dt, 1)

            def ssm_parts(b, p):
                dve.wait_ge(s_bcs, 3 * b + 3)
                vec.tensor_copy(bc3[32:64, p, :], bc_p2[32:64, :])
                vec.tensor_copy(bc3[64:96, p, :], bc_r2[64:96, :]).then_inc(s_bc3, 1)

            def ssm_hc(b, n, q):
                dve.wait_ge(s_cb, NS * b + n + 1)
                dve.wait_ge(s_h, 2 * (NS * b + n + 1))
                if not (isinstance(b, int) and b == 0 and n < 2):
                    dve.wait_ge(s_y, NS * b + n - 1)
                vec.tensor_tensor(hc[:, q, :, :], h[:, q, :, :], bank_c[:, None, :].to_broadcast([P, J, L]),
                                  ALU.mult).then_inc(s_hc, 1)

            def ssm_finish(b, p):
                dve.wait_ge(s_y, NS * (b + 1))
                for j in range(J):
                    vs = vec.scalar_tensor_tensor(out=gated[:, j, :], in0=act_x[:, p, j, :], scalar=d_skip_sb[:, j:j + 1],
                                                  in1=bank_y[j][:, :], op0=ALU.mult, op1=ALU.add)
                vs.then_inc(s_yd, 1)
                dve.wait_ge(s_yd, b + 1)
                vec.tensor_tensor(gated[:, :, :], gated[:, :, :], gate[:, p, :, :], ALU.mult).then_inc(s_gt, 1)

            def ssm_residual(b):
                dve.wait_ge(s_op, b + 1)
                xs = X[:, ts(b, TB), :]
                vec.tensor_tensor(xs, xs, bank_pre[0][:, :].rearrange("p (t d) -> p t d", t=TB), ALU.add).then_inc(s_res, 1)

            def ssm_batch(b, p, first, last):
                for n in range(NS):
                    for j in range(J):
                        dve.wait_ge(s_da, 2 * (NS * b + n) + j + 1)
                        if j == 0:
                            dve.wait_ge(s_dbu, NS * b + n + 1)
                            if not (first and n < 2):
                                dve.wait_ge(s_hc, NS * b + n - 1)
                        vec.tensor_tensor_scan(h[:, n % 2, j, :], bank_da[j][:, :], dbu[:, n % 2, j, :], 0.0,
                                               ALU.mult, ALU.add).then_inc(s_h, 1)
                    if n:
                        ssm_hc(b, n - 1, (n - 1) % 2)
                    elif not first:
                        ssm_hc(b - 1, NS - 1, 1)
                    if not first and n == 1:
                        ssm_finish(b - 1, 1 - p)
                    if not first and n == 6:
                        ssm_residual(b - 1)
                    if not last and n == 11:
                        ssm_dt(b + 1, 1 - p)
                    if not last and n == 11:
                        ssm_parts(b + 1, 1 - p)
                if last:
                    ssm_hc(b, NS - 1, 1)
                    ssm_finish(b, p)
                    ssm_residual(b)

            def moe_route(m):
                base = 12 * m
                n = 0

                def then(ins):
                    nonlocal n
                    n += 1
                    ins.then_inc(s_rt, 1)
                    dve.wait_ge(s_rt, base + n)

                big = lambda a: a[:, :, None].to_broadcast([P, T, E])
                fallb = fall[:, None, :].to_broadcast([P, T, E])
                dve.wait_ge(s_lg, m + 1)
                then(vec.tensor_tensor(logits[:, :, :], bank[7][:, 0:T * E].rearrange("p (t e) -> p t e", e=E),
                                       rb_sb[:, None, :].to_broadcast([P, T, E]), ALU.add))
                then(vec.tensor_reduce(top[:, 0, :], logits[:, :, :], AX.X, ALU.max))
                then(vec.tensor_tensor(one1[:, :, :], logits[:, :, :], big(top[:, 0, :]), ALU.is_equal))
                then(vec.tensor_tensor(lrank[:, :, :], one1[:, :, :], fallb, ALU.mult))
                then(vec.tensor_reduce(top[:, 4, :], lrank[:, :, :], AX.X, ALU.max))
                then(vec.tensor_tensor(one1[:, :, :], fallb, big(top[:, 4, :]), ALU.is_equal))
                then(vec.scalar_tensor_tensor(out=rest[:, :, :], in0=one1[:, :, :], scalar=-3.0e38, in1=logits[:, :, :],
                                              op0=ALU.mult, op1=ALU.add))
                then(vec.tensor_reduce(top[:, 1, :], rest[:, :, :], AX.X, ALU.max))
                then(vec.tensor_tensor(top[:, 2, :], top[:, 1, :], top[:, 0, :], ALU.subtract))
                then(vec.tensor_tensor(one2[:, :, :], rest[:, :, :], big(top[:, 1, :]), ALU.is_equal))
                then(vec.tensor_tensor(lrank[:, :, :], one2[:, :, :], fallb, ALU.mult))
                then(vec.tensor_reduce(top[:, 5, :], lrank[:, :, :], AX.X, ALU.max))
                base2 = [7 * m]

                def then2(ins):
                    base2[0] += 1
                    ins.then_inc(s_re2, 1)
                    dve.wait_ge(s_re2, base2[0])

                then2(vec.tensor_tensor(one2[:, :, :], fallb, big(top[:, 5, :]), ALU.is_equal))
                dve.wait_ge(s_re, m + 1)
                then2(vec.tensor_scalar(top[:, 6, :], top[:, 3, :], 1.0, None, ALU.add))
                then2(vec.reciprocal(top[:, 6, :], top[:, 6, :]))
                then2(vec.tensor_tensor(top[:, 7, :], top[:, 3, :], top[:, 6, :], ALU.mult))
                then2(vec.tensor_tensor(one1[:, :, :], one1[:, :, :], big(top[:, 6, :]), ALU.mult))
                then2(vec.tensor_tensor(one2[:, :, :], one2[:, :, :], big(top[:, 7, :]), ALU.mult))
                then2(vec.tensor_tensor(wts[:, :, :], one1[:, :, :], one2[:, :, :], ALU.add))

            def moe_combine(b, m):
                def add(e):
                    g = (m * B + b) * E + e
                    dve.wait_ge(s_dn, g + 1)
                    if not (isinstance(g, int) and g == 0):
                        dve.wait_ge(s_mx, g)
                    for t in range(TB):
                        gt = b * TB + t
                        xs = X[:, ds(gt, 1), :]
                        vs = vec.scalar_tensor_tensor(out=xs, in0=bank[6 + e % 2][:, None, ts(t, P)],
                                                      scalar=wts[:, ds(gt, 1), e], in1=xs,
                                                      op0=ALU.mult, op1=ALU.add)
                    vs.then_inc(s_mx, 1)

                for e in range(E):
                    for c in range(HC):
                        g = (m * B + b) * E + e
                        n = HC * g + c
                        dve.wait_ge(s_up, n + 1)
                        dve.wait_ge(s_sg, n + 1)
                        if not (isinstance(g, int) and g < 2):
                            dve.wait_ge(s_dn, g - 1)
                        vec.tensor_tensor(ht[:, e % 2, c, :], sg[:, c % 2, :], bank[2 + c % 2][:, :],
                                          ALU.mult).then_inc(s_ht, 1)
                    if e:
                        add(e - 1)
                add(E - 1)

            def att_inputs(b, p):
                dve.wait_ge(a_qk, b + 1)
                if not (isinstance(b, int) and b == 0):
                    dve.wait_ge(a_sp, 2 * b)
                vec.tensor_scalar(qk_f[:, 0, :], bank[0][:, :], bqk_sb[:, 0:1], DH ** -0.5, ALU.add, ALU.mult)
                vec.tensor_scalar(qk_f[:, 1, :], bank[1][:, :], bqk_sb[:, 1:2], None, ALU.add).then_inc(a_qf, 1)
                dve.wait_ge(a_v, b + 1)
                if not (isinstance(b, int) and b < 2):
                    dve.wait_ge(a_pv, NH * (b - 1))
                vec.tensor_tensor(va[:, p, :, :, 0:DH], bank[0][:, :].rearrange("p (t h d) -> p t h d", t=TB, h=NH),
                                  bv_all[:, None, :, :].to_broadcast([P, TB, NH, DH]), ALU.add)
                for r in range(R):
                    rows = slice(32 * r, 32 * r + KS_N)
                    vi = vec.tensor_tensor(vs_[rows, p, :, 0:DH], bank[1][rows, 0:G * DH].rearrange("p (g d) -> p g d", g=G),
                                           bv_str[rows, :, :], ALU.add)
                vi.then_inc(a_va, 1)

            def att_maxima(b):
                if not (isinstance(b, int) and b == 0):
                    dve.wait_ge(a_mn, b)
                for z in range(2):
                    dve.wait_ge(a_ss, 2 * b + z + 1)
                    vec.tensor_reduce(mxs[:, :, z, :], bank[z][:, :].rearrange("p (q m k) -> p q m k", q=TB, k=KS_N),
                                      AX.X, ALU.max).then_inc(a_ms, 1)
                for qt in range(TB):
                    lo, hi = reach[qt]
                    for g in range(G):
                        dve.wait_ge(a_s, NH * b + G * qt + g + 1)
                        vec.tensor_reduce(mxw[:, qt, :, 2 * g:2 * g + 2],
                                          score[(G * qt + g) % 2][:, :, lo:hi].rearrange("p (z m) k -> p z m k", z=2),
                                          AX.X, ALU.max).then_inc(a_mx, 1)
                dve.wait_ge(a_mx, NH * (b + 1))
                dve.wait_ge(a_ms, 2 * (b + 1))
                if not (isinstance(b, int) and b == 0):
                    dve.wait_ge(a_mt, b)
                vec.tensor_tensor(mxs[:, :, :, :], mxw[:, :, :, :], mxs[:, :, :, :], ALU.max).then_inc(a_mm, 1)
                dve.wait_ge(a_mm, b + 1)
                vec.tensor_scalar(mxn[:, :, :, :], mxs[:, :, :, :], -1.0, None, ALU.mult).then_inc(a_mn, 1)

            def att_normalise(b, g):
                dve.wait_ge(a_dn, G * b + g + 1)
                if not (isinstance(b, int) and b == 0 and g == 0):
                    dve.wait_ge(a_on, G * b + g)
                vec.reciprocal(rden[:, :], bank[0][:, :]).then_inc(a_rd, 1)
                dve.wait_ge(a_rd, G * b + g + 1)
                vec.tensor_tensor(otn[:, g, :], ots[:, g % 2, :], rden[:, :], ALU.mult).then_inc(a_on, 1)

            def att_residual(b):
                dve.wait_ge(a_op, b + 1)
                xs = X[:, ts(b, TB), :]
                vec.tensor_tensor(xs, xs, bank[0][:, :].rearrange("p (t d) -> p t d", t=TB), ALU.add).then_inc(a_res, 1)

            def att_step(b, p):
                att_inputs(b + 1, 1 - p)
                for g in range(G - 1):
                    att_normalise(b, g)
                att_maxima(b + 1)
                att_normalise(b, G - 1)
                att_residual(b)

            for k, stage in enumerate(stages):
                layer_norm(k)
                if stage == "ssm":
                    dve.wait_ge(s_w, 16 * 18)
                    dve.wait_ge(s_cst, 3)
                    for j in range(J):
                        for t in range(KC):
                            vec.tensor_scalar(conv_diag[:, j, t, :], ident[:, :], conv_w_sb[:, j, t:t + 1], None,
                                              ALU.mult).then_inc(s_diag, 1)
                    ssm_dt(0, 0)
                    ssm_parts(0, 0)
                    ssm_batch(0, 0, True, False)
                    with dve.Fori(0, (B - 2) // 2) as i:
                        ssm_batch(2 * i + 1, 1, False, False)
                        ssm_batch(2 * i + 2, 0, False, False)
                    ssm_batch(B - 1, 1, False, True)
                elif stage == "moe":
                    m = stages[:k].count("moe")
                    dve.wait_ge(s_wf, 16 * 5)
                    moe_route(m)
                    moe_combine(0, m)
                    with dve.Fori(1, B) as b:
                        moe_combine(b, m)
                else:
                    dve.wait_ge(a_w, 16 * 9)
                    dve.wait_ge(a_cst, 10)
                    att_inputs(0, 0)
                    att_maxima(0)
                    att_step(0, 0)
                    with dve.Fori(0, (B - 2) // 2) as i:
                        att_step(2 * i + 1, 1)
                        att_step(2 * i + 2, 0)
                    for g in range(G):
                        att_normalise(B - 1, g)
                    att_residual(B - 1)


_INS = ["L0_attn_a_x", "L0_attn_a_W_in", "L0_attn_a_b_in", "L0_attn_a_W_gate", "L0_attn_a_b_gate",
        "L0_attn_a_conv_w", "L0_attn_a_conv_b", "L0_attn_a_A_log", "L0_attn_a_D_skip", "L0_attn_a_W_delta",
        "L0_attn_a_b_delta", "L0_attn_a_W_B", "L0_attn_a_W_C", "L0_attn_a_W_out", "L0_attn_a_b_out",
        "L0_attn_b_w_qkv", "L0_attn_b_b_qkv", "L0_attn_b_w_out", "L0_attn_b_b_out", "L0_ffn_wg", "L0_ffn_bg",
        "L0_ffn_Wgate", "L0_ffn_Wup", "L0_ffn_Wdown"]


def kernel(**inputs):
    import numpy as _np
    import concourse.bacc as _bacc
    from concourse import mybir as _mybir
    from concourse.bass_utils import run_bass_kernel_spmd as _run

    nc = _bacc.Bacc("TRN2", target_bir_lowering=False, num_devices=1)
    arrays, args = {}, []
    for name in _INS:
        a = _np.asarray(inputs[name])
        if name in ("L0_ffn_Wgate", "L0_ffn_Wup"):
            a = a.transpose(2, 0, 1)
        elif name == "L0_ffn_Wdown":
            a = a.reshape(a.shape[0], a.shape[1], -1, 128).transpose(3, 0, 2, 1)
        a = _np.ascontiguousarray(a)
        arrays[f"in_{name}_dram"] = a
        args.append(nc.dram_tensor(f"in_{name}_dram", a.shape, _mybir.dt.from_np(a.dtype), kind="ExternalInput").ap())
    p, c, q = _np.arange(128)[:, None], _np.arange(256)[None, :], _np.arange(512)[None, :]
    near = (c - p >= 0) & (c - p <= 128)
    tile = (p % 32) // 4
    covered = (q >= 128 * tile - 64) & (q < 128 * tile + 192) & (p % 32 < 16)
    neg = lambda seen: _np.where(seen, 0.0, -1.0e30)
    spread = (p == 32 * (_np.arange(128)[None, :] // 32) + 8) * 1.0
    consts = _np.concatenate([neg(near | (c % 32 == 0)), neg(near | (p % 32 == 0)), neg(~covered), spread], axis=1)
    arrays["att_consts"] = _np.ascontiguousarray(consts.astype(_np.float32))
    args.append(nc.dram_tensor("att_consts", consts.shape, _mybir.dt.float32, kind="ExternalInput").ap())
    shape = inputs["L0_attn_a_x"].shape
    args.append(nc.dram_tensor("out_0_dram", shape, _mybir.dt.float32, kind="ExternalOutput").ap())
    hybrid_layer_kernel(nc, *args)
    r = _run(nc, [arrays], core_ids=[0])
    return r.results[0]["out_0_dram"]
```

```python
import concourse.bass as bass
from concourse import mybir
from contextlib import ExitStack


def hybrid_layer_kernel(nc, x, w_in, b_in, w_gate, b_gate, conv_w, conv_b, a_log, d_skip, w_delta,
                        b_delta, w_b, w_c, ssm_w_out, ssm_b_out, w_qkv, b_qkv, att_w_out, att_b_out,
                        router_w, router_b, ffn_gate, ffn_up, ffn_down, att_consts, moe_consts, out, stages=None):
    fp32 = mybir.dt.float32
    bf16 = mybir.dt.bfloat16
    ALU = mybir.AluOpType
    ACT = mybir.ActivationFunctionType
    AX = mybir.AxisListType
    if stages is None:
        stages = ("ssm", "moe", "att", "moe")

    B, L, D = x.shape
    P = 128
    T = B * L // P
    TB = L // P
    DI = w_in.shape[1]
    J = DI // P
    NS = w_b.shape[1]
    KC = conv_w.shape[2]
    PAD = KC - 1
    E = router_w.shape[0]
    HID = ffn_gate.shape[2]
    HC = HID // P
    EPS = 1e-5

    TH = T // 2
    NB = (2 * P * TH + E * (P - 1)) // P
    ROUTE_STEPS = 34
    DIGITS = 5
    WORDS = (NB - 3) // (DIGITS - 1) + 1
    OF_PARITY = ((NB + 1) // 2, NB // 2)
    ROWS_B = 4
    LEAD = 4
    DECAYS = 4

    NH = 16
    DH = D // NH
    G = 4
    R = NH // G
    STRIDE, WINDOW = 32, 64
    KS_N = L // STRIDE
    BAND = P + 2 * WINDOW
    reach = [(WINDOW if t == 0 else 0, BAND - (WINDOW if t == TB - 1 else 0)) for t in range(TB)]
    TERMS_Q = (0, 0, 0, 1, 1, 2)
    TERMS_K = (0, 1, 2, 0, 1, 0)
    TR = len(TERMS_Q) * DH

    ctx = ExitStack()
    with ctx:
        def sb(name, shape, dt=fp32):
            return ctx.enter_context(nc.sbuf_tensor(name, shape, dt))

        def sem(name):
            return ctx.enter_context(nc.semaphore(name))

        ts, ds = bass.ts, bass.ds
        bank = [ctx.enter_context(nc.psum_tensor(f"bank{i}", [P, 512], fp32)) for i in range(2)]
        score = [ctx.enter_context(nc.psum_tensor(f"score{i}", [P, 4, BAND], fp32)) for i in range(2)]
        bank += [score[i // 2][:, 2 * (i % 2):2 * (i % 2) + 2, :].rearrange("p a b -> p (a b)") for i in range(4)]
        bank += [ctx.enter_context(nc.psum_tensor(f"bank{i}", [P, 512], fp32)) for i in range(6, 8)]

        X = sb("X", [P, T, D])
        xnT = sb("xnT", [P, T * P])
        ident = sb("ident", [P, P])
        ones_row = sb("ones_row", [1, P])
        stats = sb("stats", [P, T, 6])
        mv = sb("mv", [P, T, 2])
        std = sb("std", [P, T])
        rstd = sb("rstd", [P, T])
        eps_col = sb("eps_col", [P, 1])
        zeros = sb("zeros", [P, D])
        xn = sb("xn", [P, 2, TB, D])

        identb = sb("identb", [P, P], bf16)
        rw_sb = sb("rw_sb", [P, E])
        rb_sb = sb("rb_sb", [P, E])
        wg_sb = sb("wg_sb", [P, E, HID])
        wu_sb = sb("wu_sb", [P, E, HID])
        wd_sb = sb("wd_sb", [P, E, HC, D])

        scr = ExitStack()

        def tmp(name, shape, dt=fp32):
            return scr.enter_context(nc.sbuf_tensor(name, shape, dt))

        w_in_sb = tmp("w_in_sb", [P, DI])
        w_gate_sb = tmp("w_gate_sb", [P, DI])
        w_delta_sb = tmp("w_delta_sb", [P, J, DI])
        w_bc_sb = tmp("w_bc_sb", [P, J, 3, 2 * NS])
        w_out_sb = tmp("w_out_sb", [P, J, D])
        b_out_row = tmp("b_out_row", [1, D])
        b_in_sb = tmp("b_in_sb", [P, J])
        b_gate_sb = tmp("b_gate_sb", [P, J])
        conv_w_sb = tmp("conv_w_sb", [P, J, KC])
        conv_b_sb = tmp("conv_b_sb", [P, J])
        b_delta_sb = tmp("b_delta_sb", [P, J])
        d_skip_sb = tmp("d_skip_sb", [P, J])
        a_log_sb = tmp("a_log_sb", [P, J, NS])
        a_exp = tmp("a_exp", [P, J, NS])
        a_neg = tmp("a_neg", [P, J, NS])
        conv_diag = tmp("conv_diag", [P, J, KC, P])
        pick = tmp("pick", [3 * 2 * NS, 2 * NS, P], bf16)
        xz = tmp("xz", [P, 2, J, PAD + L])
        lin = tmp("lin", [P, 2 * J, L])
        gact = tmp("gact", [P, 2, 2 * J, L])
        act_x = gact[:, :, J:, :]
        gate = gact[:, :, 0:J, :]
        pre_dt = tmp("pre_dt", [P, J, L])
        soft = tmp("soft", [P, J, L])
        dt = tmp("dt", [P, 2, J, L])
        u = tmp("u", [P, 2, J, L])
        bc_f = tmp("bc_f", [3 * 2 * NS, L])
        bc_r = tmp("bc_r", [3 * 2 * NS, L])
        bc_p2 = tmp("bc_p2", [3 * 2 * NS, L], bf16)
        bc_r2 = tmp("bc_r2", [3 * 2 * NS, L])
        bc3 = tmp("bc3", [3 * 2 * NS, 2, L], bf16)
        b_sb = tmp("b_sb", [P, ROWS_B, L])
        dbu = tmp("dbu", [P, 2, J, L])
        h = tmp("h", [P, 2, J, L])
        hc = tmp("hc", [P, 2, J, L])
        gated = tmp("gated", [P, J, L])

        bank_b, bank_c = [bank[0], bank[1]], [bank[2], bank[3]]
        decay = [[wd_sb[:, J * q + j, :, :].rearrange("p c d -> p (c d)") for j in range(J)] for q in range(DECAYS)]
        bank_y = [bank[4], bank[5]]
        bank_pre = [bank[6], bank[7]]
        scr.close()

        scr = ExitStack()
        xna = tmp("xna", [P, T, D])
        logits = tmp("logits", [P, TH, E])
        lrank = tmp("lrank", [P, TH, E])
        rest = tmp("rest", [P, TH, E])
        one1 = tmp("one1", [P, TH, E])
        one2 = tmp("one2", [P, TH, E])
        both = tmp("both", [P, TH, E])
        top = tmp("top", [P, 6, TH])
        pick_w = tmp("pick_w", [P, 2, 2, TH])
        tot = tmp("tot", [P, E, TH])
        upto = tmp("upto", [P, E, TH])
        over = tmp("over", [P, E, TH])
        n_blocks = tmp("n_blocks", [P, E])
        ends = tmp("ends", [P, E])
        starts = tmp("starts", [P, E])
        place = tmp("place", [P, E, TH])
        placed = tmp("placed", [P, 2, TH, E])
        row_f = tmp("row_f", [P, 2, TH])
        row = tmp("row", [P, 2, 2, TH], mybir.dt.uint32)
        ended = tmp("ended", [1, NB, E])
        expert_f = tmp("expert_f", [1, 2 + NB])
        word = tmp("word", [1, WORDS])
        expert = tmp("expert", [1, 2, WORDS], mybir.dt.int32)
        mc = tmp("mc", [P, 2 * P + E * TH + TH + NB + E + E])
        xg = tmp("xg", [P, 2, D])
        xgT = tmp("xgT", [P, 2, P])
        sg = tmp("sg", [P, 2, HID])
        hid = tmp("hid", [P, 2, HID])
        hidT = tmp("hidT", [P, 2, HC, P])
        y_sb = tmp("y_sb", [P, 2, D])
        yg = tmp("yg", [P, 2, 2, TH, D])
        mc_parts, at = [], 0
        for n in (P, P, E * TH, TH, NB, E, E):
            mc_parts.append(mc[:, at:at + n])
            at += n
        before, ones_sq, keep, thresholds, counting, fall, ones_e = mc_parts
        scr.close()

        scr = ExitStack()
        xt = tmp("xt", [P, 2, L])
        wqkv_sb = tmp("wqkv_sb", [P, 3 * D])
        wo_sb = tmp("wo_sb", [P, G, D])
        bo_row = tmp("bo_row", [1, D])
        bqk_sb = tmp("bqk_sb", [P, 2])
        bv_all = tmp("bv_all", [P, NH, DH])
        bv_str = tmp("bv_str", [P, G, DH])
        consts_f = tmp("consts_f", [P, 2 * BAND + L + P])
        consts_b = tmp("consts_b", [P, 2 * BAND + L], bf16)
        qk_f = tmp("qk_f", [P, 2, L])
        qk_r = tmp("qk_r", [P, 2, L])
        qk_p = tmp("qk_p", [P, 2, 3, L], bf16)
        qs = tmp("qs", [P, 2, NH // 2, L], bf16)
        ks = tmp("ks", [P, 2, NH // 2, L], bf16)
        va = tmp("va", [P, 2, TB, NH, 32])
        vs_ = tmp("vs_", [P, 2, G, 32])
        mxw = tmp("mxw", [P, TB, 2, NH // 2])
        mxs = tmp("mxs", [P, TB, 2, NH // 2])
        mxn = tmp("mxn", [P, TB, 2, NH // 2])
        m_f = tmp("m_f", [NH, L])
        m_r = tmp("m_r", [NH, L])
        m_p = tmp("m_p", [NH, 3, L], bf16)
        pt = tmp("pt", [P, 2, TB * BAND])
        pts = tmp("pts", [P, 2, L])
        ots = tmp("ots", [P, 2, L])
        otn = tmp("otn", [P, G, L])
        rden = tmp("rden", [P, L])
        scr.close()
        band_q = consts_b[:, 0:BAND]
        band_k = consts_b[:, BAND:2 * BAND]
        far_k = consts_b[:, 2 * BAND:]
        den_pick = consts_f[:, 2 * BAND + L:]
        sorted_x = [nc.dram_tensor(f"sorted_x{c}", (NB * P, D), fp32).ap() for c in range(2)]
        sorted_y = [nc.dram_tensor(f"sorted_y{c}", (NB * P, D), fp32).ap() for c in range(2)]
        qk_dram = nc.dram_tensor("qk_parts", (2, 2, 3, P, L), bf16).ap()

        s_x = [sem(f"s_x{c}") for c in range(4)]
        s_cst = sem("s_cst")
        s_lnst = sem("s_lnst")
        s_var = sem("s_var")
        s_std = sem("s_std")
        s_rstd = sem("s_rstd")
        s_xn = sem("s_xn")
        s_xt = sem("s_xt")
        s_xnT = sem("s_xnT")
        s_w = sem("s_w")
        s_aneg = sem("s_aneg")
        s_diag = sem("s_diag")
        s_unit = sem("s_unit")
        s_unita = sem("s_unita")
        s_silu = sem("s_silu")
        s_soft = sem("s_soft")
        s_bc = sem("s_bc")
        s_dt = sem("s_dt")
        s_u = sem("s_u")
        s_bcs = sem("s_bcs")
        s_bc3 = sem("s_bc3")
        s_bb = sem("s_bb")
        s_cb = sem("s_cb")
        s_bcp = sem("s_bcp")
        s_da = sem("s_da")
        s_dbu = sem("s_dbu")
        s_h = sem("s_h")
        s_hc = sem("s_hc")
        s_y = sem("s_y")
        s_yd = sem("s_yd")
        s_gt = sem("s_gt")
        s_op = sem("s_op")
        s_res = sem("s_res")
        s_wf = sem("s_wf")
        s_wd = sem("s_wd")
        s_lg = sem("s_lg")
        s_rt = sem("s_rt")
        s_df = sem("s_df")
        s_re = sem("s_re")
        s_both = sem("s_both")
        s_pr = sem("s_pr")
        s_row = sem("s_row")
        s_mc = sem("s_mc")
        s_z = sem("s_z")
        s_xna = sem("s_xna")
        s_sc = [sem(f"s_sc{c}") for c in range(2)]
        s_xl = [sem(f"s_xl{p}") for p in range(2)]
        s_tx = sem("s_tx")
        s_xgT = sem("s_xgT")
        s_g = sem("s_g")
        s_sg = sem("s_sg")
        s_up = sem("s_up")
        s_hd = sem("s_hd")
        s_th = sem("s_th")
        s_ht = sem("s_ht")
        s_dn = sem("s_dn")
        s_yb = sem("s_yb")
        s_ys = [sem(f"s_ys{p}") for p in range(2)]
        s_yg = [sem(f"s_yg{g}") for g in range(TB)]
        s_a1 = sem("s_a1")
        s_ad = sem("s_ad")
        s_out = sem("s_out")
        a_w = sem("a_w")
        a_cst = sem("a_cst")
        a_wo = sem("a_wo")
        a_xt = sem("a_xt")
        a_qk = sem("a_qk")
        a_qf = sem("a_qf")
        a_sa = sem("a_sa")
        a_sp = sem("a_sp")
        a_st = sem("a_st")
        a_ld = [sem(f"a_ld{p}") for p in range(2)]
        a_v = sem("a_v")
        a_va = sem("a_va")
        a_s = sem("a_s")
        a_ss = sem("a_ss")
        a_mx = sem("a_mx")
        a_ms = sem("a_ms")
        a_mm = sem("a_mm")
        a_mn = sem("a_mn")
        a_mt = sem("a_mt")
        a_ma = sem("a_ma")
        a_mp = sem("a_mp")
        a_ml = [sem(f"a_ml{p}") for p in range(2)]
        a_t = sem("a_t")
        a_tf = sem("a_tf")
        a_e = sem("a_e")
        a_ef = sem("a_ef")
        a_pv = sem("a_pv")
        a_ot = sem("a_ot")
        a_dn = sem("a_dn")
        a_rd = sem("a_rd")
        a_on = sem("a_on")
        a_op = sem("a_op")
        a_res = sem("a_res")

        block = ctx.enter_context(nc.Block())

        @block.sync
        def _(sp):
            xv = x.rearrange("b (t p) d -> p (b t) d", p=P)
            for c in range(4):
                sp.dma_start(X[:, ts(c, T // 4), :], xv[:, ts(c, T // 4), :]).then_inc(s_x[c], 16)
            nc_allow = ctx.enter_context(nc.allow_non_contiguous_dma(reason="small per-channel vectors"))
            if "ssm" in stages:
                col = lambda v: v.rearrange("(j p) -> p j", p=P)
                loads = [
                    (w_in_sb[:, :], w_in), (w_gate_sb[:, :], w_gate),
                    (w_delta_sb[:, :, :], w_delta.rearrange("(j p) n -> p j n", p=P)),
                    (w_out_sb[:, :, :], ssm_w_out.rearrange("(j p) n -> p j n", p=P)),
                    (b_out_row[:, :], ssm_b_out.rearrange("(a n) -> a n", a=1)),
                    (b_in_sb[:, :], col(b_in)), (b_gate_sb[:, :], col(b_gate)),
                    (conv_w_sb[:, :, :], conv_w.rearrange("(j p) a k -> p j (a k)", p=P)),
                    (conv_b_sb[:, :], col(conv_b)), (b_delta_sb[:, :], col(b_delta)),
                    (d_skip_sb[:, :], col(d_skip)),
                    (a_log_sb[:, :, :], a_log.rearrange("(j p) n -> p j n", p=P)),
                ]
                for r in range(3):
                    loads.append((w_bc_sb[:, :, r, 0:NS], w_b.rearrange("(j p) n -> p j n", p=P)))
                    loads.append((w_bc_sb[:, :, r, NS:2 * NS], w_c.rearrange("(j p) n -> p j n", p=P)))
                assert len(loads) == 18
                for dst, src in loads:
                    sp.dma_start(dst, src).then_inc(s_w, 16)
            if "moe" in stages:
                for dst, src in [
                    (rw_sb[:, :], router_w.rearrange("e d -> d e")),
                    (rb_sb[:, :], router_b.rearrange("(a e) -> a e", a=1).to_broadcast([P, E])),
                    (wg_sb[:, :, :], ffn_gate), (wu_sb[:, :, :], ffn_up),
                ]:
                    sp.dma_start(dst, src).then_inc(s_wf, 16)
                sp.wait_ge(s_cst, 3)
                for c in range(2):
                    sp.dma_start(sorted_x[c].rearrange("(n p) d -> p n d", p=P),
                                 zeros[:, None, :].to_broadcast([P, NB, D])).then_inc(s_z, 16)

            def moe_blocks(m, c):
                q = 2 * m + c
                sp.wait_ge(s_sc[c], 16 * 2 * TH * (m + 1))

                def load(j, p):
                    if not (isinstance(j, int) and j < 2):
                        sp.wait_ge(s_tx, q * NB + j - 1)
                    sp.dma_start(xg[:, p, :], sorted_x[c][ts(j, P), :]).then_inc(s_xl[p], 16)

                def store(j, p):
                    sp.wait_ge(s_yb, q * NB + j + 1)
                    sp.dma_start(sorted_y[c][ts(j, P), :], y_sb[:, p, :]).then_inc(s_ys[p], 16)

                load(0, 0)
                load(1, 1)
                load(2, 0)
                with sp.Fori(0, (NB - 3) // 2) as i:
                    for p in range(2):
                        load(2 * i + 3 + p, 1 - p)
                        store(2 * i + p, p)
                for j in range(NB - 3, NB):
                    store(j, j % 2)

            def moe(k):
                m = stages[:k].count("moe")
                if k and stages[k - 1] == "ssm":
                    sp.wait_ge(s_res, B)
                elif k:
                    sp.wait_ge(a_res, B)
                sp.dma_start(mc[:, :], moe_consts).then_inc(s_mc, 16)
                if m == 0:
                    sp.dma_start(wd_sb[:, :, :, :], ffn_down).then_inc(s_wd, 16)
                for c in range(2):
                    moe_blocks(m, c)

            def attention(k):
                if k and stages[k - 1] == "moe":
                    sp.wait_ge(s_ad, T)
                sp.wait_ge(s_cst, 7)
                bv = b_qkv[2 * D:]
                loads = [(wqkv_sb[:, :], w_qkv), (bo_row[:, :], att_b_out.rearrange("(a n) -> a n", a=1)),
                         (bqk_sb[:, :], b_qkv[0:2 * D].rearrange("(c p) -> p c", p=P)),
                         (bv_all[:, :, :], bv.rearrange("(a h d) -> a h d", a=1, h=NH).to_broadcast([P, NH, DH])),
                         (consts_f[:, :], att_consts)]
                for r in range(R):
                    loads.append((bv_str[ts(r, 32), :, :],
                                  bv.rearrange("(g r d) -> r g d", g=G, r=R)[r:r + 1].to_broadcast([32, G, DH])))
                for dst, src in loads:
                    sp.dma_start(dst, src).then_inc(a_w, 16)
                sp.wait_ge(a_cst, 1)
                for r in range(R):
                    sp.dma_start(wo_sb[32 * r:32 * r + DH, :, :],
                                 att_w_out.rearrange("(g r d) n -> r d g n", g=G, r=R)[r]).then_inc(a_wo, 16)

                def stack(b, p):
                    sp.wait_ge(a_sp, 2 * b + 2)
                    if not (isinstance(b, int) and b < 2):
                        sp.wait_ge(a_pv, NH * (b - 1))
                    sp.dma_start(qk_dram[p].rearrange("c t p n -> p c t n"), qk_p[:, :, :, :]).then_inc(a_st, 16)
                    sp.wait_ge(a_st, 16 * b + 16)
                    for c, (dst, terms) in enumerate(((qs, TERMS_Q), (ks, TERMS_K))):
                        for z in range(2):
                            for i, t in enumerate(terms):
                                src = qk_dram[p, c, t].rearrange("(m z d) n -> z d m n", z=2, d=DH)[z]
                                at = 64 * z + DH * i
                                sp.dma_start(dst[at:at + DH, p, :, :], src).then_inc(a_ld[p], 16)

                def stack_max(b, p):
                    sp.wait_ge(a_mp, 2 * b + 2)
                    for z in range(2):
                        for t in range(3):
                            at = 64 * z + TR + t
                            sp.dma_start(qs[at:at + 1, p, :, :], m_p[ts(z, NH // 2), t, :]).then_inc(a_ml[p], 16)

                for b in range(2):
                    stack(b, b)
                    stack_max(b, b)
                with sp.Fori(0, (B - 2) // 2) as i:
                    for p in range(2):
                        stack(2 * i + 2 + p, p)
                        stack_max(2 * i + 2 + p, p)
            for k, stage in enumerate(stages):
                if stage == "moe":
                    moe(k)
                elif stage == "att":
                    attention(k)
            last = stages[-1]
            if last == "moe":
                sp.wait_ge(s_ad, T * stages.count("moe"))
            elif last == "ssm":
                sp.wait_ge(s_res, B)
            else:
                sp.wait_ge(a_res, B)
            ov = out.rearrange("b (t p) d -> p (b t) d", p=P)
            for c in range(4):
                sp.dma_start(ov[:, ts(c, T // 4), :], X[:, ts(c, T // 4), :]).then_inc(s_out, 16)
            sp.wait_ge(s_out, 64)

        @block.gpsimd
        def _(pool):
            nc.gpsimd.memset(ident[:, :], 0.0).then_inc(s_cst, 1)
            nc.gpsimd.memset(ones_row[:, :], 1.0)
            nc.gpsimd.memset(eps_col[:, :], EPS)
            nc.gpsimd.memset(zeros[:, :], 0.0)
            nc.gpsimd.memset(xz[:, :, :, 0:PAD], 0.0)
            nc.gpsimd.memset(pick[:, :, :], 0.0).then_inc(s_cst, 1)
            pool.wait_ge(s_cst, 2)
            nc.gpsimd.affine_select(out=ident[:, :], in_=ident[:, :], compare_op=ALU.not_equal, fill=1.0,
                                    base=0, pattern=[[-1, P]], channel_multiplier=1).then_inc(s_cst, 1)
            for k in range(3):
                if k:
                    pool.wait_ge(s_cst, 3 + k)
                nc.gpsimd.affine_select(out=pick[:, :, :], in_=pick[:, :, :], compare_op=ALU.not_equal,
                                        fill=1.0, base=-2 * NS * k, pattern=[[-1, 2 * NS], [0, P]],
                                        channel_multiplier=1).then_inc(s_cst, 1)

            pool.wait_ge(s_cst, 6)
            nc.gpsimd.tensor_copy(identb[:, :], ident[:, :]).then_inc(s_cst, 1)

            def ssm_split_bc(b, p, k):
                if k == 0:
                    pool.wait_ge(s_bc, b + 1)
                    nc.gpsimd.tensor_tensor(bc_r[:, :], bc_f[:, :], bc3[:, p, :], ALU.subtract).then_inc(s_bcs, 1)
                elif k == 1:
                    if not (isinstance(b, int) and b == 0):
                        pool.wait_ge(s_bc3, b)
                    nc.gpsimd.tensor_tensor(bc_p2[:, :], bc_f[:, :], bc3[:, p, :], ALU.subtract).then_inc(s_bcs, 1)
                else:
                    pool.wait_ge(s_bcs, 3 * b + 2)
                    nc.gpsimd.tensor_tensor(bc_r2[:, :], bc_r[:, :], bc_p2[:, :], ALU.subtract).then_inc(s_bcs, 1)

            def ssm_u(b, p):
                pool.wait_ge(s_dt, b + 1)
                nc.gpsimd.tensor_tensor(u[:, p, :, :], dt[:, p, :, :], act_x[:, p, :, :], ALU.mult).then_inc(s_u, 1)

            def ssm_batch(b, p, last):
                for n in range(NS):
                    if n == 0:
                        pool.wait_ge(s_u, b + 1)
                    pool.wait_ge(s_bcp, NS * b + n + 1)
                    if not (isinstance(b, int) and b == 0 and n < 2):
                        pool.wait_ge(s_h, 2 * (NS * b + n - 1))
                    nc.gpsimd.tensor_tensor(dbu[:, n % 2, :, :], u[:, p, :, :],
                                            b_sb[:, n % ROWS_B, None, :].to_broadcast([P, J, L]),
                                            ALU.mult).then_inc(s_dbu, 1)
                    if not last and n == 10:
                        ssm_split_bc(b + 1, 1 - p, 0)
                        ssm_split_bc(b + 1, 1 - p, 1)
                    if not last and n == 11:
                        ssm_split_bc(b + 1, 1 - p, 2)
                    if not last and n == 14:
                        ssm_u(b + 1, 1 - p)

            if "ssm" in stages:
                for k in range(3):
                    ssm_split_bc(0, 0, k)
                ssm_u(0, 0)
                ssm_batch(0, 0, False)
                with pool.Fori(0, (B - 2) // 2) as i:
                    ssm_batch(2 * i + 1, 1, False)
                    ssm_batch(2 * i + 2, 0, False)
                ssm_batch(B - 1, 1, True)

            def moe(m):
                for c in range(2):
                    q = 2 * m + c
                    pool.wait_ge(s_row, q + 1)
                    pool.wait_ge(s_z, 32)
                    for t in range(TH):
                        for k in range(2):
                            nc.gpsimd.indirect_dma_start(
                                sorted_x[c], bass.IndirectOffsetOnAxis(ap=row[:, c, k, t:t + 1], axis=0),
                                xna[:, TH * c + t, :], None).then_inc(s_sc[c], 16)
                for c in range(2):
                    q = 2 * m + c
                    for p in range(2):
                        pool.wait_ge(s_ys[p], 16 * OF_PARITY[p] * (q + 1))
                    for t in range(TH):
                        for k in range(2):
                            nc.gpsimd.indirect_dma_start(
                                yg[:, c, k, t, :], None, sorted_y[c],
                                bass.IndirectOffsetOnAxis(ap=row[:, c, k, t:t + 1], axis=0)).then_inc(s_yg[t // TB], 16)

            if "moe" in stages and stages[0] != "att":
                moe(0)

            if "att" in stages:
                if stages[0] == "moe" or stages[:2] == ("ssm", "moe"):
                    pool.wait_ge(s_ad, T)
                nc.gpsimd.memset(wo_sb[:, :, :], 0.0).then_inc(a_cst, 1)
                nc.gpsimd.memset(va[:, :, :, :, :], 0.0).then_inc(a_cst, 1)
                nc.gpsimd.memset(vs_[:, :, :, :], 0.0).then_inc(a_cst, 1)
                nc.gpsimd.memset(ks[:, :, :, :], 1.0).then_inc(a_cst, 1)
                pool.wait_ge(a_cst, 4)
                nc.gpsimd.memset(va[:, :, :, :, DH:DH + 1], 1.0).then_inc(a_cst, 1)
                for r in range(R):
                    nc.gpsimd.memset(vs_[32 * r:32 * r + KS_N, :, :, DH:DH + 1], 1.0).then_inc(a_cst, 1)
                    pool.wait_ge(a_cst, 6 + r)
                pool.wait_ge(a_w, 16 * 9)
                nc.gpsimd.tensor_copy(consts_b[:, :], consts_f[:, 0:2 * BAND + L]).then_inc(a_cst, 1)
                k_att = stages.index("att")

                def att_xt(b, p):
                    if not (isinstance(b, int) and b < 2):
                        pool.wait_ge(a_v, b - 1)
                    pool.wait_ge(s_xnT, B * (k_att + 1))
                    nc.gpsimd.tensor_copy(xt[:, p, :], xnT[:, ts(b, L)]).then_inc(a_xt, 1)

                def att_split(b, p):
                    pool.wait_ge(a_sa, 2 * b + 1)
                    nc.gpsimd.tensor_tensor(qk_r[:, :, :], qk_f[:, :, :], qk_p[:, :, 0, :], ALU.subtract).then_inc(a_sp, 1)
                    pool.wait_ge(a_sa, 2 * b + 2)
                    pool.wait_ge(a_sp, 2 * b + 1)
                    nc.gpsimd.tensor_tensor(qk_p[:, :, 2, :], qk_r[:, :, :], qk_p[:, :, 1, :], ALU.subtract).then_inc(a_sp, 1)

                def att_split_max(b, p):
                    pool.wait_ge(a_ma, 3 * b + 2)
                    nc.gpsimd.tensor_tensor(m_r[:, :], m_f[:, :], m_p[:, 0, :], ALU.subtract).then_inc(a_mp, 1)
                    pool.wait_ge(a_ma, 3 * b + 3)
                    pool.wait_ge(a_mp, 2 * b + 1)
                    nc.gpsimd.tensor_tensor(m_p[:, 2, :], m_r[:, :], m_p[:, 1, :], ALU.subtract).then_inc(a_mp, 1)

                def att_next(b, p, last=False):
                    att_split(b, p)
                    if not last:
                        att_xt(b + 1, 1 - p)
                    att_split_max(b, p)

                att_xt(0, 0)
                att_next(0, 0)
                att_next(1, 1)
                with pool.Fori(0, (B - 4) // 2) as i:
                    att_next(2 * i + 2, 0)
                    att_next(2 * i + 3, 1)
                att_next(B - 2, 0)
                att_next(B - 1, 1, True)
                if stages[-1] == "moe":
                    moe(stages.count("moe") - 1)

        @block.scalar
        def _(act):
            def layer_norm(k):
                for c in range(2):
                    act.wait_ge(s_var, 2 * k + c + 1)
                    if k == 0 and c == 0:
                        act.wait_ge(s_cst, 2 if stages[0] == "ssm" else 7)
                    nc.scalar.activation(std[:, ts(c, TH)], mv[:, ts(c, TH), 1], ACT.Sqrt, bias=eps_col[:, :]).then_inc(s_std, 1)
                    for b in range(c * B // 2, (c + 1) * B // 2):
                        act.wait_ge(s_xt, B * k + b + 1)
                        nc.scalar.activation(xnT[:, ts(b, L)], bank[b % 2][:, :], ACT.Copy).then_inc(s_xnT, 1)
                    if stages[k] == "moe":
                        q = 2 * stages[:k].count("moe") + c
                        act.wait_ge(s_df, q + 1)
                        nc.scalar.activation(top[:, 3, :], top[:, 2, :], ACT.Exp).then_inc(s_re, 1)

            def ssm_read(b, p, k):
                act.wait_ge(s_unit, 9 * b + k + 1)
                ps = bank_pre[(k + (k > 5)) % 2]
                if k in (0, 1):
                    nc.scalar.activation(xz[:, p, k, PAD:], ps[:, :], ACT.Identity,
                                         bias=b_in_sb[:, k:k + 1]).then_inc(s_unita, 1)
                elif k in (2, 3):
                    if k == 2 and not (isinstance(b, int) and b == 0):
                        act.wait_ge(s_silu, b)
                    nc.scalar.activation(lin[:, k - 2, :], ps[:, :], ACT.Identity,
                                         bias=b_gate_sb[:, k - 2:k - 1]).then_inc(s_unita, 1)
                elif k in (4, 5):
                    nc.scalar.activation(lin[:, J + k - 4, :], ps[:, :], ACT.Identity,
                                         bias=conv_b_sb[:, k - 4:k - 3]).then_inc(s_unita, 1)
                elif k == 6:
                    if not (isinstance(b, int) and b == 0):
                        act.wait_ge(s_bcs, 3 * b)
                    nc.scalar.activation(bc_f[:, :], ps[0:96, :], ACT.Copy).then_inc(s_unita, 1)
                    act.wait_ge(s_unita, 9 * b + 7)
                    nc.scalar.activation(bc3[:, p, :], bc_f[:, :], ACT.Copy).then_inc(s_bc, 1)
                else:
                    if k == 7 and not (isinstance(b, int) and b == 0):
                        act.wait_ge(s_dt, b)
                    nc.scalar.activation(pre_dt[:, k - 7, :], ps[:, :], ACT.Identity,
                                         bias=b_delta_sb[:, k - 7:k - 6]).then_inc(s_unita, 1)

            def ssm_silu(b, p):
                act.wait_ge(s_unita, 9 * b + 6)
                if not (isinstance(b, int) and b < 2):
                    act.wait_ge(s_gt, b - 1)
                nc.scalar.activation(gact[:, p, :, :], lin[:, :, :], ACT.Silu).then_inc(s_silu, 1)
                nc.scalar.preload_act_table_set("natural_log_exp_and_others")

            def ssm_soft(b, k):
                if k == 0:
                    act.wait_ge(s_unita, 9 * b + 9)
                    nc.scalar.activation(soft[:, :, :], pre_dt[:, :, :], ACT.Abs).then_inc(s_soft, 1)
                elif k == 1:
                    act.wait_ge(s_soft, 3 * b + 1)
                    nc.scalar.activation(soft[:, :, :], soft[:, :, :], ACT.Exp, scale=-1.0).then_inc(s_soft, 1)
                else:
                    act.wait_ge(s_soft, 3 * b + 2)
                    nc.scalar.activation(soft[:, :, :], soft[:, :, :], ACT.Ln, bias=1.0).then_inc(s_soft, 1)

            def ssm_prepare(b, p, n):
                for k in {3: (0, 1), 4: (2,), 5: (3,), 7: (4,), 9: (5,), 11: (6,), 12: (7,), 13: (8,)}.get(n, ()):
                    ssm_read(b, p, k)
                if n == 9:
                    ssm_silu(b, p)
                for k in {14: (0, 1), 15: (2,)}.get(n, ()):
                    ssm_soft(b, k)

            def ssm_row_b(b, n):
                act.wait_ge(s_bb, NS * b + n + 1)
                if not (isinstance(b, int) and b == 0 and n < ROWS_B):
                    act.wait_ge(s_dbu, NS * b + n + 1 - ROWS_B)
                nc.scalar.activation(b_sb[:, n % ROWS_B, :], bank_b[n % 2][:, :], ACT.Copy).then_inc(s_bcp, 1)

            def ssm_batch(b, p, first, last):
                if first:
                    ssm_row_b(b, 0)
                for n in range(NS):
                    if n + 1 < NS:
                        ssm_row_b(b, n + 1)
                    elif not last:
                        ssm_row_b(b + 1, 0)
                    for j in range(J):
                        if n == 0 and j == 0:
                            act.wait_ge(s_dt, b + 1)
                        if not (first and n < DECAYS):
                            act.wait_ge(s_h, 2 * (NS * b + n - DECAYS) + j + 1)
                        nc.scalar.activation(decay[n % DECAYS][j], dt[:, p, j, :], ACT.Exp,
                                             scale=a_neg[:, j, n:n + 1]).then_inc(s_da, 1)
                    if not last:
                        ssm_prepare(b + 1, 1 - p, n)

            def moe_blocks(m, c):
                base = (2 * m + c) * NB

                def tokens(j, p):
                    act.wait_ge(s_tx, base + j + 1)
                    if not (isinstance(base + j, int) and base + j < 2):
                        act.wait_ge(s_up, base + j - 1)
                    nc.scalar.activation(xgT[:, p, :], bank[5][:, 0:P], ACT.Copy).then_inc(s_xgT, 1)

                def silu(j, p):
                    act.wait_ge(s_g, base + j + 1)
                    if not (isinstance(base + j, int) and base + j < 2):
                        act.wait_ge(s_hd, base + j - 1)
                    nc.scalar.activation(sg[:, p, :], bank[p][:, :], ACT.Silu).then_inc(s_sg, 1)

                def turned(j, p):
                    act.wait_ge(s_th, base + j + 1)
                    if not (isinstance(base + j, int) and base + j < 2):
                        act.wait_ge(s_dn, base + j - 1)
                    nc.scalar.activation(hidT[:, p, :, :], bank[4][:, :].rearrange("p (c n) -> p c n", c=HC),
                                         ACT.Copy).then_inc(s_ht, 1)

                def step(j, p):
                    if not (isinstance(j, int) and j == 0):
                        turned(j - 1, 1 - p)
                    silu(j, p)
                    if not (isinstance(j, int) and j == NB - 1):
                        tokens(j + 1, 1 - p)

                tokens(0, 0)
                for j in range(2):
                    step(j, j)
                with act.Fori(1, NB // 2) as i:
                    for p in range(2):
                        step(2 * i + p, p)
                step(NB - 1, 0)
                turned(NB - 1, 0)

            def att_split(b, p):
                act.wait_ge(a_qf, b + 1)
                if not (isinstance(b, int) and b == 0):
                    act.wait_ge(a_st, 16 * b)
                nc.scalar.activation(qk_p[:, :, 0, :], qk_f[:, :, :], ACT.Copy).then_inc(a_sa, 1)
                act.wait_ge(a_sp, 2 * b + 1)
                nc.scalar.activation(qk_p[:, :, 1, :], qk_r[:, :, :], ACT.Copy).then_inc(a_sa, 1)

            def att_split_max(b, p, k):
                act.wait_ge(a_mt, b + 1)
                if not (isinstance(b, int) and b == 0):
                    act.wait_ge(a_ml[1 - p], 96 * (k + p))
                nc.scalar.activation(m_f[:, :], bank[0][0:NH, :], ACT.Copy).then_inc(a_ma, 1)
                act.wait_ge(a_ma, 3 * b + 1)
                nc.scalar.activation(m_p[:, 0, :], m_f[:, :], ACT.Copy).then_inc(a_ma, 1)
                act.wait_ge(a_mp, 2 * b + 1)
                nc.scalar.activation(m_p[:, 1, :], m_r[:, :], ACT.Copy).then_inc(a_ma, 1)

            def att_exps(b, p):
                def sums(g):
                    act.wait_ge(a_pv, NH * b + R * (g + 1))
                    if not (isinstance(b, int) and b == 0 and g < 2):
                        act.wait_ge(a_on, G * b + g - 1)
                    nc.scalar.activation(ots[:, g % 2, :], bank[6 + g % 2][:, :], ACT.Copy).then_inc(a_ot, 1)

                for h_ in range(NH):
                    g = h_ // R
                    if h_ % R == 0:
                        act.wait_ge(a_tf, G * b + g + 1)
                        if not (isinstance(b, int) and b == 0 and g < 2):
                            act.wait_ge(a_pv, NH * b + R * (g - 1))
                        nc.scalar.activation(pts[:, g % 2, :], bank[1][:, :], ACT.Exp).then_inc(a_ef, 1)
                    act.wait_ge(a_t, NH * b + h_ + 1)
                    if not (isinstance(b, int) and b == 0 and h_ < 2):
                        act.wait_ge(a_pv, NH * b + h_ - 1)
                    nc.scalar.activation(pt[:, h_ % 2, WINDOW:TB * BAND - WINDOW],
                                         score[h_ % 2][:, :, :].rearrange("p a b -> p (a b)")[:, WINDOW:TB * BAND - WINDOW],
                                         ACT.Exp).then_inc(a_e, 1)
                    if h_ >= R + 1 and (h_ - R - 1) % R == 0:
                        sums((h_ - R - 1) // R)
                sums(G - 1)

            for k, stage in enumerate(stages):
                layer_norm(k)
                if stage == "ssm":
                    act.wait_ge(s_w, 16 * 18)
                    nc.scalar.activation(a_exp[:, :, :], a_log_sb[:, :, :], ACT.Exp).then_inc(s_aneg, 1)
                    act.wait_ge(s_aneg, 1)
                    nc.scalar.mul(a_neg[:, :, :], a_exp[:, :, :], -1.0).then_inc(s_aneg, 1)
                    act.wait_ge(s_aneg, 2)
                    for n in range(NS):
                        ssm_prepare(0, 0, n)
                    ssm_batch(0, 0, True, False)
                    with act.Fori(0, (B - 2) // 2) as i:
                        ssm_batch(2 * i + 1, 1, False, False)
                        ssm_batch(2 * i + 2, 0, False, False)
                    ssm_batch(B - 1, 1, False, True)
                elif stage == "moe":
                    for c in range(2):
                        moe_blocks(stages[:k].count("moe"), c)
                else:
                    att_split(0, 0)
                    att_split_max(0, 0, 0)
                    att_split(1, 1)
                    att_exps(0, 0)
                    att_split_max(1, 1, 0)
                    with act.Fori(0, (B - 2) // 2) as i:
                        for p in range(2):
                            b = 2 * i + 1 + p
                            att_split(b + 1, p)
                            att_exps(b, 1 - p)
                            att_split_max(b + 1, p, i + 1)
                    att_exps(B - 1, 1)

        @block.tensor
        def _(pe):
            def layer_norm(k):
                if k == 0:
                    pe.wait_ge(s_cst, 3)
                moe = stages[k] == "moe"
                for b in range(B):
                    p = b % 2
                    pe.wait_ge(s_xn, B * k + b + 1)
                    if B * k + b >= 2:
                        pe.wait_ge(s_xnT, B * k + b - 1)
                    for t in range(TB):
                        src = xna[:, TB * b + t, :] if moe else xn[:, p, t, :]
                        mm = nc.tensor.transpose(bank[p][:, ts(t, P)], src, ident[:, :])
                    mm.then_inc(s_xt, 1)
                    if moe and b % (B // 2) == B // 2 - 1:
                        moe_route(k, 2 * b // B)

            def moe_route(k, c):
                m = stages[:k].count("moe")
                pe.wait_ge(s_xnT, B * k + (c + 1) * B // 2)
                pe.wait_ge(s_wf, 16 * 4)
                if c:
                    pe.wait_ge(s_row, 2 * m + c)
                for t in range(TH):
                    mm = nc.tensor.matmul(bank[7][:, ts(t, E)], xnT[:, ts(TH * c + t, P)], rw_sb[:, :], start=True,
                                          stop=True, skip_group_check=True)
                mm.then_inc(s_lg, 1)
                pe.wait_ge(s_both, 2 * m + c + 1)
                flat = both[:, :, :].rearrange("p t e -> p (t e)")
                nc.tensor.matmul(bank[6][:, 0:TH * E], ones_sq, flat, start=True, stop=True, skip_group_check=True)
                nc.tensor.matmul(bank[6][:, TH * E:2 * TH * E], before, flat, start=True, stop=True,
                                 skip_group_check=True).then_inc(s_pr, 1)

            def ssm_unit(b, p, k, part=None):
                if k == 0:
                    if not (isinstance(b, int) and b == 0):
                        pe.wait_ge(s_unita, 9 * b - 1)
                elif k == 1:
                    if not (isinstance(b, int) and b == 0):
                        pe.wait_ge(s_unita, 9 * b)
                elif k == 7:
                    if not (isinstance(b, int) and b < 2):
                        pe.wait_ge(s_res, b - 1)
                elif not part:
                    pe.wait_ge(s_unita, 9 * b + (k - 1 if k < 6 else k if k == 6 else 7))
                ps = bank_pre[(k + (k > 5)) % 2]
                xs = xnT[:, ts(b, L)]
                if k < 4:
                    w = w_in_sb if k < 2 else w_gate_sb
                    mm = nc.tensor.matmul(ps[:, :], w[:, ts(k % 2, P)], xs, start=True, stop=True)
                elif k < 6:
                    for t in (0, 1) if part == 0 else (2, 3):
                        mm = nc.tensor.matmul(ps[:, :], conv_diag[:, k - 4, t, :], xz[:, p, k - 4, t:t + L],
                                              start=(t == 0), stop=(t == KC - 1))
                    if part == 0:
                        return
                else:
                    pe.wait_ge(s_silu, b + 1)
                    for c in range(J):
                        w = w_bc_sb[:, c, :, :] if k == 6 else w_delta_sb[:, c, ts(k - 7, P)]
                        mm = nc.tensor.matmul(ps[0:96, :] if k == 6 else ps[:, :], w, act_x[:, p, c, :],
                                              start=(c == 0), stop=(c == J - 1))
                mm.then_inc(s_unit, 1)

            def ssm_prepare(b, p, n):
                for k, part in {0: ((0, None), (1, None)), 1: ((2, None),), 2: ((3, None),), 3: ((4, 0),), 4: ((4, 1),),
                                5: ((5, 0),), 6: ((5, 1),), 8: ((6, None),), 9: ((7, None),), 10: ((8, None),)}.get(n, ()):
                    ssm_unit(b, p, k, part)

            def ssm_row_b(b, p, n):
                if n == 0:
                    pe.wait_ge(s_bc3, b + 1)
                if not (isinstance(b, int) and b == 0 and n < 2):
                    pe.wait_ge(s_bcp, NS * b + n - 1)
                nc.tensor.matmul(bank_b[n % 2][:, :], pick[:, n, :], bc3[:, p, :], start=True, stop=True).then_inc(s_bb, 1)

            def ssm_row_c(b, p, n):
                if not (isinstance(b, int) and b == 0 and n < 2):
                    pe.wait_ge(s_hc, NS * b + n - 1)
                nc.tensor.matmul(bank_c[n % 2][:, :], pick[:, NS + n, :], bc3[:, p, :], start=True, stop=True).then_inc(s_cb, 1)

            def ssm_accumulate(b, n, q):
                pe.wait_ge(s_hc, NS * b + n + 1)
                if n == 0 and not (isinstance(b, int) and b == 0):
                    pe.wait_ge(s_yd, b)
                for j in range(J):
                    mm = nc.tensor.matmul(bank_y[j][:, :], ident[:, :], hc[:, q, j, :],
                                          start=(n == 0), stop=(n == NS - 1))
                mm.then_inc(s_y, 1)

            def ssm_out(b, p, last):
                pe.wait_ge(s_gt, b + 1)
                if not last:
                    pe.wait_ge(s_unita, 9 * B - 1 if isinstance(b, int) and b == B - 2 else 9 * (b + 2) + 5)
                else:
                    pe.wait_ge(s_res, b)
                for t in range(TB):
                    nc.tensor.matmul(bank_pre[0][:, ts(t, P)], ones_row[:, :], b_out_row[:, :], start=True, stop=False,
                                     skip_group_check=True)
                    for j in range(J):
                        mm = nc.tensor.matmul(bank_pre[0][:, ts(t, P)], gated[:, j, ts(t, P)], w_out_sb[:, j, :],
                                              start=False, stop=(j == J - 1), skip_group_check=True)
                mm.then_inc(s_op, 1)

            def ssm_batch(b, p, first, last):
                if first:
                    for n in range(LEAD):
                        ssm_row_b(b, p, n)
                    ssm_row_c(b, p, 0)
                for n in range(NS):
                    if n + 1 < NS:
                        ssm_row_c(b, p, n + 1)
                    elif not last:
                        ssm_row_c(b + 1, 1 - p, 0)
                    if n + LEAD < NS:
                        ssm_row_b(b, p, n + LEAD)
                    elif not last:
                        ssm_row_b(b + 1, 1 - p, n + LEAD - NS)
                    if n:
                        ssm_accumulate(b, n - 1, (n - 1) % 2)
                    elif not first:
                        ssm_accumulate(b - 1, NS - 1, 1)
                    if not last:
                        ssm_prepare(b + 1, 1 - p, n)
                    if not first and n == 7:
                        ssm_out(b - 1, 1 - p, False)
                if last:
                    ssm_accumulate(b, NS - 1, 1)
                    ssm_out(b, p, True)

            def moe_blocks(m, c):
                base = (2 * m + c) * NB

                def experts(i):
                    word = pe.value_load(expert[0:1, c, ds(i, 1)], min_val=0, max_val=E ** DIGITS - 1)
                    return [(word // E ** r) % E for r in range(DIGITS)]

                def tokens(j, p):
                    pe.wait_ge(s_xl[p], 16 * ((2 * m + c) * OF_PARITY[p] + 1) + (j - p) * 8)
                    if not (isinstance(base + j, int) and base + j < 1):
                        pe.wait_ge(s_xgT, base + j)
                    nc.tensor.transpose(bank[5][:, 0:P], xg[:, p, :], ident[:, :]).then_inc(s_tx, 1)

                def gate_up(w, out, done, e, p):
                    nc.tensor.matmul(out[:, None, :], xgT[:, p, :], w[:, ds(e, 1), :], start=True, stop=True).then_inc(done, 1)

                def hidden(j, p):
                    pe.wait_ge(s_hd, base + j + 1)
                    if not (isinstance(base + j, int) and base + j < 1):
                        pe.wait_ge(s_ht, base + j)
                    for ch in range(HC):
                        mm = nc.tensor.transpose(bank[4][:, ts(ch, P)], hid[:, p, ts(ch, P)], ident[:, :])
                    mm.then_inc(s_th, 1)

                def down(j, p, e):
                    pe.wait_ge(s_ht, base + j + 1)
                    if not (isinstance(base + j, int) and base + j < 2):
                        pe.wait_ge(s_yb, base + j - 1)
                    for ch in range(HC):
                        mm = nc.tensor.matmul(bank[6 + p][:, None, 0:P], hidT[:, p, ch, :], wd_sb[:, ds(e, 1), ch, :],
                                              start=(ch == 0), stop=(ch == HC - 1))
                    mm.then_inc(s_dn, 1)

                def step(j, p, e_before, e):
                    if not (isinstance(j, int) and j == 0):
                        hidden(j - 1, 1 - p)
                    pe.wait_ge(s_xgT, base + j + 1)
                    if not (isinstance(base + j, int) and base + j < 2):
                        pe.wait_ge(s_sg, base + j - 1)
                    gate_up(wg_sb, bank[p], s_g, e, p)
                    if not (isinstance(base + j, int) and base + j < 2):
                        pe.wait_ge(s_hd, base + j - 1)
                    gate_up(wu_sb, bank[2 + p], s_up, e, p)
                    if not (isinstance(j, int) and j == NB - 1):
                        tokens(j + 1, 1 - p)
                    if not (isinstance(j, int) and j == 0):
                        down(j - 1, 1 - p, e_before)

                pe.wait_ge(s_row, 2 * m + c + 1)
                pe.wait_ge(s_wd, 16)
                tokens(0, 0)
                e = experts(0)
                for j in range(3):
                    step(j, j % 2, e[j + 1], e[j + 2])
                with pe.Fori(0, (NB - 7) // 4) as i:
                    e = experts(i + 1)
                    for r in range(4):
                        step(4 * i + 3 + r, (r + 1) % 2, e[r], e[r + 1])
                e = experts(WORDS - 1)
                for r in range(4):
                    step(NB - 4 + r, (r + 1) % 2, e[r], e[r + 1])
                hidden(NB - 1, 0)
                down(NB - 1, 0, e[4])

            def att_project(b, p):
                pe.wait_ge(a_xt, b + 1)
                if isinstance(b, int) and b == 1:
                    pe.wait_ge(a_qf, 1)
                elif not (isinstance(b, int) and b == 0):
                    pe.wait_ge(a_ot, G * (b - 1))
                for c in range(2):
                    mm = nc.tensor.matmul(bank[6 + c][:, :], wqkv_sb[:, ts(c, D)], xt[:, p, :], start=True, stop=True)
                mm.then_inc(a_qk, 1)
                if not (isinstance(b, int) and b == 0):
                    pe.wait_ge(a_mx, NH * b)
                for t in range(TB):
                    nc.tensor.matmul(bank[2][:, ts(t, P)], xt[:, p, ts(t, P)], wqkv_sb[:, 2 * D:], start=True, stop=True,
                                     skip_group_check=True)
                wv = wqkv_sb[:, 2 * D:].rearrange("p (g r d) -> p r g d", g=G, r=R)
                for r in range(R):
                    mm = nc.tensor.matmul(bank[4][32 * r:32 * r + KS_N, 0:G * DH], xt[:, p, 0:L:STRIDE], wv[:, r, :, :],
                                          start=True, stop=True)
                mm.then_inc(a_v, 1)

            def att_scores(b, p, k):
                pe.wait_ge(a_ld[p], 384 * (k + 1))
                if isinstance(b, int) and b == 0:
                    pe.wait_ge(a_va, 1)
                else:
                    pe.wait_ge(a_ef, G * b)
                    pe.wait_ge(a_rd, G * b - 1)
                for z in range(2):
                    for qt in range(TB):
                        for m in range(NH // 2):
                            mm = nc.tensor.matmul(bank[z][:, ds(P * qt + KS_N * m, KS_N)],
                                                  qs[64 * z:64 * z + TR, p, m, ts(qt, P)],
                                                  ks[64 * z:64 * z + TR, p, m, 0:L:STRIDE], start=True, stop=True,
                                                  skip_group_check=True)
                    mm.then_inc(a_ss, 1)
                for qt in range(TB):
                    lo, hi = reach[qt]
                    for g in range(G):
                        u_ = G * qt + g
                        if u_ >= 2:
                            pe.wait_ge(a_mx, NH * b + u_ - 1)
                        elif not (isinstance(b, int) and b == 0):
                            pe.wait_ge(a_e, NH * b)
                        sc = score[u_ % 2]
                        for c in range(2):
                            nc.tensor.matmul(sc[:, 2 * c:2 * c + 2, :], identb[:, :],
                                             band_q[:, None, :].to_broadcast([P, 2, BAND]), start=True, stop=False,
                                             skip_group_check=True)
                        for r in range(R):
                            z, m = r // 2, 2 * g + r % 2
                            k0 = P * qt - WINDOW
                            mm = nc.tensor.matmul(sc[:, r, lo:hi], qs[64 * z:64 * z + TR, p, m, ts(qt, P)],
                                                  ks[64 * z:64 * z + TR, p, m, k0 + lo:k0 + hi], start=False, stop=True,
                                                  skip_group_check=True)
                        mm.then_inc(a_s, 1)

            def att_max(b, p):
                pe.wait_ge(a_mn, b + 1)
                for qt in range(TB):
                    mm = nc.tensor.transpose(bank[0][0:NH, ts(qt, P)], mxn[:, qt, :, :].rearrange("p z m -> p (z m)"), ident[:, :])
                mm.then_inc(a_mt, 1)

            def att_heads(b, p, k, last):
                TM = TR + 3

                def far(g):
                    if g == 0:
                        pe.wait_ge(a_va, b + 1 if last else b + 2)
                    else:
                        pe.wait_ge(a_ef, G * b + g)
                    nc.tensor.matmul(bank[1][:, :], identb[:, :], far_k, start=True, stop=False, skip_group_check=True)
                    for r in range(R):
                        h_ = R * g + r
                        at = 64 * (h_ % 2)
                        mm = nc.tensor.matmul(bank[1][32 * r:32 * r + KS_N, :], ks[at:at + TM, p, h_ // 2, 0:L:STRIDE],
                                              qs[at:at + TM, p, h_ // 2, :], start=False, stop=True, skip_group_check=True)
                    mm.then_inc(a_tf, 1)

                def near(h_):
                    if h_ >= 2:
                        pe.wait_ge(a_e, NH * b + h_ - 1)
                    else:
                        pe.wait_ge(a_mx, NH * (b + 1))
                    sc = score[h_ % 2]
                    for c in range(2):
                        nc.tensor.matmul(sc[:, 2 * c:2 * c + 2, :], identb[:, :],
                                         band_k[:, None, :].to_broadcast([P, 2, BAND]), start=True, stop=False,
                                         skip_group_check=True)
                    at = 64 * (h_ % 2)
                    for kt in range(TB):
                        lo, hi = reach[kt]
                        q0 = P * kt - WINDOW
                        mm = nc.tensor.matmul(sc[:, kt, lo:hi], ks[at:at + TM, p, h_ // 2, ts(kt, P)],
                                              qs[at:at + TM, p, h_ // 2, q0 + lo:q0 + hi], start=False, stop=True,
                                              skip_group_check=True)
                    mm.then_inc(a_t, 1)

                def sums(h_):
                    g, r = h_ // R, h_ % R
                    acc = bank[6 + g % 2]
                    if r == 0:
                        pe.wait_ge(a_ef, G * b + g + 1)
                        if not (isinstance(b, int) and b == 0 and g < 2):
                            pe.wait_ge(a_ot, G * b + g - 1)
                    pe.wait_ge(a_e, NH * b + h_ + 1)
                    for kt in range(TB):
                        lo, hi = reach[kt]
                        q0 = P * kt - WINDOW
                        nc.tensor.matmul(acc[ts(r, 32), q0 + lo:q0 + hi], va[:, p, kt, h_, :],
                                         pt[:, h_ % 2, BAND * kt + lo:BAND * kt + hi], start=(kt == 0), stop=False,
                                         skip_group_check=True)
                    nc.tensor.matmul(acc[ts(r, 32), :], vs_[ts(r, 32), p, g, :], pts[ts(r, 32), g % 2, :],
                                     start=False, stop=True, skip_group_check=True).then_inc(a_pv, 1)

                pe.wait_ge(a_ml[p], 96 * (k + 1))
                for h_ in range(NH):
                    if h_ % R == 0:
                        far(h_ // R)
                    near(h_)
                    if h_:
                        sums(h_ - 1)
                    if h_ >= R + 2 and (h_ - R - 2) % R == 0:
                        att_spread(b, (h_ - R - 2) // R, last)
                sums(NH - 1)

            def att_spread(b, g, last):
                pe.wait_ge(a_ot, G * b + g + 1)
                if g == 0 and isinstance(b, int) and b == 0:
                    pe.wait_ge(a_ma, 1)
                elif g == 0:
                    pe.wait_ge(a_res, b)
                elif g == G - 1 and not last:
                    pe.wait_ge(a_ma, 3 * (b + 1) + 1)
                else:
                    pe.wait_ge(a_rd, G * b + g)
                nc.tensor.matmul(bank[0][:, :], den_pick, ots[:, g % 2, :], start=True, stop=True).then_inc(a_dn, 1)

            def att_out(b):
                pe.wait_ge(a_on, G * (b + 1))
                for t in range(TB):
                    nc.tensor.matmul(bank[0][:, ts(t, P)], ones_row[:, :], bo_row[:, :], start=True, stop=False,
                                     skip_group_check=True)
                    for g in range(G):
                        mm = nc.tensor.matmul(bank[0][:, ts(t, P)], otn[:, g, ts(t, P)], wo_sb[:, g, :], start=False,
                                              stop=(g == G - 1), skip_group_check=True)
                mm.then_inc(a_op, 1)

            def att_step(b, p, k, project=True):
                att_heads(b, p, k, False)
                att_scores(b + 1, 1 - p, k + p)
                att_max(b + 1, 1 - p)
                att_spread(b, G - 1, False)
                if project:
                    att_project(b + 2, p)
                att_out(b)

            for k, stage in enumerate(stages):
                layer_norm(k)
                if stage == "ssm":
                    pe.wait_ge(s_xnT, B * (k + 1))
                    pe.wait_ge(s_w, 16 * 18)
                    pe.wait_ge(s_diag, J * KC)
                    pe.wait_ge(s_cst, 6)
                    for n in range(NS):
                        ssm_prepare(0, 0, n)
                    ssm_batch(0, 0, True, False)
                    with pe.Fori(0, (B - 2) // 2) as i:
                        ssm_batch(2 * i + 1, 1, False, False)
                        ssm_batch(2 * i + 2, 0, False, False)
                    ssm_batch(B - 1, 1, False, True)
                elif stage == "moe":
                    for c in range(2):
                        moe_blocks(stages[:k].count("moe"), c)
                else:
                    pe.wait_ge(a_w, 16 * 9)
                    pe.wait_ge(a_wo, 16 * R)
                    pe.wait_ge(a_cst, 10)
                    pe.wait_ge(s_cst, 7)
                    att_project(0, 0)
                    att_scores(0, 0, 0)
                    att_max(0, 0)
                    att_project(1, 1)
                    att_step(0, 0, 0)
                    with pe.Fori(0, (B - 4) // 2) as i:
                        att_step(2 * i + 1, 1, i)
                        att_step(2 * i + 2, 0, i + 1)
                    att_step(B - 3, 1, B // 2 - 2)
                    att_step(B - 2, 0, B // 2 - 1, False)
                    att_heads(B - 1, 1, B // 2 - 1, True)
                    att_spread(B - 1, G - 1, True)
                    att_out(B - 1)

        @block.vector
        def _(dve):
            vec = nc.vector

            def layer_norm(k, c):
                moe = stages[k] == "moe"
                if k and stages[k - 1] == "ssm":
                    dve.wait_ge(s_res, B)
                elif k and stages[k - 1] == "moe":
                    dve.wait_ge(s_ad, T * stages[:k].count("moe") - (TH if c == 0 else 0))
                elif k:
                    dve.wait_ge(a_res, B)
                for t in range(TH * c, TH * (c + 1)):
                    if k == 0 and t % (T // 4) == 0:
                        dve.wait_ge(s_x[4 * t // T], 16)
                    vec.bn_stats(stats[:, t, :], X[:, t, :]).then_inc(s_lnst, 1)
                dve.wait_ge(s_lnst, T * k + TH * (c + 1))
                for t in range(TH * c, TH * (c + 1)):
                    vs = vec.bn_aggr(mv[:, t, :], stats[:, t, :])
                vs.then_inc(s_var, 1)
                dve.wait_ge(s_std, 2 * k + c + 1)
                vec.reciprocal(rstd[:, ts(c, TH)], std[:, ts(c, TH)]).then_inc(s_rstd, 1)
                dve.wait_ge(s_rstd, 2 * k + c + 1)
                for b in range(c * B // 2, (c + 1) * B // 2):
                    if B * k + b >= 2:
                        dve.wait_ge(s_xt, B * k + b - 1)
                    for t in range(TB):
                        g = b * TB + t
                        dst = xna[:, g, :] if moe else xn[:, b % 2, t, :]
                        vs = vec.tensor_scalar(dst, X[:, g, :], mv[:, g, 0:1], rstd[:, g:g + 1],
                                               ALU.subtract, ALU.mult)
                    vs.then_inc(s_xn, 1)
                if moe:
                    moe_route(stages[:k].count("moe"), c)

            def ssm_dt(b, p):
                dve.wait_ge(s_soft, 3 * b + 3)
                if not (isinstance(b, int) and b < 2):
                    dve.wait_ge(s_da, 2 * NS * (b - 1))
                vec.scalar_tensor_tensor(out=dt[:, p, :, :], in0=pre_dt[:, :, :], scalar=0.0, in1=soft[:, :, :],
                                         op0=ALU.max, op1=ALU.add).then_inc(s_dt, 1)

            def ssm_parts(b, p):
                dve.wait_ge(s_bcs, 3 * b + 3)
                vec.tensor_copy(bc3[32:64, p, :], bc_p2[32:64, :])
                vec.tensor_copy(bc3[64:96, p, :], bc_r2[64:96, :]).then_inc(s_bc3, 1)

            def ssm_hc(b, n, q):
                dve.wait_ge(s_cb, NS * b + n + 1)
                dve.wait_ge(s_h, 2 * (NS * b + n + 1))
                if not (isinstance(b, int) and b == 0 and n < 2):
                    dve.wait_ge(s_y, NS * b + n - 1)
                vec.tensor_tensor(hc[:, q, :, :], h[:, q, :, :], bank_c[n % 2][:, None, :].to_broadcast([P, J, L]),
                                  ALU.mult).then_inc(s_hc, 1)

            def ssm_finish(b, p):
                dve.wait_ge(s_y, NS * (b + 1))
                for j in range(J):
                    vs = vec.scalar_tensor_tensor(out=gated[:, j, :], in0=act_x[:, p, j, :], scalar=d_skip_sb[:, j:j + 1],
                                                  in1=bank_y[j][:, :], op0=ALU.mult, op1=ALU.add)
                vs.then_inc(s_yd, 1)
                dve.wait_ge(s_yd, b + 1)
                vec.tensor_tensor(gated[:, :, :], gated[:, :, :], gate[:, p, :, :], ALU.mult).then_inc(s_gt, 1)

            def ssm_residual(b):
                dve.wait_ge(s_op, b + 1)
                xs = X[:, ts(b, TB), :]
                vec.tensor_tensor(xs, xs, bank_pre[0][:, :].rearrange("p (t d) -> p t d", t=TB), ALU.add).then_inc(s_res, 1)

            def ssm_batch(b, p, first, last):
                for n in range(NS):
                    for j in range(J):
                        dve.wait_ge(s_da, 2 * (NS * b + n) + j + 1)
                        if j == 0:
                            dve.wait_ge(s_dbu, NS * b + n + 1)
                            if not (first and n < 2):
                                dve.wait_ge(s_hc, NS * b + n - 1)
                        vec.tensor_tensor_scan(h[:, n % 2, j, :], decay[n % DECAYS][j], dbu[:, n % 2, j, :], 0.0,
                                               ALU.mult, ALU.add).then_inc(s_h, 1)
                    if n:
                        ssm_hc(b, n - 1, (n - 1) % 2)
                    elif not first:
                        ssm_hc(b - 1, NS - 1, 1)
                    if not first and n == 1:
                        ssm_finish(b - 1, 1 - p)
                    if not first and n == 8:
                        ssm_residual(b - 1)
                    if not last and n == 13:
                        ssm_dt(b + 1, 1 - p)
                    if not last and n == 11:
                        ssm_parts(b + 1, 1 - p)
                if last:
                    ssm_hc(b, NS - 1, 1)
                    ssm_finish(b, p)
                    ssm_residual(b)

            def moe_route(m, c):
                q = 2 * m + c
                n = [ROUTE_STEPS * q]

                def then(ins):
                    n[0] += 1
                    ins.then_inc(s_rt, 1)
                    dve.wait_ge(s_rt, n[0])

                big = lambda a: a[:, :, None].to_broadcast([P, TH, E])
                fallb = fall[:, None, :].to_broadcast([P, TH, E])
                tile_first = lambda a: a.rearrange("p e t -> p t e")
                expert_first = lambda a: a.rearrange("p (t e) -> p e t", e=E)
                dve.wait_ge(s_mc, 16 * (m + 1))
                dve.wait_ge(s_lg, q + 1)
                then(vec.tensor_tensor(logits[:, :, :], bank[7][:, 0:TH * E].rearrange("p (t e) -> p t e", e=E),
                                       rb_sb[:, None, :].to_broadcast([P, TH, E]), ALU.add))
                then(vec.tensor_reduce(top[:, 0, :], logits[:, :, :], AX.X, ALU.max))
                then(vec.tensor_tensor(one1[:, :, :], logits[:, :, :], big(top[:, 0, :]), ALU.is_equal))
                then(vec.tensor_tensor(lrank[:, :, :], one1[:, :, :], fallb, ALU.mult))
                then(vec.tensor_reduce(top[:, 4, :], lrank[:, :, :], AX.X, ALU.max))
                then(vec.tensor_tensor(one1[:, :, :], fallb, big(top[:, 4, :]), ALU.is_equal))
                then(vec.scalar_tensor_tensor(out=rest[:, :, :], in0=one1[:, :, :], scalar=-3.0e38, in1=logits[:, :, :],
                                              op0=ALU.mult, op1=ALU.add))
                then(vec.tensor_reduce(top[:, 1, :], rest[:, :, :], AX.X, ALU.max))
                vec.tensor_tensor(top[:, 2, :], top[:, 1, :], top[:, 0, :], ALU.subtract).then_inc(s_df, 1)
                then(vec.tensor_tensor(one2[:, :, :], rest[:, :, :], big(top[:, 1, :]), ALU.is_equal))
                then(vec.tensor_tensor(lrank[:, :, :], one2[:, :, :], fallb, ALU.mult))
                then(vec.tensor_reduce(top[:, 5, :], lrank[:, :, :], AX.X, ALU.max))
                then(vec.tensor_tensor(one2[:, :, :], fallb, big(top[:, 5, :]), ALU.is_equal))
                vec.tensor_tensor(both[:, :, :], one1[:, :, :], one2[:, :, :], ALU.add).then_inc(s_both, 1)
                dve.wait_ge(s_re, q + 1)
                then(vec.tensor_scalar(top[:, 4, :], top[:, 3, :], 1.0, None, ALU.add))
                then(vec.reciprocal(pick_w[:, c, 0, :], top[:, 4, :]))
                vec.tensor_tensor(pick_w[:, c, 1, :], top[:, 3, :], pick_w[:, c, 0, :], ALU.mult)
                dve.wait_ge(s_pr, q + 1)
                then(vec.tensor_copy(tot[:, :, :], expert_first(bank[6][:, 0:TH * E])))
                then(vec.tensor_tensor_scan(upto[:, :, :].rearrange("p e t -> p (e t)"), keep,
                                            tot[:, :, :].rearrange("p e t -> p (e t)"), 0.0, ALU.mult, ALU.add))
                then(vec.tensor_tensor(over[:, :, :], upto[:, :, TH - 1:TH].to_broadcast([P, E, TH]),
                                       thresholds[:, None, :].to_broadcast([P, E, TH]), ALU.is_gt))
                then(vec.tensor_reduce(n_blocks[:, :], over[:, :, :], AX.X, ALU.add))
                then(vec.tensor_tensor_scan(ends[:, :], ones_e, n_blocks[:, :], 0.0, ALU.mult, ALU.add))
                then(vec.tensor_tensor(starts[:, :], ends[:, :], n_blocks[:, :], ALU.subtract))
                then(vec.tensor_tensor(upto[:, :, :], upto[:, :, :], tot[:, :, :], ALU.subtract))
                then(vec.scalar_tensor_tensor(out=place[:, :, :], in0=starts[:, :, None].to_broadcast([P, E, TH]),
                                              scalar=float(P), in1=upto[:, :, :], op0=ALU.mult, op1=ALU.add))
                then(vec.tensor_tensor(place[:, :, :], place[:, :, :], expert_first(bank[6][:, TH * E:2 * TH * E]), ALU.add))
                for k, one in enumerate((one1, one2)):
                    then(vec.tensor_tensor(placed[:, k, :, :], one[:, :, :], tile_first(place[:, :, :]), ALU.mult))
                then(vec.tensor_reduce(row_f[:, :, :], placed[:, :, :, :], AX.X, ALU.add))
                vec.tensor_copy(row[:, c, :, :], row_f[:, :, :])
                then(vec.tensor_tensor(ended[:, :, :], ends[0:1, None, :].to_broadcast([1, NB, E]),
                                       counting[0:1, :, None].to_broadcast([1, NB, E]), ALU.is_le))
                vec.memset(expert_f[:, 0:2], 0.0)
                then(vec.tensor_reduce(expert_f[:, 2:], ended[:, :, :], AX.X, ALU.add))
                then(vec.tensor_scalar(expert_f[:, :], expert_f[:, :], float(E - 1), None, ALU.min))
                digit = lambda r: expert_f[:, r:r + (WORDS - 1) * (DIGITS - 1) + 1:DIGITS - 1]
                then(vec.tensor_copy(word[:, :], digit(DIGITS - 1)))
                for r in range(DIGITS - 2, -1, -1):
                    then(vec.scalar_tensor_tensor(out=word[:, :], in0=word[:, :], scalar=float(E), in1=digit(r),
                                                  op0=ALU.mult, op1=ALU.add))
                vec.tensor_copy(expert[:, c, :], word[:, :]).then_inc(s_row, 1)
                assert n[0] == ROUTE_STEPS * (q + 1), n[0]

            def moe_add(m, c, t, r):
                n = (2 * m + c) * TH // 2 + r
                for k in range(2):
                    if k:
                        dve.wait_ge(s_a1, n + 1)
                    for g in range(2):
                        xs = X[:, ds(TH * c + t + g, 1), :]
                        vs = vec.scalar_tensor_tensor(out=xs, in0=yg[:, c, k, ds(t + g, 1), :],
                                                      scalar=pick_w[:, c, k, ds(t + g, 1)], in1=xs,
                                                      op0=ALU.mult, op1=ALU.add)
                    vs.then_inc(s_ad if k else s_a1, 2 if k else 1)

            def moe_blocks(m, c):
                q = 2 * m + c
                base = q * NB

                def hidden(j, p):
                    dve.wait_ge(s_up, base + j + 1)
                    dve.wait_ge(s_sg, base + j + 1)
                    if not (isinstance(base + j, int) and base + j < 2):
                        dve.wait_ge(s_th, base + j - 1)
                    vec.tensor_tensor(hid[:, p, :], sg[:, p, :], bank[2 + p][:, :], ALU.mult).then_inc(s_hd, 1)

                def result(j, p):
                    dve.wait_ge(s_dn, base + j + 1)
                    if not (q == 0 and isinstance(j, int) and j < 2):
                        dve.wait_ge(s_ys[p], 16 * q * OF_PARITY[p] + (j - p) * 8)
                    vec.tensor_copy(y_sb[:, p, :], bank[6 + p][:, 0:P]).then_inc(s_yb, 1)

                def step(j, p):
                    hidden(j, p)
                    if not (isinstance(j, int) and j == 0):
                        result(j - 1, 1 - p)

                for j in range(4):
                    step(j, j % 2)
                pairs, adds = (NB - 5) // 2, TH // 2 if c else 0
                with dve.Fori(0, pairs - adds) as i:
                    for p in range(2):
                        step(2 * i + 4 + p, p)
                if adds:
                    for g in range(TB):
                        dve.wait_ge(s_yg[g], 16 * 2 * TB * q)
                    with dve.Fori(0, adds) as i:
                        for p in range(2):
                            step(2 * (i + pairs - adds) + 4 + p, p)
                        moe_add(m, 0, 2 * i, i)
                step(NB - 1, 0)
                result(NB - 1, 0)

            def moe_finish(m):
                for r in range(TH // 2):
                    if r % 2 == 0:
                        dve.wait_ge(s_yg[r // 2], 16 * 2 * TB * (2 * m + 2))
                    moe_add(m, 1, 2 * r, r)

            def att_inputs(b, p):
                dve.wait_ge(a_qk, b + 1)
                if not (isinstance(b, int) and b == 0):
                    dve.wait_ge(a_sp, 2 * b)
                vec.tensor_scalar(qk_f[:, 0, :], bank[6][:, :], bqk_sb[:, 0:1], DH ** -0.5, ALU.add, ALU.mult)
                vec.tensor_scalar(qk_f[:, 1, :], bank[7][:, :], bqk_sb[:, 1:2], None, ALU.add).then_inc(a_qf, 1)
                dve.wait_ge(a_v, b + 1)
                if not (isinstance(b, int) and b < 2):
                    dve.wait_ge(a_pv, NH * (b - 1))
                vec.tensor_tensor(va[:, p, :, :, 0:DH], bank[2][:, :].rearrange("p (t h d) -> p t h d", t=TB, h=NH),
                                  bv_all[:, None, :, :].to_broadcast([P, TB, NH, DH]), ALU.add)
                for r in range(R):
                    rows = slice(32 * r, 32 * r + KS_N)
                    vi = vec.tensor_tensor(vs_[rows, p, :, 0:DH], bank[4][rows, 0:G * DH].rearrange("p (g d) -> p g d", g=G),
                                           bv_str[rows, :, :], ALU.add)
                vi.then_inc(a_va, 1)

            def att_maxima(b):
                if not (isinstance(b, int) and b == 0):
                    dve.wait_ge(a_mn, b)
                for z in range(2):
                    dve.wait_ge(a_ss, 2 * b + z + 1)
                    vec.tensor_reduce(mxs[:, :, z, :], bank[z][:, :].rearrange("p (q m k) -> p q m k", q=TB, k=KS_N),
                                      AX.X, ALU.max).then_inc(a_ms, 1)
                for qt in range(TB):
                    lo, hi = reach[qt]
                    for g in range(G):
                        dve.wait_ge(a_s, NH * b + G * qt + g + 1)
                        vec.tensor_reduce(mxw[:, qt, :, 2 * g:2 * g + 2],
                                          score[(G * qt + g) % 2][:, :, lo:hi].rearrange("p (z m) k -> p z m k", z=2),
                                          AX.X, ALU.max).then_inc(a_mx, 1)
                dve.wait_ge(a_mx, NH * (b + 1))
                dve.wait_ge(a_ms, 2 * (b + 1))
                if not (isinstance(b, int) and b == 0):
                    dve.wait_ge(a_mt, b)
                vec.tensor_tensor(mxs[:, :, :, :], mxw[:, :, :, :], mxs[:, :, :, :], ALU.max).then_inc(a_mm, 1)
                dve.wait_ge(a_mm, b + 1)
                vec.tensor_scalar(mxn[:, :, :, :], mxs[:, :, :, :], -1.0, None, ALU.mult).then_inc(a_mn, 1)

            def att_normalise(b, g):
                dve.wait_ge(a_dn, G * b + g + 1)
                if not (isinstance(b, int) and b == 0 and g == 0):
                    dve.wait_ge(a_on, G * b + g)
                vec.reciprocal(rden[:, :], bank[0][:, :]).then_inc(a_rd, 1)
                dve.wait_ge(a_rd, G * b + g + 1)
                vec.tensor_tensor(otn[:, g, :], ots[:, g % 2, :], rden[:, :], ALU.mult).then_inc(a_on, 1)

            def att_residual(b):
                dve.wait_ge(a_op, b + 1)
                xs = X[:, ts(b, TB), :]
                vec.tensor_tensor(xs, xs, bank[0][:, :].rearrange("p (t d) -> p t d", t=TB), ALU.add).then_inc(a_res, 1)

            def att_step(b, p, inputs=True):
                for g in range(G - 1):
                    att_normalise(b, g)
                att_maxima(b + 1)
                att_normalise(b, G - 1)
                if inputs:
                    att_inputs(b + 2, p)
                att_residual(b)

            layer_norm(0, 0)
            for k, stage in enumerate(stages):
                layer_norm(k, 1)
                if stage == "ssm":
                    dve.wait_ge(s_w, 16 * 18)
                    dve.wait_ge(s_cst, 3)
                    for j in range(J):
                        for t in range(KC):
                            vec.tensor_scalar(conv_diag[:, j, t, :], ident[:, :], conv_w_sb[:, j, t:t + 1], None,
                                              ALU.mult).then_inc(s_diag, 1)
                    ssm_dt(0, 0)
                    ssm_parts(0, 0)
                    ssm_batch(0, 0, True, False)
                    with dve.Fori(0, (B - 2) // 2) as i:
                        ssm_batch(2 * i + 1, 1, False, False)
                        ssm_batch(2 * i + 2, 0, False, False)
                    ssm_batch(B - 1, 1, False, True)
                    if k + 1 < len(stages):
                        layer_norm(k + 1, 0)
                elif stage == "moe":
                    for c in range(2):
                        moe_blocks(stages[:k].count("moe"), c)
                    if k + 1 < len(stages):
                        layer_norm(k + 1, 0)
                    moe_finish(stages[:k].count("moe"))
                else:
                    dve.wait_ge(a_w, 16 * 9)
                    dve.wait_ge(a_cst, 10)
                    att_inputs(0, 0)
                    att_maxima(0)
                    att_inputs(1, 1)
                    att_step(0, 0)
                    with dve.Fori(0, (B - 4) // 2) as i:
                        att_step(2 * i + 1, 1)
                        att_step(2 * i + 2, 0)
                    att_step(B - 3, 1)
                    att_step(B - 2, 0, False)
                    for g in range(G):
                        att_normalise(B - 1, g)
                    att_residual(B - 1)
                    if k + 1 < len(stages):
                        layer_norm(k + 1, 0)


_INS = ["L0_attn_a_x", "L0_attn_a_W_in", "L0_attn_a_b_in", "L0_attn_a_W_gate", "L0_attn_a_b_gate",
        "L0_attn_a_conv_w", "L0_attn_a_conv_b", "L0_attn_a_A_log", "L0_attn_a_D_skip", "L0_attn_a_W_delta",
        "L0_attn_a_b_delta", "L0_attn_a_W_B", "L0_attn_a_W_C", "L0_attn_a_W_out", "L0_attn_a_b_out",
        "L0_attn_b_w_qkv", "L0_attn_b_b_qkv", "L0_attn_b_w_out", "L0_attn_b_b_out", "L0_ffn_wg", "L0_ffn_bg",
        "L0_ffn_Wgate", "L0_ffn_Wup", "L0_ffn_Wdown"]


def kernel(**inputs):
    import numpy as _np
    import concourse.bacc as _bacc
    from concourse import mybir as _mybir
    from concourse.bass_utils import run_bass_kernel_spmd as _run

    nc = _bacc.Bacc("TRN2", target_bir_lowering=False, num_devices=1)
    arrays, args = {}, []
    for name in _INS:
        a = _np.asarray(inputs[name])
        if name in ("L0_ffn_Wgate", "L0_ffn_Wup"):
            a = a.transpose(2, 0, 1)
        elif name == "L0_ffn_Wdown":
            a = a.reshape(a.shape[0], a.shape[1], -1, 128).transpose(3, 0, 2, 1)
        a = _np.ascontiguousarray(a)
        arrays[f"in_{name}_dram"] = a
        args.append(nc.dram_tensor(f"in_{name}_dram", a.shape, _mybir.dt.from_np(a.dtype), kind="ExternalInput").ap())
    p, c, q = _np.arange(128)[:, None], _np.arange(256)[None, :], _np.arange(512)[None, :]
    near = (c - p >= 0) & (c - p <= 128)
    tile = (p % 32) // 4
    covered = (q >= 128 * tile - 64) & (q < 128 * tile + 192) & (p % 32 < 16)
    neg = lambda seen: _np.where(seen, 0.0, -1.0e30)
    spread = (p == 32 * (_np.arange(128)[None, :] // 32) + 8) * 1.0
    consts = _np.concatenate([neg(near | (c % 32 == 0)), neg(near | (p % 32 == 0)), neg(~covered), spread], axis=1)
    arrays["att_consts"] = _np.ascontiguousarray(consts.astype(_np.float32))
    args.append(nc.dram_tensor("att_consts", consts.shape, _mybir.dt.float32, kind="ExternalInput").ap())
    full = lambda a: _np.broadcast_to(_np.asarray(a, _np.float32)[None, :], (128, len(a)))
    routing = _np.concatenate([(p < _np.arange(128)[None, :]) * 1.0, _np.ones((128, 128)),
                               full((_np.arange(8 * 16) % 16 > 0) * 1.0), full(128 * _np.arange(16)),
                               full(_np.arange(39)), full(8 - _np.arange(8)), full(_np.ones(8))], axis=1)
    arrays["moe_consts"] = _np.ascontiguousarray(routing.astype(_np.float32))
    args.append(nc.dram_tensor("moe_consts", routing.shape, _mybir.dt.float32, kind="ExternalInput").ap())
    shape = inputs["L0_attn_a_x"].shape
    args.append(nc.dram_tensor("out_0_dram", shape, _mybir.dt.float32, kind="ExternalOutput").ap())
    hybrid_layer_kernel(nc, *args)
    r = _run(nc, [arrays], core_ids=[0])
    return r.results[0]["out_0_dram"]
```

```python
import concourse.bass as bass
from concourse import mybir
from contextlib import ExitStack


def hybrid_layer_kernel(nc, x, w_in, b_in, w_gate, b_gate, conv_w, conv_b, a_log, d_skip, w_delta,
                        b_delta, w_b, w_c, ssm_w_out, ssm_b_out, w_qkv, b_qkv, att_w_out, att_b_out,
                        router_w, router_b, ffn_gate, ffn_up, ffn_down, att_consts, moe_consts, out, stages=None):
    fp32 = mybir.dt.float32
    bf16 = mybir.dt.bfloat16
    ALU = mybir.AluOpType
    ACT = mybir.ActivationFunctionType
    AX = mybir.AxisListType
    if stages is None:
        stages = ("ssm", "moe", "att", "moe")

    def early(k):
        return 0 < k < len(stages) and stages[k] == "moe"

    B, L, D = x.shape
    P = 128
    T = B * L // P
    TB = L // P
    DI = w_in.shape[1]
    J = DI // P
    NS = w_b.shape[1]
    KC = conv_w.shape[2]
    PAD = KC - 1
    E = router_w.shape[0]
    HID = ffn_gate.shape[2]
    HC = HID // P
    EPS = 1e-5

    TH = T // 2
    NB = (2 * P * TH + E * (P - 1)) // P
    STEPS_AHEAD, TILES_AHEAD = range(10, 16), 1
    ROUTE_STEPS = 34
    DIGITS = 5
    WORDS = (NB - 3) // (DIGITS - 1) + 1
    BESIDE, ABOVE = 12008, 512
    OF_PARITY = ((NB + 1) // 2, NB // 2)
    ROWS_B = 4
    LEAD = 4
    DECAYS = 4

    NH = 16
    DH = D // NH
    G = 4
    R = NH // G
    STRIDE, WINDOW = 32, 64
    KS_N = L // STRIDE
    BAND = P + 2 * WINDOW
    reach = [(WINDOW if t == 0 else 0, BAND - (WINDOW if t == TB - 1 else 0)) for t in range(TB)]
    TERMS_Q = (0, 0, 0, 1, 1, 2)
    TERMS_K = (0, 1, 2, 0, 1, 0)
    TR = len(TERMS_Q) * DH

    ctx = ExitStack()
    with ctx:
        def sb(name, shape, dt=fp32):
            return ctx.enter_context(nc.sbuf_tensor(name, shape, dt))

        def sem(name):
            return ctx.enter_context(nc.semaphore(name))

        ts, ds = bass.ts, bass.ds
        bank = [ctx.enter_context(nc.psum_tensor(f"bank{i}", [P, 512], fp32)) for i in range(2)]
        score = [ctx.enter_context(nc.psum_tensor(f"score{i}", [P, 4, BAND], fp32)) for i in range(2)]
        bank += [score[i // 2][:, 2 * (i % 2):2 * (i % 2) + 2, :].rearrange("p a b -> p (a b)") for i in range(4)]
        bank += [ctx.enter_context(nc.psum_tensor(f"bank{i}", [P, 512], fp32)) for i in range(6, 8)]

        X = sb("X", [P, T, D])
        xnT = sb("xnT", [P, T * P])
        ident = sb("ident", [P, P])
        ones_row = sb("ones_row", [1, P])
        stats = sb("stats", [P, T, 6])
        mv = sb("mv", [P, T, 2])
        std = sb("std", [P, T])
        rstd = sb("rstd", [P, T])
        eps_col = sb("eps_col", [P, 1])
        zeros = sb("zeros", [P, D])
        xn = sb("xn", [P, 2, TB, D])

        identb = sb("identb", [P, P], bf16)
        rw_sb = sb("rw_sb", [P, E])
        rb_sb = sb("rb_sb", [P, E])
        wg_sb = sb("wg_sb", [P, E, HID])
        wu_sb = sb("wu_sb", [P, E, HID])
        wd_sb = sb("wd_sb", [P, E, HC, D])

        scr = ExitStack()

        def tmp(name, shape, dt=fp32):
            return scr.enter_context(nc.sbuf_tensor(name, shape, dt))

        w_in_sb = tmp("w_in_sb", [P, DI])
        w_gate_sb = tmp("w_gate_sb", [P, DI])
        w_delta_sb = tmp("w_delta_sb", [P, J, DI])
        w_bc_sb = tmp("w_bc_sb", [P, J, 3, 2 * NS])
        w_out_sb = tmp("w_out_sb", [P, J, D])
        b_out_row = tmp("b_out_row", [1, D])
        b_in_sb = tmp("b_in_sb", [P, J])
        b_gate_sb = tmp("b_gate_sb", [P, J])
        conv_w_sb = tmp("conv_w_sb", [P, J, KC])
        conv_b_sb = tmp("conv_b_sb", [P, J])
        b_delta_sb = tmp("b_delta_sb", [P, J])
        d_skip_sb = tmp("d_skip_sb", [P, J])
        a_log_sb = tmp("a_log_sb", [P, J, NS])
        a_exp = tmp("a_exp", [P, J, NS])
        a_neg = tmp("a_neg", [P, J, NS])
        conv_diag = tmp("conv_diag", [P, J, KC, P])
        pick = tmp("pick", [3 * 2 * NS, 2 * NS, P], bf16)
        gact = tmp("gact", [P, 2, 2 * J, L])
        act_x = gact[:, :, J:, :]
        gate = gact[:, :, 0:J, :]
        dt = tmp("dt", [P, 2, J, L])
        u = tmp("u", [P, 2, J, L])
        bc_f = tmp("bc_f", [3 * 2 * NS, L])
        bc_r = tmp("bc_r", [3 * 2 * NS, L])
        bc_p2 = tmp("bc_p2", [3 * 2 * NS, L], bf16)
        bc_r2 = tmp("bc_r2", [3 * 2 * NS, L])
        bc3 = tmp("bc3", [3 * 2 * NS, 2, L], bf16)
        b_sb = tmp("b_sb", [P, ROWS_B, L])
        dbu = tmp("dbu", [P, 2, J, L])
        h = tmp("h", [P, 2, J, L])
        hc = tmp("hc", [P, 2, J, L])
        gated = tmp("gated", [P, J, L])
        xz = tmp("xz", [P, 2, J, PAD + L])
        lin = tmp("lin", [P, 2 * J, L])
        pre_dt = tmp("pre_dt", [P, J, L])
        soft = tmp("soft", [P, J, L])

        bank_b, bank_c = [bank[0], bank[1]], [bank[2], bank[3]]
        decay = [[wd_sb[:, J * q + j, :, :].rearrange("p c d -> p (c d)") for j in range(J)] for q in range(DECAYS)]
        bank_y = [bank[4], bank[5]]
        bank_pre = [bank[6], bank[7]]
        scr.close()

        scr = ExitStack()
        xna_late = tmp("xna_late", [P, TH, D])
        xg = tmp("xg", [P, 2, D])
        xgT = tmp("xgT", [P, 2, P])
        sg = tmp("sg", [P, 2, HID])
        hid = tmp("hid", [P, 2, HID])
        hidT = tmp("hidT", [P, 2, HC, P])
        y_sb = tmp("y_sb", [P, 2, D])
        yg = [tmp("yg0", [P, 2, TH, D])]
        beside = tmp("beside", [P, BESIDE])
        yg.append(tmp("yg1", [P, 2, TH, D]))
        above = tmp("above", [P, ABOVE])
        pick_w = tmp("pick_w", [P, 2, 2, TH])
        row = tmp("row", [P, 2, 2, TH], mybir.dt.uint32)
        xna = [tmp("xna_early", [P, TH, D]), xna_late]
        ones3 = tmp("ones3", [P, 3, TH, E])
        one1, one2, lrank = (ones3[:, i, :, :] for i in range(3))
        over = lrank.rearrange("p t e -> p (t e)").rearrange("p (e t) -> p e t", e=E)
        ended = ones3[0:1, :, :, :].rearrange("p a t e -> p (a t e)")[:, 0:NB * E].rearrange("p (n e) -> p n e", e=E)
        placed = tmp("placed", [P, 2, TH, E])
        logits, both = placed[:, 0, :, :], placed[:, 1, :, :]
        rest = tmp("rest", [P, TH, E])
        place = rest[:, :, :].rearrange("p t e -> p (t e)").rearrange("p (e t) -> p e t", e=E)
        top = tmp("top", [P, 6, TH])
        counts = tmp("counts", [P, 2, TH * E])
        tot = tmp("tot", [P, E, TH])
        upto = tmp("upto", [P, E, TH])
        n_blocks = tmp("n_blocks", [P, E])
        ends = tmp("ends", [P, E])
        starts = tmp("starts", [P, E])
        row_f = tmp("row_f", [P, 2, TH])
        expert_f = tmp("expert_f", [1, 2 + NB])
        word = tmp("word", [1, WORDS])
        expert = tmp("expert", [1, 2, WORDS], mybir.dt.int32)
        mc = tmp("mc", [P, 2 * P + E * TH + TH + NB + E + E])
        mc_parts, at = [], 0
        for n in (P, P, E * TH, TH, NB, E, E):
            mc_parts.append(mc[:, at:at + n])
            at += n
        before, ones_sq, keep, thresholds, counting, fall, ones_e = mc_parts
        scr.close()

        scr = ExitStack()
        xt = tmp("xt", [P, 2, L])
        wqkv_sb = tmp("wqkv_sb", [P, 3 * D])
        wo_sb = tmp("wo_sb", [P, G, D])
        bo_row = tmp("bo_row", [1, D])
        bqk_sb = tmp("bqk_sb", [P, 2])
        bv_all = tmp("bv_all", [P, NH, DH])
        bv_str = tmp("bv_str", [P, G, DH])
        den_pick = tmp("den_pick", [P, P])
        consts_b = tmp("consts_b", [P, 2 * BAND + L], bf16)
        qk_f = tmp("qk_f", [P, 2, L])
        qk_r = tmp("qk_r", [P, 2, L])
        qk_p = tmp("qk_p", [P, 2, 3, L], bf16)
        qs = tmp("qs", [P, 2, NH // 2, L], bf16)
        ks = tmp("ks", [P, 2, NH // 2, L], bf16)
        va = tmp("va", [P, 2, TB, NH, 32])
        vs_ = tmp("vs_", [P, 2, G, 32])
        mxw = tmp("mxw", [P, TB, 2, NH // 2])
        mxs = tmp("mxs", [P, TB, 2, NH // 2])
        mxn = tmp("mxn", [P, TB, 2, NH // 2])
        m_f, m_r = qk_r[0:NH, 0, :], qk_r[0:NH, 1, :]
        m_p = tmp("m_p", [NH, 3, L], bf16)
        pt = tmp("pt", [P, 2, TB * BAND])
        pts = tmp("pts", [P, 2, L])
        ots = tmp("ots", [P, 2, L])
        otn = tmp("otn", [P, G, L])
        rden = tmp("rden", [P, L])
        scr.close()
        band_q = consts_b[:, 0:BAND]
        band_k = consts_b[:, BAND:2 * BAND]
        far_k = consts_b[:, 2 * BAND:]
        consts_f = pt[:, :, :].rearrange("p a b -> p (a b)")[:, 0:2 * BAND + L]
        sorted_x = [nc.dram_tensor(f"sorted_x{c}", (NB * P, D), fp32).ap() for c in range(2)]
        sorted_y = [nc.dram_tensor(f"sorted_y{c}", (NB * P, D), fp32).ap() for c in range(2)]
        qk_dram = nc.dram_tensor("qk_parts", (2, 2, 3, P, L), bf16).ap()

        s_x = [sem(f"s_x{c}") for c in range(4)]
        s_cst = sem("s_cst")
        s_lnst = sem("s_lnst")
        s_var = sem("s_var")
        s_std = sem("s_std")
        s_rstd = sem("s_rstd")
        s_xn = sem("s_xn")
        s_xt = sem("s_xt")
        s_xnT = sem("s_xnT")
        s_w = sem("s_w")
        s_aneg = sem("s_aneg")
        s_diag = sem("s_diag")
        s_unit = sem("s_unit")
        s_unita = sem("s_unita")
        s_silu = sem("s_silu")
        s_soft = sem("s_soft")
        s_bc = sem("s_bc")
        s_dt = sem("s_dt")
        s_u = sem("s_u")
        s_bcs = sem("s_bcs")
        s_bc3 = sem("s_bc3")
        s_bb = sem("s_bb")
        s_cb = sem("s_cb")
        s_bcp = sem("s_bcp")
        s_da = sem("s_da")
        s_dbu = sem("s_dbu")
        s_h = sem("s_h")
        s_hc = sem("s_hc")
        s_y = sem("s_y")
        s_yd = sem("s_yd")
        s_gt = sem("s_gt")
        s_op = sem("s_op")
        s_res = sem("s_res")
        s_wf = sem("s_wf")
        s_wd = sem("s_wd")
        s_lg = sem("s_lg")
        s_rt = sem("s_rt")
        s_df = sem("s_df")
        s_re = sem("s_re")
        s_both = sem("s_both")
        s_pr = sem("s_pr")
        s_cnt = sem("s_cnt")
        s_row = sem("s_row")
        s_mc = sem("s_mc")
        s_z = sem("s_z")
        s_sc = [sem(f"s_sc{c}") for c in range(2)]
        s_xl = [sem(f"s_xl{p}") for p in range(2)]
        s_tx = sem("s_tx")
        s_xgT = sem("s_xgT")
        s_g = sem("s_g")
        s_sg = sem("s_sg")
        s_up = sem("s_up")
        s_hd = sem("s_hd")
        s_th = sem("s_th")
        s_ht = sem("s_ht")
        s_dn = sem("s_dn")
        s_yb = sem("s_yb")
        s_ys = [sem(f"s_ys{p}") for p in range(2)]
        s_yg = [sem(f"s_yg{g}") for g in range(TB)]
        s_a1 = sem("s_a1")
        s_ad = sem("s_ad")
        s_out = sem("s_out")
        a_w = sem("a_w")
        a_cst = sem("a_cst")
        a_wo = sem("a_wo")
        a_xt = sem("a_xt")
        a_qk = sem("a_qk")
        a_qf = sem("a_qf")
        a_sa = sem("a_sa")
        a_sp = sem("a_sp")
        a_st = sem("a_st")
        a_ld = [sem(f"a_ld{p}") for p in range(2)]
        a_v = sem("a_v")
        a_va = sem("a_va")
        a_s = sem("a_s")
        a_ss = sem("a_ss")
        a_mx = sem("a_mx")
        a_ms = sem("a_ms")
        a_mm = sem("a_mm")
        a_mn = sem("a_mn")
        a_mt = sem("a_mt")
        a_ma = sem("a_ma")
        a_mp = sem("a_mp")
        a_ml = [sem(f"a_ml{p}") for p in range(2)]
        a_t = sem("a_t")
        a_tf = sem("a_tf")
        a_e = sem("a_e")
        a_ef = sem("a_ef")
        a_pv = sem("a_pv")
        a_ot = sem("a_ot")
        a_dn = sem("a_dn")
        a_rd = sem("a_rd")
        a_on = sem("a_on")
        a_op = sem("a_op")
        a_res = sem("a_res")

        block = ctx.enter_context(nc.Block())

        @block.sync
        def _(sp):
            xv = x.rearrange("b (t p) d -> p (b t) d", p=P)
            for c in range(4):
                sp.dma_start(X[:, ts(c, T // 4), :], xv[:, ts(c, T // 4), :]).then_inc(s_x[c], 16)
            ctx.enter_context(nc.allow_non_contiguous_dma(reason="small per-channel vectors"))
            if "ssm" in stages:
                col = lambda v: v.rearrange("(j p) -> p j", p=P)
                loads = [
                    (w_in_sb[:, :], w_in), (w_gate_sb[:, :], w_gate),
                    (w_delta_sb[:, :, :], w_delta.rearrange("(j p) n -> p j n", p=P)),
                    (w_out_sb[:, :, :], ssm_w_out.rearrange("(j p) n -> p j n", p=P)),
                    (b_out_row[:, :], ssm_b_out.rearrange("(a n) -> a n", a=1)),
                    (b_in_sb[:, :], col(b_in)), (b_gate_sb[:, :], col(b_gate)),
                    (conv_w_sb[:, :, :], conv_w.rearrange("(j p) a k -> p j (a k)", p=P)),
                    (conv_b_sb[:, :], col(conv_b)), (b_delta_sb[:, :], col(b_delta)),
                    (d_skip_sb[:, :], col(d_skip)),
                    (a_log_sb[:, :, :], a_log.rearrange("(j p) n -> p j n", p=P)),
                ]
                for r in range(3):
                    loads.append((w_bc_sb[:, :, r, 0:NS], w_b.rearrange("(j p) n -> p j n", p=P)))
                    loads.append((w_bc_sb[:, :, r, NS:2 * NS], w_c.rearrange("(j p) n -> p j n", p=P)))
                assert len(loads) == 18
                for dst, src in loads:
                    sp.dma_start(dst, src).then_inc(s_w, 16)
            if "moe" in stages:
                for dst, src in [
                    (rw_sb[:, :], router_w.rearrange("e d -> d e")),
                    (rb_sb[:, :], router_b.rearrange("(a e) -> a e", a=1).to_broadcast([P, E])),
                    (wg_sb[:, :, :], ffn_gate), (wu_sb[:, :, :], ffn_up),
                ]:
                    sp.dma_start(dst, src).then_inc(s_wf, 16)
                sp.wait_ge(s_cst, 3)
                for c in range(2):
                    sp.dma_start(sorted_x[c].rearrange("(n p) d -> p n d", p=P),
                                 zeros[:, None, :].to_broadcast([P, NB, D])).then_inc(s_z, 16)

            def moe_blocks(m, c):
                q = 2 * m + c
                sp.wait_ge(s_sc[c], 16 * 2 * TH * (m + 1))

                def load(j, p):
                    if not (isinstance(j, int) and j < 2):
                        sp.wait_ge(s_tx, q * NB + j - 1)
                    sp.dma_start(xg[:, p, :], sorted_x[c][ts(j, P), :]).then_inc(s_xl[p], 16)

                def store(j, p):
                    sp.wait_ge(s_yb, q * NB + j + 1)
                    sp.dma_start(sorted_y[c][ts(j, P), :], y_sb[:, p, :]).then_inc(s_ys[p], 16)

                load(0, 0)
                load(1, 1)
                load(2, 0)
                with sp.Fori(0, (NB - 3) // 2) as i:
                    for p in range(2):
                        load(2 * i + 3 + p, 1 - p)
                        store(2 * i + p, p)
                for j in range(NB - 3, NB):
                    store(j, j % 2)

            def moe(k):
                m = stages[:k].count("moe")
                if m == 0 and not (k and stages[k - 1] == "att"):
                    if k:
                        sp.wait_ge(s_dt, B)
                    sp.dma_start(mc[:, :], moe_consts).then_inc(s_mc, 16)
                if k and stages[k - 1] == "ssm":
                    sp.wait_ge(s_res, B)
                elif k:
                    sp.wait_ge(a_res, B)
                if m == 0:
                    sp.dma_start(wd_sb[:, :, :, :], ffn_down).then_inc(s_wd, 16)
                for c in range(2):
                    moe_blocks(m, c)

            def attention(k):
                if k:
                    for p in range(2):
                        sp.wait_ge(s_ys[p], 16 * OF_PARITY[p] * 2)
                sp.wait_ge(s_cst, 7)
                if "moe" not in stages[:k]:
                    sp.dma_start(mc[:, :], moe_consts).then_inc(s_mc, 16)
                bv = b_qkv[2 * D:]
                loads = [(wqkv_sb[:, :], w_qkv), (bo_row[:, :], att_b_out.rearrange("(a n) -> a n", a=1)),
                         (bqk_sb[:, :], b_qkv[0:2 * D].rearrange("(c p) -> p c", p=P)),
                         (bv_all[:, :, :], bv.rearrange("(a h d) -> a h d", a=1, h=NH).to_broadcast([P, NH, DH])),
                         (consts_f, att_consts[:, 0:2 * BAND + L]), (den_pick[:, :], att_consts[:, 2 * BAND + L:])]
                for r in range(R):
                    loads.append((bv_str[ts(r, 32), :, :],
                                  bv.rearrange("(g r d) -> r g d", g=G, r=R)[r:r + 1].to_broadcast([32, G, DH])))
                for dst, src in loads:
                    sp.dma_start(dst, src).then_inc(a_w, 16)
                sp.wait_ge(a_cst, 1)
                for r in range(R):
                    sp.dma_start(wo_sb[32 * r:32 * r + DH, :, :],
                                 att_w_out.rearrange("(g r d) n -> r d g n", g=G, r=R)[r]).then_inc(a_wo, 16)

                def stack(b, p):
                    sp.wait_ge(a_sp, 2 * b + 2)
                    if not (isinstance(b, int) and b < 2):
                        sp.wait_ge(a_pv, NH * (b - 1))
                    sp.dma_start(qk_dram[p].rearrange("c t p n -> p c t n"), qk_p[:, :, :, :]).then_inc(a_st, 16)
                    sp.wait_ge(a_st, 16 * b + 16)
                    for c, (dst, terms) in enumerate(((qs, TERMS_Q), (ks, TERMS_K))):
                        for z in range(2):
                            for i, t in enumerate(terms):
                                src = qk_dram[p, c, t].rearrange("(m z d) n -> z d m n", z=2, d=DH)[z]
                                at = 64 * z + DH * i
                                sp.dma_start(dst[at:at + DH, p, :, :], src).then_inc(a_ld[p], 16)

                def stack_max(b, p):
                    sp.wait_ge(a_mp, 2 * b + 2)
                    for z in range(2):
                        for t in range(3):
                            at = 64 * z + TR + t
                            sp.dma_start(qs[at:at + 1, p, :, :], m_p[ts(z, NH // 2), t, :]).then_inc(a_ml[p], 16)

                for b in range(2):
                    stack(b, b)
                    stack_max(b, b)
                with sp.Fori(0, (B - 2) // 2) as i:
                    for p in range(2):
                        stack(2 * i + 2 + p, p)
                        stack_max(2 * i + 2 + p, p)
            for k, stage in enumerate(stages):
                if stage == "moe":
                    moe(k)
                elif stage == "att":
                    attention(k)
            ov = out.rearrange("b (t p) d -> p (b t) d", p=P)
            for b in range(B):
                if stages[-1] == "moe":
                    sp.wait_ge(s_ad, T * (stages.count("moe") - 1) + TB * (b + 1))
                else:
                    sp.wait_ge(s_res if stages[-1] == "ssm" else a_res, b + 1)
                sp.dma_start(ov[:, ts(b, TB), :], X[:, ts(b, TB), :]).then_inc(s_out, 16)
            sp.wait_ge(s_out, 16 * B)

        @block.gpsimd
        def _(pool):
            nc.gpsimd.memset(ident[:, :], 0.0).then_inc(s_cst, 1)
            nc.gpsimd.memset(ones_row[:, :], 1.0)
            nc.gpsimd.memset(eps_col[:, :], EPS)
            nc.gpsimd.memset(zeros[:, :], 0.0)
            nc.gpsimd.memset(xz[:, :, :, 0:PAD], 0.0)
            nc.gpsimd.memset(pick[:, :, :], 0.0).then_inc(s_cst, 1)
            pool.wait_ge(s_cst, 2)
            nc.gpsimd.affine_select(out=ident[:, :], in_=ident[:, :], compare_op=ALU.not_equal, fill=1.0,
                                    base=0, pattern=[[-1, P]], channel_multiplier=1).then_inc(s_cst, 1)
            for k in range(3):
                if k:
                    pool.wait_ge(s_cst, 3 + k)
                nc.gpsimd.affine_select(out=pick[:, :, :], in_=pick[:, :, :], compare_op=ALU.not_equal,
                                        fill=1.0, base=-2 * NS * k, pattern=[[-1, 2 * NS], [0, P]],
                                        channel_multiplier=1).then_inc(s_cst, 1)

            pool.wait_ge(s_cst, 6)
            nc.gpsimd.tensor_copy(identb[:, :], ident[:, :]).then_inc(s_cst, 1)

            def ssm_split_bc(b, p, k):
                if k == 0:
                    pool.wait_ge(s_bc, b + 1)
                    nc.gpsimd.tensor_tensor(bc_r[:, :], bc_f[:, :], bc3[:, p, :], ALU.subtract).then_inc(s_bcs, 1)
                elif k == 1:
                    if not (isinstance(b, int) and b == 0):
                        pool.wait_ge(s_bc3, b)
                    nc.gpsimd.tensor_tensor(bc_p2[:, :], bc_f[:, :], bc3[:, p, :], ALU.subtract).then_inc(s_bcs, 1)
                else:
                    pool.wait_ge(s_bcs, 3 * b + 2)
                    nc.gpsimd.tensor_tensor(bc_r2[:, :], bc_r[:, :], bc_p2[:, :], ALU.subtract).then_inc(s_bcs, 1)

            def ssm_u(b, p):
                pool.wait_ge(s_dt, b + 1)
                nc.gpsimd.tensor_tensor(u[:, p, :, :], dt[:, p, :, :], act_x[:, p, :, :], ALU.mult).then_inc(s_u, 1)

            def ssm_batch(b, p, last, along={}):
                for n in range(NS):
                    if n == 0:
                        pool.wait_ge(s_u, b + 1)
                    pool.wait_ge(s_bcp, NS * b + n + 1)
                    if not (isinstance(b, int) and b == 0 and n < 2):
                        pool.wait_ge(s_h, 2 * (NS * b + n - 1))
                    nc.gpsimd.tensor_tensor(dbu[:, n % 2, :, :], u[:, p, :, :],
                                            b_sb[:, n % ROWS_B, None, :].to_broadcast([P, J, L]),
                                            ALU.mult).then_inc(s_dbu, 1)
                    if not last and n == 10:
                        ssm_split_bc(b + 1, 1 - p, 0)
                        ssm_split_bc(b + 1, 1 - p, 1)
                    if not last and n == 11:
                        ssm_split_bc(b + 1, 1 - p, 2)
                    if not last and n == 14:
                        ssm_u(b + 1, 1 - p)
                    if n in along:
                        along[n]()

            def scatter(m, c, tiles):
                pool.wait_ge(s_row, 2 * m + c + 1)
                pool.wait_ge(s_z, 32)
                for t in tiles:
                    for k in range(2):
                        nc.gpsimd.indirect_dma_start(
                            sorted_x[c], bass.IndirectOffsetOnAxis(ap=row[:, c, k, t:t + 1], axis=0),
                            xna[c][:, t, :], None).then_inc(s_sc[c], 16)

            if "ssm" in stages:
                for k in range(3):
                    ssm_split_bc(0, 0, k)
                ssm_u(0, 0)
                ssm_batch(0, 0, False)
                with pool.Fori(0, (B - 2) // 2) as i:
                    ssm_batch(2 * i + 1, 1, False)
                    ssm_batch(2 * i + 2, 0, False)
                along = {}
                if early(1):
                    for i, n in enumerate(STEPS_AHEAD):
                        along[n] = lambda i=i: scatter(0, 0, range(TILES_AHEAD * i, TILES_AHEAD * (i + 1)))
                ssm_batch(B - 1, 1, True, along)

            def moe(m):
                done = TILES_AHEAD * len(STEPS_AHEAD) if m == 0 and stages[0] == "ssm" else 0
                scatter(m, 0, range(done, TH))
                scatter(m, 1, range(TH))
                for c in range(2):
                    q = 2 * m + c
                    for p in range(2):
                        pool.wait_ge(s_ys[p], 16 * OF_PARITY[p] * (q + 1))
                    for t in range(TH):
                        for k in range(2):
                            nc.gpsimd.indirect_dma_start(
                                yg[c][:, k, t, :], None, sorted_y[c],
                                bass.IndirectOffsetOnAxis(ap=row[:, c, k, t:t + 1], axis=0)).then_inc(s_yg[t // TB], 16)

            if "moe" in stages and stages[0] != "att":
                moe(0)

            if "att" in stages:
                def att_split(b, p):
                    pool.wait_ge(a_sa, 2 * b + 1)
                    if not (isinstance(b, int) and b == 0):
                        pool.wait_ge(a_mp, 2 * b)
                    nc.gpsimd.tensor_tensor(qk_r[:, :, :], qk_f[:, :, :], qk_p[:, :, 0, :], ALU.subtract).then_inc(a_sp, 1)
                    pool.wait_ge(a_sa, 2 * b + 2)
                    pool.wait_ge(a_sp, 2 * b + 1)
                    nc.gpsimd.tensor_tensor(qk_p[:, :, 2, :], qk_r[:, :, :], qk_p[:, :, 1, :], ALU.subtract).then_inc(a_sp, 1)

                def att_split_max(b, p):
                    pool.wait_ge(a_ma, 3 * b + 2)
                    nc.gpsimd.tensor_tensor(m_r, m_f, m_p[:, 0, :], ALU.subtract).then_inc(a_mp, 1)
                    pool.wait_ge(a_ma, 3 * b + 3)
                    pool.wait_ge(a_mp, 2 * b + 1)
                    nc.gpsimd.tensor_tensor(m_p[:, 2, :], m_r, m_p[:, 1, :], ALU.subtract).then_inc(a_mp, 1)

                def att_next(b, p):
                    att_split(b, p)
                    att_split_max(b, p)

                att_next(0, 0)
                att_next(1, 1)
                with pool.Fori(1, B // 2) as i:
                    att_next(2 * i, 0)
                    att_next(2 * i + 1, 1)
                if stages[-1] == "moe":
                    moe(stages.count("moe") - 1)

        @block.scalar
        def _(act):
            def deviations(k, c):
                act.wait_ge(s_var, 2 * k + c + 1)
                if k == 0 and c == 0:
                    act.wait_ge(s_cst, 2 if stages[0] == "ssm" else 7)
                nc.scalar.activation(std[:, ts(c, TH)], mv[:, ts(c, TH), 1], ACT.Sqrt, bias=eps_col[:, :]).then_inc(s_std, 1)

            def turned_over(k, b, n_bank):
                act.wait_ge(s_xt, B * k + b + 1)
                nc.scalar.activation(xnT[:, ts(b, L)], bank[n_bank][:, :], ACT.Copy).then_inc(s_xnT, 1)

            def transposed(k, c, first_bank):
                for b in range(c * B // 2, (c + 1) * B // 2):
                    turned_over(k, b, first_bank + b % 2)

            def moe_exp(m, c):
                act.wait_ge(s_df, 2 * m + c + 1)
                nc.scalar.activation(top[:, 3, :], top[:, 2, :], ACT.Exp).then_inc(s_re, 1)

            def layer_norm(k, c):
                deviations(k, c)
                transposed(k, c, 0)
                if stages[k] == "moe":
                    moe_exp(stages[:k].count("moe"), c)

            def layer_norms(k):
                if early(k):
                    return
                layer_norm(k, 0)
                if stages[k] == "att":
                    att_xt(0, 0)
                    att_split(0, 0)
                layer_norm(k, 1)

            def ssm_read(b, p, k):
                act.wait_ge(s_unit, 9 * b + k + 1)
                ps = bank_pre[(k + (k > 5)) % 2]
                if k in (0, 1):
                    nc.scalar.activation(xz[:, p, k, PAD:], ps[:, :], ACT.Identity,
                                         bias=b_in_sb[:, k:k + 1]).then_inc(s_unita, 1)
                elif k in (2, 3):
                    if k == 2 and not (isinstance(b, int) and b == 0):
                        act.wait_ge(s_silu, b)
                    nc.scalar.activation(lin[:, k - 2, :], ps[:, :], ACT.Identity,
                                         bias=b_gate_sb[:, k - 2:k - 1]).then_inc(s_unita, 1)
                elif k in (4, 5):
                    nc.scalar.activation(lin[:, J + k - 4, :], ps[:, :], ACT.Identity,
                                         bias=conv_b_sb[:, k - 4:k - 3]).then_inc(s_unita, 1)
                elif k == 6:
                    if not (isinstance(b, int) and b == 0):
                        act.wait_ge(s_bcs, 3 * b)
                    nc.scalar.activation(bc_f[:, :], ps[0:96, :], ACT.Copy).then_inc(s_unita, 1)
                    act.wait_ge(s_unita, 9 * b + 7)
                    nc.scalar.activation(bc3[:, p, :], bc_f[:, :], ACT.Copy).then_inc(s_bc, 1)
                else:
                    if k == 7 and not (isinstance(b, int) and b == 0):
                        act.wait_ge(s_dt, b)
                    nc.scalar.activation(pre_dt[:, k - 7, :], ps[:, :], ACT.Identity,
                                         bias=b_delta_sb[:, k - 7:k - 6]).then_inc(s_unita, 1)

            def ssm_silu(b, p):
                act.wait_ge(s_unita, 9 * b + 6)
                if not (isinstance(b, int) and b < 2):
                    act.wait_ge(s_gt, b - 1)
                nc.scalar.activation(gact[:, p, :, :], lin[:, :, :], ACT.Silu).then_inc(s_silu, 1)
                nc.scalar.preload_act_table_set("natural_log_exp_and_others")

            def ssm_soft(b, k):
                if k == 0:
                    act.wait_ge(s_unita, 9 * b + 9)
                    nc.scalar.activation(soft[:, :, :], pre_dt[:, :, :], ACT.Abs).then_inc(s_soft, 1)
                elif k == 1:
                    act.wait_ge(s_soft, 3 * b + 1)
                    nc.scalar.activation(soft[:, :, :], soft[:, :, :], ACT.Exp, scale=-1.0).then_inc(s_soft, 1)
                else:
                    act.wait_ge(s_soft, 3 * b + 2)
                    nc.scalar.activation(soft[:, :, :], soft[:, :, :], ACT.Ln, bias=1.0).then_inc(s_soft, 1)

            def ssm_prepare(b, p, n):
                for k in {3: (0, 1), 4: (2,), 5: (3,), 7: (4,), 9: (5,), 11: (6,), 12: (7,), 13: (8,)}.get(n, ()):
                    ssm_read(b, p, k)
                if n == 9:
                    ssm_silu(b, p)
                for k in {14: (0, 1), 15: (2,)}.get(n, ()):
                    ssm_soft(b, k)

            def ssm_row_b(b, n):
                act.wait_ge(s_bb, NS * b + n + 1)
                if not (isinstance(b, int) and b == 0 and n < ROWS_B):
                    act.wait_ge(s_dbu, NS * b + n + 1 - ROWS_B)
                nc.scalar.activation(b_sb[:, n % ROWS_B, :], bank_b[n % 2][:, :], ACT.Copy).then_inc(s_bcp, 1)

            def ssm_batch(b, p, first, last, along={}):
                if first:
                    ssm_row_b(b, 0)
                for n in range(NS):
                    if n + 1 < NS:
                        ssm_row_b(b, n + 1)
                    elif not last:
                        ssm_row_b(b + 1, 0)
                    for j in range(J):
                        if n == 0 and j == 0:
                            act.wait_ge(s_dt, b + 1)
                        if not (first and n < DECAYS):
                            act.wait_ge(s_h, 2 * (NS * b + n - DECAYS) + j + 1)
                        nc.scalar.activation(decay[n % DECAYS][j], dt[:, p, j, :], ACT.Exp,
                                             scale=a_neg[:, j, n:n + 1]).then_inc(s_da, 1)
                    if not last:
                        ssm_prepare(b + 1, 1 - p, n)
                    if n in along:
                        along[n]()

            def moe_blocks(m, c, along={}):
                base = (2 * m + c) * NB
                peeled = 12 if along else 2

                def tokens(j, p):
                    act.wait_ge(s_tx, base + j + 1)
                    if not (isinstance(base + j, int) and base + j < 2):
                        act.wait_ge(s_up, base + j - 1)
                    nc.scalar.activation(xgT[:, p, :], bank[5][:, 0:P], ACT.Copy).then_inc(s_xgT, 1)

                def silu(j, p):
                    act.wait_ge(s_g, base + j + 1)
                    if not (isinstance(base + j, int) and base + j < 2):
                        act.wait_ge(s_hd, base + j - 1)
                    nc.scalar.activation(sg[:, p, :], bank[p][:, :], ACT.Silu).then_inc(s_sg, 1)

                def turned(j, p):
                    act.wait_ge(s_th, base + j + 1)
                    if not (isinstance(base + j, int) and base + j < 2):
                        act.wait_ge(s_dn, base + j - 1)
                    nc.scalar.activation(hidT[:, p, :, :], bank[4][:, :].rearrange("p (c n) -> p c n", c=HC),
                                         ACT.Copy).then_inc(s_ht, 1)

                def step(j, p):
                    if not (isinstance(j, int) and j == 0):
                        turned(j - 1, 1 - p)
                    silu(j, p)
                    if not (isinstance(j, int) and j == NB - 1):
                        tokens(j + 1, 1 - p)

                tokens(0, 0)
                for j in range(peeled):
                    step(j, j % 2)
                    if j in along:
                        along[j]()
                with act.Fori(peeled // 2, NB // 2) as i:
                    for p in range(2):
                        step(2 * i + p, p)
                step(NB - 1, 0)
                turned(NB - 1, 0)

            def att_split(b, p):
                act.wait_ge(a_qf, b + 1)
                if not (isinstance(b, int) and b == 0):
                    act.wait_ge(a_st, 16 * b)
                nc.scalar.activation(qk_p[:, :, 0, :], qk_f[:, :, :], ACT.Copy).then_inc(a_sa, 1)
                act.wait_ge(a_sp, 2 * b + 1)
                nc.scalar.activation(qk_p[:, :, 1, :], qk_r[:, :, :], ACT.Copy).then_inc(a_sa, 1)

            def att_xt(b, p):
                if not (isinstance(b, int) and b < 2):
                    act.wait_ge(a_v, b - 1)
                act.wait_ge(s_xnT, B * stages.index("att") + b + 1)
                nc.scalar.activation(xt[:, p, :], xnT[:, ts(b, L)], ACT.Copy).then_inc(a_xt, 1)

            def att_split_max(b, p, k):
                act.wait_ge(a_mt, b + 1)
                if not (isinstance(b, int) and b == 0):
                    act.wait_ge(a_ml[1 - p], 96 * (k + p))
                nc.scalar.activation(m_f, bank[0][0:NH, :], ACT.Copy).then_inc(a_ma, 1)
                act.wait_ge(a_ma, 3 * b + 1)
                nc.scalar.activation(m_p[:, 0, :], m_f, ACT.Copy).then_inc(a_ma, 1)
                act.wait_ge(a_mp, 2 * b + 1)
                nc.scalar.activation(m_p[:, 1, :], m_r, ACT.Copy).then_inc(a_ma, 1)

            def att_exps(b, p, at_head=None):
                def sums(g):
                    act.wait_ge(a_pv, NH * b + R * (g + 1))
                    if not (isinstance(b, int) and b == 0 and g < 2):
                        act.wait_ge(a_on, G * b + g - 1)
                    nc.scalar.activation(ots[:, g % 2, :], bank[6 + g % 2][:, :], ACT.Copy).then_inc(a_ot, 1)

                for h_ in range(NH):
                    if at_head and h_ in at_head:
                        at_head[h_]()
                    g = h_ // R
                    if h_ % R == 0:
                        act.wait_ge(a_tf, G * b + g + 1)
                        if not (isinstance(b, int) and b == 0 and g < 2):
                            act.wait_ge(a_pv, NH * b + R * (g - 1))
                        nc.scalar.activation(pts[:, g % 2, :], bank[1][:, :], ACT.Exp).then_inc(a_ef, 1)
                    act.wait_ge(a_t, NH * b + h_ + 1)
                    if not (isinstance(b, int) and b == 0 and h_ < 2):
                        act.wait_ge(a_pv, NH * b + h_ - 1)
                    nc.scalar.activation(pt[:, h_ % 2, WINDOW:TB * BAND - WINDOW],
                                         score[h_ % 2][:, :, :].rearrange("p a b -> p (a b)")[:, WINDOW:TB * BAND - WINDOW],
                                         ACT.Exp).then_inc(a_e, 1)
                    if h_ >= R + 1 and (h_ - R - 1) % R == 0:
                        sums((h_ - R - 1) // R)
                sums(G - 1)

            for k, stage in enumerate(stages):
                layer_norms(k)
                if stage == "ssm":
                    act.wait_ge(s_w, 16 * 18)
                    nc.scalar.activation(a_exp[:, :, :], a_log_sb[:, :, :], ACT.Exp).then_inc(s_aneg, 1)
                    act.wait_ge(s_aneg, 1)
                    nc.scalar.mul(a_neg[:, :, :], a_exp[:, :, :], -1.0).then_inc(s_aneg, 1)
                    act.wait_ge(s_aneg, 2)
                    for n in range(NS):
                        ssm_prepare(0, 0, n)
                    ssm_batch(0, 0, True, False)
                    with act.Fori(0, (B - 2) // 2) as i:
                        ssm_batch(2 * i + 1, 1, False, False)
                        ssm_batch(2 * i + 2, 0, False, False)
                    along = {}
                    if early(k + 1):
                        along = {2: lambda: deviations(k + 1, 0), 6: lambda: moe_exp(0, 0)}
                        for n in range(2):
                            along[4 + n] = lambda n=n: [turned_over(k + 1, b, 6 + b % 2) for b in (2 * n, 2 * n + 1)]
                    ssm_batch(B - 1, 1, False, True, along)
                elif stage == "moe":
                    m = stages[:k].count("moe")
                    along = {}
                    if early(k):
                        along = {1: lambda: deviations(k, 1), 10: lambda: moe_exp(m, 1)}
                        for b in range(B // 2, B):
                            along[b - B // 2 + 3] = lambda b=b: turned_over(k, b, 7)
                    moe_blocks(m, 0, along)
                    moe_blocks(m, 1)
                else:
                    att_xt(1, 1)
                    att_split_max(0, 0, 0)
                    att_split(1, 1)

                    def att_step(b, p, i, more=True, at_head=None):
                        att_exps(b, p, at_head)
                        if at_head:
                            transposed(k + 1, 0, 6)
                        if more:
                            att_xt(b + 2, p)
                        att_split_max(b + 1, 1 - p, i)
                        if more:
                            att_split(b + 2, p)

                    att_step(0, 0, 0)
                    with act.Fori(0, (B - 4) // 2) as i:
                        att_step(2 * i + 1, 1, i + 1)
                        att_step(2 * i + 2, 0, i + 1)
                    att_step(B - 3, 1, B // 2 - 1)
                    follow = k + 1 < len(stages)
                    att_step(B - 2, 0, B // 2 - 1, False, {10: lambda: deviations(k + 1, 0)} if follow else None)
                    att_exps(B - 1, 1, {3: lambda: moe_exp(stages[:k].count("moe"), 0)} if follow else None)

        @block.tensor
        def _(pe):
            def transpose(k, b, n_bank, ahead):
                pe.wait_ge(s_xn, B * k + b + 1)
                if B * k + b >= ahead:
                    pe.wait_ge(s_xnT, B * k + b + 1 - ahead)
                for t in range(TB):
                    g = TB * b + t
                    src = xna[g // TH][:, g % TH, :] if stages[k] == "moe" else xn[:, b % 2, t, :]
                    mm = nc.tensor.transpose(bank[n_bank][:, ts(t, P)], src, ident[:, :])
                mm.then_inc(s_xt, 1)

            def transposes(k, c, first_bank):
                if k == 0 and c == 0:
                    pe.wait_ge(s_cst, 3)
                for b in range(c * B // 2, (c + 1) * B // 2):
                    transpose(k, b, first_bank + b % 2, 2)

            def layer_norms(k):
                moe = stages[k] == "moe"
                if early(k):
                    return
                for c in range(2):
                    transposes(k, c, 0)
                    if moe:
                        moe_logits(k, c)
                        moe_counts(k, c)
                    elif stages[k] == "att" and c == 0:
                        pe.wait_ge(a_w, 16 * 10)
                        pe.wait_ge(a_cst, 10)
                        att_project(0, 0)

            def moe_logits(k, c):
                m = stages[:k].count("moe")
                pe.wait_ge(s_xnT, B * k + (c + 1) * B // 2)
                pe.wait_ge(s_wf, 16 * 4)
                if c:
                    pe.wait_ge(s_cnt, 2 * m + c)
                for t in range(TH):
                    mm = nc.tensor.matmul(bank[7][:, ts(t, E)], xnT[:, ts(TH * c + t, P)], rw_sb[:, :], start=True,
                                          stop=True, skip_group_check=True)
                mm.then_inc(s_lg, 1)

            def moe_counts(k, c):
                pe.wait_ge(s_both, 2 * stages[:k].count("moe") + c + 1)
                flat = both.rearrange("p t e -> p (t e)")
                nc.tensor.matmul(bank[7][:, TH * E:2 * TH * E], ones_sq, flat, start=True, stop=True, skip_group_check=True)
                nc.tensor.matmul(bank[7][:, 2 * TH * E:3 * TH * E], before, flat, start=True, stop=True,
                                 skip_group_check=True).then_inc(s_pr, 1)

            def ssm_unit(b, p, k, part=None):
                if k == 0:
                    if not (isinstance(b, int) and b == 0):
                        pe.wait_ge(s_unita, 9 * b - 1)
                elif k == 1:
                    if not (isinstance(b, int) and b == 0):
                        pe.wait_ge(s_unita, 9 * b)
                elif k == 7:
                    if not (isinstance(b, int) and b < 2):
                        pe.wait_ge(s_res, b - 1)
                elif not part:
                    pe.wait_ge(s_unita, 9 * b + (k - 1 if k < 6 else k if k == 6 else 7))
                ps = bank_pre[(k + (k > 5)) % 2]
                xs = xnT[:, ts(b, L)]
                if k < 4:
                    w = w_in_sb if k < 2 else w_gate_sb
                    mm = nc.tensor.matmul(ps[:, :], w[:, ts(k % 2, P)], xs, start=True, stop=True)
                elif k < 6:
                    for t in (0, 1) if part == 0 else (2, 3):
                        mm = nc.tensor.matmul(ps[:, :], conv_diag[:, k - 4, t, :], xz[:, p, k - 4, t:t + L],
                                              start=(t == 0), stop=(t == KC - 1))
                    if part == 0:
                        return
                else:
                    pe.wait_ge(s_silu, b + 1)
                    for c in range(J):
                        w = w_bc_sb[:, c, :, :] if k == 6 else w_delta_sb[:, c, ts(k - 7, P)]
                        mm = nc.tensor.matmul(ps[0:96, :] if k == 6 else ps[:, :], w, act_x[:, p, c, :],
                                              start=(c == 0), stop=(c == J - 1))
                mm.then_inc(s_unit, 1)

            def ssm_prepare(b, p, n):
                for k, part in {0: ((0, None), (1, None)), 1: ((2, None),), 2: ((3, None),), 3: ((4, 0),), 4: ((4, 1),),
                                5: ((5, 0),), 6: ((5, 1),), 8: ((6, None),), 9: ((7, None),), 10: ((8, None),)}.get(n, ()):
                    ssm_unit(b, p, k, part)

            def ssm_row_b(b, p, n):
                if n == 0:
                    pe.wait_ge(s_bc3, b + 1)
                if not (isinstance(b, int) and b == 0 and n < 2):
                    pe.wait_ge(s_bcp, NS * b + n - 1)
                nc.tensor.matmul(bank_b[n % 2][:, :], pick[:, n, :], bc3[:, p, :], start=True, stop=True).then_inc(s_bb, 1)

            def ssm_row_c(b, p, n):
                if not (isinstance(b, int) and b == 0 and n < 2):
                    pe.wait_ge(s_hc, NS * b + n - 1)
                nc.tensor.matmul(bank_c[n % 2][:, :], pick[:, NS + n, :], bc3[:, p, :], start=True, stop=True).then_inc(s_cb, 1)

            def ssm_accumulate(b, n, q):
                pe.wait_ge(s_hc, NS * b + n + 1)
                if n == 0 and not (isinstance(b, int) and b == 0):
                    pe.wait_ge(s_yd, b)
                for j in range(J):
                    mm = nc.tensor.matmul(bank_y[j][:, :], ident[:, :], hc[:, q, j, :],
                                          start=(n == 0), stop=(n == NS - 1))
                mm.then_inc(s_y, 1)

            def ssm_out(b, p, last):
                pe.wait_ge(s_gt, b + 1)
                if not last:
                    pe.wait_ge(s_unita, 9 * B - 1 if isinstance(b, int) and b == B - 2 else 9 * (b + 2) + 5)
                else:
                    pe.wait_ge(s_res, b)
                for t in range(TB):
                    nc.tensor.matmul(bank_pre[0][:, ts(t, P)], ones_row[:, :], b_out_row[:, :], start=True, stop=False,
                                     skip_group_check=True)
                    for j in range(J):
                        mm = nc.tensor.matmul(bank_pre[0][:, ts(t, P)], gated[:, j, ts(t, P)], w_out_sb[:, j, :],
                                              start=False, stop=(j == J - 1), skip_group_check=True)
                mm.then_inc(s_op, 1)

            def ssm_batch(b, p, first, last, along={}):
                if first:
                    for n in range(LEAD):
                        ssm_row_b(b, p, n)
                    ssm_row_c(b, p, 0)
                for n in range(NS):
                    if n + 1 < NS:
                        ssm_row_c(b, p, n + 1)
                    elif not last:
                        ssm_row_c(b + 1, 1 - p, 0)
                    if n + LEAD < NS:
                        ssm_row_b(b, p, n + LEAD)
                    elif not last:
                        ssm_row_b(b + 1, 1 - p, n + LEAD - NS)
                    if n:
                        ssm_accumulate(b, n - 1, (n - 1) % 2)
                    elif not first:
                        ssm_accumulate(b - 1, NS - 1, 1)
                    if not last:
                        ssm_prepare(b + 1, 1 - p, n)
                    if not first and n == 7:
                        ssm_out(b - 1, 1 - p, False)
                    if n in along:
                        along[n]()
                if last:
                    ssm_accumulate(b, NS - 1, 1)
                    ssm_out(b, p, True)

            def moe_blocks(m, c, along={}):
                groups = 3 if along else 0
                base = (2 * m + c) * NB

                def experts(i):
                    word = pe.value_load(expert[0:1, c, ds(i, 1)], min_val=0, max_val=E ** DIGITS - 1)
                    return [(word // E ** r) % E for r in range(DIGITS)]

                def tokens(j, p):
                    pe.wait_ge(s_xl[p], 16 * ((2 * m + c) * OF_PARITY[p] + 1) + (j - p) * 8)
                    if not (isinstance(base + j, int) and base + j < 1):
                        pe.wait_ge(s_xgT, base + j)
                    nc.tensor.transpose(bank[5][:, 0:P], xg[:, p, :], ident[:, :]).then_inc(s_tx, 1)

                def gate_up(w, out, done, e, p):
                    nc.tensor.matmul(out[:, None, :], xgT[:, p, :], w[:, ds(e, 1), :], start=True, stop=True).then_inc(done, 1)

                def hidden(j, p):
                    pe.wait_ge(s_hd, base + j + 1)
                    if not (isinstance(base + j, int) and base + j < 1):
                        pe.wait_ge(s_ht, base + j)
                    for ch in range(HC):
                        mm = nc.tensor.transpose(bank[4][:, ts(ch, P)], hid[:, p, ts(ch, P)], ident[:, :])
                    mm.then_inc(s_th, 1)

                def down(j, p, e):
                    pe.wait_ge(s_ht, base + j + 1)
                    if not (isinstance(base + j, int) and base + j < 1):
                        pe.wait_ge(s_yb, base + j)
                    for ch in range(HC):
                        mm = nc.tensor.matmul(bank[6][:, None, 0:P], hidT[:, p, ch, :], wd_sb[:, ds(e, 1), ch, :],
                                              start=(ch == 0), stop=(ch == HC - 1))
                    mm.then_inc(s_dn, 1)

                def step(j, p, e_before, e):
                    if not (isinstance(j, int) and j == 0):
                        hidden(j - 1, 1 - p)
                    pe.wait_ge(s_xgT, base + j + 1)
                    if not (isinstance(base + j, int) and base + j < 2):
                        pe.wait_ge(s_sg, base + j - 1)
                    gate_up(wg_sb, bank[p], s_g, e, p)
                    if not (isinstance(base + j, int) and base + j < 2):
                        pe.wait_ge(s_hd, base + j - 1)
                    gate_up(wu_sb, bank[2 + p], s_up, e, p)
                    if not (isinstance(j, int) and j == NB - 1):
                        tokens(j + 1, 1 - p)
                    if not (isinstance(j, int) and j == 0):
                        down(j - 1, 1 - p, e_before)

                pe.wait_ge(s_row, 2 * m + c + 1)
                pe.wait_ge(s_wd, 16)
                tokens(0, 0)
                e = experts(0)
                for j in range(3 + 4 * groups):
                    r = (j - 3) % 4 if j >= 3 else j + 1
                    if j >= 3 and r == 0:
                        e = experts((j - 3) // 4 + 1)
                    step(j, j % 2, e[r], e[r + 1])
                    if j in along:
                        along[j]()
                with pe.Fori(groups, (NB - 7) // 4) as i:
                    e = experts(i + 1)
                    for r in range(4):
                        step(4 * i + 3 + r, (r + 1) % 2, e[r], e[r + 1])
                e = experts(WORDS - 1)
                for r in range(4):
                    step(NB - 4 + r, (r + 1) % 2, e[r], e[r + 1])
                hidden(NB - 1, 0)
                down(NB - 1, 0, e[4])

            def att_project(b, p):
                pe.wait_ge(a_xt, b + 1)
                if isinstance(b, int) and b == 1:
                    pe.wait_ge(a_qf, 1)
                elif not (isinstance(b, int) and b == 0):
                    pe.wait_ge(a_ot, G * (b - 1))
                for c in range(2):
                    mm = nc.tensor.matmul(bank[6 + c][:, :], wqkv_sb[:, ts(c, D)], xt[:, p, :], start=True, stop=True)
                mm.then_inc(a_qk, 1)
                if not (isinstance(b, int) and b == 0):
                    pe.wait_ge(a_mx, NH * b)
                for t in range(TB):
                    nc.tensor.matmul(bank[2][:, ts(t, P)], xt[:, p, ts(t, P)], wqkv_sb[:, 2 * D:], start=True, stop=True,
                                     skip_group_check=True)
                wv = wqkv_sb[:, 2 * D:].rearrange("p (g r d) -> p r g d", g=G, r=R)
                for r in range(R):
                    mm = nc.tensor.matmul(bank[4][32 * r:32 * r + KS_N, 0:G * DH], xt[:, p, 0:L:STRIDE], wv[:, r, :, :],
                                          start=True, stop=True)
                mm.then_inc(a_v, 1)

            def att_scores(b, p, k, between=None):
                pe.wait_ge(a_ld[p], 384 * (k + 1))
                if isinstance(b, int) and b == 0:
                    pe.wait_ge(a_va, 1)
                else:
                    pe.wait_ge(a_ef, G * b)
                    pe.wait_ge(a_rd, G * b - 1)
                for z in range(2):
                    for qt in range(TB):
                        for m in range(NH // 2):
                            mm = nc.tensor.matmul(bank[z][:, ds(P * qt + KS_N * m, KS_N)],
                                                  qs[64 * z:64 * z + TR, p, m, ts(qt, P)],
                                                  ks[64 * z:64 * z + TR, p, m, 0:L:STRIDE], start=True, stop=True,
                                                  skip_group_check=True)
                    mm.then_inc(a_ss, 1)
                for qt in range(TB):
                    if between and qt == 1:
                        between()
                    lo, hi = reach[qt]
                    for g in range(G):
                        u_ = G * qt + g
                        if u_ >= 2:
                            pe.wait_ge(a_mx, NH * b + u_ - 1)
                        elif not (isinstance(b, int) and b == 0):
                            pe.wait_ge(a_e, NH * b)
                        sc = score[u_ % 2]
                        for c in range(2):
                            nc.tensor.matmul(sc[:, 2 * c:2 * c + 2, :], identb[:, :],
                                             band_q[:, None, :].to_broadcast([P, 2, BAND]), start=True, stop=False,
                                             skip_group_check=True)
                        for r in range(R):
                            z, m = r // 2, 2 * g + r % 2
                            k0 = P * qt - WINDOW
                            mm = nc.tensor.matmul(sc[:, r, lo:hi], qs[64 * z:64 * z + TR, p, m, ts(qt, P)],
                                                  ks[64 * z:64 * z + TR, p, m, k0 + lo:k0 + hi], start=False, stop=True,
                                                  skip_group_check=True)
                        mm.then_inc(a_s, 1)

            def att_max(b, p):
                pe.wait_ge(a_mn, b + 1)
                for qt in range(TB):
                    mm = nc.tensor.transpose(bank[0][0:NH, ts(qt, P)], mxn[:, qt, :, :].rearrange("p z m -> p (z m)"), ident[:, :])
                mm.then_inc(a_mt, 1)

            def att_heads(b, p, k, last, counts=None):
                TM = TR + 3

                def far(g):
                    if g == 0:
                        pe.wait_ge(a_va, b + 1 if last else b + 2)
                    else:
                        pe.wait_ge(a_ef, G * b + g)
                    nc.tensor.matmul(bank[1][:, :], identb[:, :], far_k, start=True, stop=False, skip_group_check=True)
                    for r in range(R):
                        h_ = R * g + r
                        at = 64 * (h_ % 2)
                        mm = nc.tensor.matmul(bank[1][32 * r:32 * r + KS_N, :], ks[at:at + TM, p, h_ // 2, 0:L:STRIDE],
                                              qs[at:at + TM, p, h_ // 2, :], start=False, stop=True, skip_group_check=True)
                    mm.then_inc(a_tf, 1)

                def near(h_):
                    if h_ >= 2:
                        pe.wait_ge(a_e, NH * b + h_ - 1)
                    else:
                        pe.wait_ge(a_mx, NH * (b + 1))
                    sc = score[h_ % 2]
                    for c in range(2):
                        nc.tensor.matmul(sc[:, 2 * c:2 * c + 2, :], identb[:, :],
                                         band_k[:, None, :].to_broadcast([P, 2, BAND]), start=True, stop=False,
                                         skip_group_check=True)
                    at = 64 * (h_ % 2)
                    for kt in range(TB):
                        lo, hi = reach[kt]
                        q0 = P * kt - WINDOW
                        mm = nc.tensor.matmul(sc[:, kt, lo:hi], ks[at:at + TM, p, h_ // 2, ts(kt, P)],
                                              qs[at:at + TM, p, h_ // 2, q0 + lo:q0 + hi], start=False, stop=True,
                                              skip_group_check=True)
                    mm.then_inc(a_t, 1)

                def sums(h_):
                    g, r = h_ // R, h_ % R
                    acc = bank[6 + g % 2]
                    if r == 0:
                        if counts and g == 1:
                            pe.wait_ge(s_cnt, 2 * stages[:counts].count("moe") + 1)
                        pe.wait_ge(a_ef, G * b + g + 1)
                        if not (isinstance(b, int) and b == 0 and g < 2):
                            pe.wait_ge(a_ot, G * b + g - 1)
                    pe.wait_ge(a_e, NH * b + h_ + 1)
                    for kt in range(TB):
                        lo, hi = reach[kt]
                        q0 = P * kt - WINDOW
                        nc.tensor.matmul(acc[ts(r, 32), q0 + lo:q0 + hi], va[:, p, kt, h_, :],
                                         pt[:, h_ % 2, BAND * kt + lo:BAND * kt + hi], start=(kt == 0), stop=False,
                                         skip_group_check=True)
                    nc.tensor.matmul(acc[ts(r, 32), :], vs_[ts(r, 32), p, g, :], pts[ts(r, 32), g % 2, :],
                                     start=False, stop=True, skip_group_check=True).then_inc(a_pv, 1)

                pe.wait_ge(a_ml[p], 96 * (k + 1))
                for h_ in range(NH):
                    if h_ % R == 0:
                        far(h_ // R)
                    near(h_)
                    if h_:
                        sums(h_ - 1)
                    if counts and h_ == 3:
                        moe_counts(counts, 0)
                    if h_ >= R + 2 and (h_ - R - 2) % R == 0:
                        att_spread(b, (h_ - R - 2) // R, last)
                sums(NH - 1)

            def att_spread(b, g, last):
                pe.wait_ge(a_ot, G * b + g + 1)
                if g == 0 and isinstance(b, int) and b == 0:
                    pe.wait_ge(a_ma, 1)
                elif g == 0:
                    pe.wait_ge(a_res, b)
                elif g == G - 1 and not last:
                    pe.wait_ge(a_ma, 3 * (b + 1) + 1)
                else:
                    pe.wait_ge(a_rd, G * b + g)
                nc.tensor.matmul(bank[0][:, :], den_pick[:, :], ots[:, g % 2, :], start=True, stop=True).then_inc(a_dn, 1)

            def att_out(b):
                pe.wait_ge(a_on, G * (b + 1))
                for t in range(TB):
                    nc.tensor.matmul(bank[0][:, ts(t, P)], ones_row[:, :], bo_row[:, :], start=True, stop=False,
                                     skip_group_check=True)
                    for g in range(G):
                        mm = nc.tensor.matmul(bank[0][:, ts(t, P)], otn[:, g, ts(t, P)], wo_sb[:, g, :], start=False,
                                              stop=(g == G - 1), skip_group_check=True)
                mm.then_inc(a_op, 1)

            def att_step(b, p, k, project=True, between=None):
                att_heads(b, p, k, False)
                att_scores(b + 1, 1 - p, k + p, between)
                att_max(b + 1, 1 - p)
                att_spread(b, G - 1, False)
                if project:
                    att_project(b + 2, p)
                att_out(b)

            for k, stage in enumerate(stages):
                layer_norms(k)
                if stage == "ssm":
                    pe.wait_ge(s_xnT, B * (k + 1))
                    pe.wait_ge(s_w, 16 * 18)
                    pe.wait_ge(s_diag, J * KC)
                    pe.wait_ge(s_cst, 6)
                    for n in range(NS):
                        ssm_prepare(0, 0, n)
                    ssm_batch(0, 0, True, False)
                    with pe.Fori(0, (B - 2) // 2) as i:
                        ssm_batch(2 * i + 1, 1, False, False)
                        ssm_batch(2 * i + 2, 0, False, False)
                    along = {}
                    if early(k + 1):
                        def turn(b):
                            pe.wait_ge(s_unita, 9 * B)
                            transpose(k + 1, b, 6 + b % 2, 2)

                        along = {3: lambda: moe_logits(k + 1, 0), 6: lambda: moe_counts(k + 1, 0)}
                        for n in range(2):
                            along[1 + n] = lambda n=n: [turn(b) for b in (2 * n, 2 * n + 1)]
                    ssm_batch(B - 1, 1, False, True, along)
                elif stage == "moe":
                    along = {}
                    if early(k):
                        along = {7: lambda: moe_logits(k, 1), 11: lambda: moe_counts(k, 1)}
                        for b in range(B // 2, B):
                            along[b - B // 2 + 3] = lambda b=b: transpose(k, b, 7, 1)
                    moe_blocks(stages[:k].count("moe"), 0, along)
                    moe_blocks(stages[:k].count("moe"), 1)
                else:
                    pe.wait_ge(a_wo, 16 * R)
                    pe.wait_ge(s_cst, 7)
                    pe.wait_ge(s_xnT, B * (k + 1))
                    att_scores(0, 0, 0)
                    att_max(0, 0)
                    att_project(1, 1)
                    att_step(0, 0, 0)
                    with pe.Fori(0, (B - 4) // 2) as i:
                        att_step(2 * i + 1, 1, i)
                        att_step(2 * i + 2, 0, i + 1)
                    att_step(B - 3, 1, B // 2 - 2)
                    follow = k + 1 < len(stages)

                    def next_first_half():
                        pe.wait_ge(a_ot, G * (B - 1))
                        transposes(k + 1, 0, 6)
                        moe_logits(k + 1, 0)

                    att_step(B - 2, 0, B // 2 - 1, False, next_first_half if follow else None)
                    att_heads(B - 1, 1, B // 2 - 1, True, k + 1 if follow else None)
                    att_spread(B - 1, G - 1, True)
                    att_out(B - 1)

        @block.vector
        def _(dve):
            vec = nc.vector

            def statistics(k, c):
                if k and stages[k - 1] == "ssm":
                    dve.wait_ge(s_res, B // 2 * (c + 1))
                elif k and stages[k - 1] == "moe":
                    dve.wait_ge(s_ad, T * stages[:k].count("moe") - (TH if c == 0 else 0))
                elif k:
                    dve.wait_ge(a_res, B // 2 * (c + 1))
                for t in range(TH * c, TH * (c + 1)):
                    if k == 0 and t % (T // 4) == 0:
                        dve.wait_ge(s_x[4 * t // T], 16)
                    vec.bn_stats(stats[:, t, :], X[:, t, :]).then_inc(s_lnst, 1)

            def variances(k, c):
                dve.wait_ge(s_lnst, T * k + TH * (c + 1))
                for t in range(TH * c, TH * (c + 1)):
                    vs = vec.bn_aggr(mv[:, t, :], stats[:, t, :])
                vs.then_inc(s_var, 1)

            def normalise(k, c):
                moe = stages[k] == "moe"
                dve.wait_ge(s_std, 2 * k + c + 1)
                vec.reciprocal(rstd[:, ts(c, TH)], std[:, ts(c, TH)]).then_inc(s_rstd, 1)
                dve.wait_ge(s_rstd, 2 * k + c + 1)
                for b in range(c * B // 2, (c + 1) * B // 2):
                    if B * k + b >= 2 and not moe:
                        dve.wait_ge(s_xt, B * k + b - 1)
                    for t in range(TB):
                        g = b * TB + t
                        dst = xna[c][:, g % TH, :] if moe else xn[:, b % 2, t, :]
                        vs = vec.tensor_scalar(dst, X[:, g, :], mv[:, g, 0:1], rstd[:, g:g + 1],
                                               ALU.subtract, ALU.mult)
                    vs.then_inc(s_xn, 1)

            def layer_norm(k, c):
                statistics(k, c)
                variances(k, c)
                normalise(k, c)
                if stages[k] == "moe":
                    moe_route(stages[:k].count("moe"), c)

            def ssm_dt(b, p):
                dve.wait_ge(s_soft, 3 * b + 3)
                if not (isinstance(b, int) and b < 2):
                    dve.wait_ge(s_da, 2 * NS * (b - 1))
                vec.scalar_tensor_tensor(out=dt[:, p, :, :], in0=pre_dt[:, :, :], scalar=0.0, in1=soft[:, :, :],
                                         op0=ALU.max, op1=ALU.add).then_inc(s_dt, 1)

            def ssm_parts(b, p):
                dve.wait_ge(s_bcs, 3 * b + 3)
                vec.tensor_copy(bc3[32:64, p, :], bc_p2[32:64, :])
                vec.tensor_copy(bc3[64:96, p, :], bc_r2[64:96, :]).then_inc(s_bc3, 1)

            def ssm_hc(b, n, q):
                dve.wait_ge(s_cb, NS * b + n + 1)
                dve.wait_ge(s_h, 2 * (NS * b + n + 1))
                if not (isinstance(b, int) and b == 0 and n < 2):
                    dve.wait_ge(s_y, NS * b + n - 1)
                vec.tensor_tensor(hc[:, q, :, :], h[:, q, :, :], bank_c[n % 2][:, None, :].to_broadcast([P, J, L]),
                                  ALU.mult).then_inc(s_hc, 1)

            def ssm_finish(b, p):
                dve.wait_ge(s_y, NS * (b + 1))
                for j in range(J):
                    vs = vec.scalar_tensor_tensor(out=gated[:, j, :], in0=act_x[:, p, j, :], scalar=d_skip_sb[:, j:j + 1],
                                                  in1=bank_y[j][:, :], op0=ALU.mult, op1=ALU.add)
                vs.then_inc(s_yd, 1)
                dve.wait_ge(s_yd, b + 1)
                vec.tensor_tensor(gated[:, :, :], gated[:, :, :], gate[:, p, :, :], ALU.mult).then_inc(s_gt, 1)

            def ssm_residual(b):
                dve.wait_ge(s_op, b + 1)
                xs = X[:, ts(b, TB), :]
                vec.tensor_tensor(xs, xs, bank_pre[0][:, :].rearrange("p (t d) -> p t d", t=TB), ALU.add).then_inc(s_res, 1)

            def ssm_batch(b, p, first, last, along=None):
                def step(n):
                    for j in range(J):
                        dve.wait_ge(s_da, 2 * (NS * b + n) + j + 1)
                        if j == 0:
                            dve.wait_ge(s_dbu, NS * b + n + 1)
                            if not (first and n < 2):
                                dve.wait_ge(s_hc, NS * b + n - 1)
                        vec.tensor_tensor_scan(h[:, n % 2, j, :], decay[n % DECAYS][j], dbu[:, n % 2, j, :], 0.0,
                                               ALU.mult, ALU.add).then_inc(s_h, 1)
                    if n:
                        ssm_hc(b, n - 1, (n - 1) % 2)
                    elif not first:
                        ssm_hc(b - 1, NS - 1, 1)
                    if not first and n == 1:
                        ssm_finish(b - 1, 1 - p)
                    if not first and n == 8:
                        ssm_residual(b - 1)
                    if not last and n == 13:
                        ssm_dt(b + 1, 1 - p)
                    if not last and n == 11:
                        ssm_parts(b + 1, 1 - p)

                steps = iter(range(NS))
                if along:
                    along(lambda: step(next(steps)))
                for n in steps:
                    step(n)
                if last:
                    ssm_hc(b, NS - 1, 1)
                    ssm_finish(b, p)
                    ssm_residual(b)

            def moe_route(m, c, pause=None, pauses=()):
                def part(i):
                    if i in pauses:
                        pause()

                q = 2 * m + c
                n = [ROUTE_STEPS * q]

                def then(ins):
                    n[0] += 1
                    ins.then_inc(s_rt, 1)
                    dve.wait_ge(s_rt, n[0])

                big = lambda a: a[:, :, None].to_broadcast([P, TH, E])
                fallb = fall[:, None, :].to_broadcast([P, TH, E])
                tile_first = lambda a: a.rearrange("p e t -> p t e")
                expert_first = lambda a: a.rearrange("p (t e) -> p e t", e=E)
                dve.wait_ge(s_mc, 16)
                dve.wait_ge(s_lg, q + 1)
                then(vec.tensor_tensor(logits, bank[7][:, 0:TH * E].rearrange("p (t e) -> p t e", e=E),
                                       rb_sb[:, None, :].to_broadcast([P, TH, E]), ALU.add))
                then(vec.tensor_reduce(top[:, 0, :], logits, AX.X, ALU.max))
                then(vec.tensor_tensor(one1, logits, big(top[:, 0, :]), ALU.is_equal))
                part(1)
                then(vec.tensor_tensor(lrank, one1, fallb, ALU.mult))
                then(vec.tensor_reduce(top[:, 4, :], lrank, AX.X, ALU.max))
                then(vec.tensor_tensor(one1, fallb, big(top[:, 4, :]), ALU.is_equal))
                then(vec.scalar_tensor_tensor(out=rest[:, :, :], in0=one1, scalar=-3.0e38, in1=logits,
                                              op0=ALU.mult, op1=ALU.add))
                then(vec.tensor_reduce(top[:, 1, :], rest[:, :, :], AX.X, ALU.max))
                vec.tensor_tensor(top[:, 2, :], top[:, 1, :], top[:, 0, :], ALU.subtract).then_inc(s_df, 1)
                part(2)
                then(vec.tensor_tensor(one2, rest[:, :, :], big(top[:, 1, :]), ALU.is_equal))
                then(vec.tensor_tensor(lrank, one2, fallb, ALU.mult))
                then(vec.tensor_reduce(top[:, 5, :], lrank, AX.X, ALU.max))
                then(vec.tensor_tensor(one2, fallb, big(top[:, 5, :]), ALU.is_equal))
                vec.tensor_tensor(both, one1, one2, ALU.add).then_inc(s_both, 1)
                part(3)
                dve.wait_ge(s_re, q + 1)
                then(vec.tensor_scalar(top[:, 4, :], top[:, 3, :], 1.0, None, ALU.add))
                then(vec.reciprocal(pick_w[:, c, 0, :], top[:, 4, :]))
                vec.tensor_tensor(pick_w[:, c, 1, :], top[:, 3, :], pick_w[:, c, 0, :], ALU.mult)
                part(4)
                dve.wait_ge(s_pr, q + 1)
                vec.tensor_copy(counts[:, :, :], bank[7][:, TH * E:3 * TH * E].rearrange("p (a n) -> p a n", a=2)).then_inc(s_cnt, 1)
                dve.wait_ge(s_cnt, q + 1)
                then(vec.tensor_copy(tot[:, :, :], expert_first(counts[:, 0, :])))
                then(vec.tensor_tensor_scan(upto[:, :, :].rearrange("p e t -> p (e t)"), keep,
                                            tot[:, :, :].rearrange("p e t -> p (e t)"), 0.0, ALU.mult, ALU.add))
                then(vec.tensor_tensor(over, upto[:, :, TH - 1:TH].to_broadcast([P, E, TH]),
                                       thresholds[:, None, :].to_broadcast([P, E, TH]), ALU.is_gt))
                part(5)
                then(vec.tensor_reduce(n_blocks[:, :], over, AX.X, ALU.add))
                then(vec.tensor_tensor_scan(ends[:, :], ones_e, n_blocks[:, :], 0.0, ALU.mult, ALU.add))
                then(vec.tensor_tensor(starts[:, :], ends[:, :], n_blocks[:, :], ALU.subtract))
                then(vec.tensor_tensor(upto[:, :, :], upto[:, :, :], tot[:, :, :], ALU.subtract))
                then(vec.scalar_tensor_tensor(out=place, in0=starts[:, :, None].to_broadcast([P, E, TH]),
                                              scalar=float(P), in1=upto[:, :, :], op0=ALU.mult, op1=ALU.add))
                part(6)
                then(vec.tensor_tensor(place, place, expert_first(counts[:, 1, :]), ALU.add))
                for k, one in enumerate((one1, one2)):
                    then(vec.tensor_tensor(placed[:, k, :, :], one, tile_first(place), ALU.mult))
                then(vec.tensor_reduce(row_f[:, :, :], placed[:, :, :, :], AX.X, ALU.add))
                vec.tensor_copy(row[:, c, :, :], row_f[:, :, :])
                part(7)
                then(vec.tensor_tensor(ended, ends[0:1, None, :].to_broadcast([1, NB, E]),
                                       counting[0:1, :, None].to_broadcast([1, NB, E]), ALU.is_le))
                vec.memset(expert_f[:, 0:2], 0.0)
                then(vec.tensor_reduce(expert_f[:, 2:], ended, AX.X, ALU.add))
                then(vec.tensor_scalar(expert_f[:, :], expert_f[:, :], float(E - 1), None, ALU.min))
                digit = lambda r: expert_f[:, r:r + (WORDS - 1) * (DIGITS - 1) + 1:DIGITS - 1]
                then(vec.tensor_copy(word[:, :], digit(DIGITS - 1)))
                for r in range(DIGITS - 2, -1, -1):
                    then(vec.scalar_tensor_tensor(out=word[:, :], in0=word[:, :], scalar=float(E), in1=digit(r),
                                                  op0=ALU.mult, op1=ALU.add))
                vec.tensor_copy(expert[:, c, :], word[:, :]).then_inc(s_row, 1)
                assert n[0] == ROUTE_STEPS * (q + 1), n[0]

            def moe_add(m, c, t, r):
                n = (2 * m + c) * TH // 2 + r
                for k in range(2):
                    if k:
                        dve.wait_ge(s_a1, n + 1)
                    for g in range(2):
                        xs = X[:, ds(TH * c + t + g, 1), :]
                        vs = vec.scalar_tensor_tensor(out=xs, in0=yg[c][:, k, ds(t + g, 1), :],
                                                      scalar=pick_w[:, c, k, ds(t + g, 1)], in1=xs,
                                                      op0=ALU.mult, op1=ALU.add)
                    vs.then_inc(s_ad if k else s_a1, 2 if k else 1)

            def moe_blocks(m, c, along=None):
                q = 2 * m + c
                base = q * NB

                def hidden(j, p):
                    dve.wait_ge(s_up, base + j + 1)
                    dve.wait_ge(s_sg, base + j + 1)
                    if not (isinstance(base + j, int) and base + j < 2):
                        dve.wait_ge(s_th, base + j - 1)
                    vec.tensor_tensor(hid[:, p, :], sg[:, p, :], bank[2 + p][:, :], ALU.mult).then_inc(s_hd, 1)

                def result(j, p):
                    dve.wait_ge(s_dn, base + j + 1)
                    if not (q == 0 and isinstance(j, int) and j < 2):
                        dve.wait_ge(s_ys[p], 16 * q * OF_PARITY[p] + (j - p) * 8)
                    vec.tensor_copy(y_sb[:, p, :], bank[6][:, 0:P]).then_inc(s_yb, 1)

                def step(j, p):
                    hidden(j, p)
                    if not (isinstance(j, int) and j == 0):
                        result(j - 1, 1 - p)

                peeled = 18 if along else 4
                blocks = iter(range(peeled))

                def pause():
                    j = next(blocks)
                    step(j, j % 2)

                if along:
                    pause()
                    along(pause)
                for j in blocks:
                    step(j, j % 2)
                pairs, adds = (NB - 1 - peeled) // 2, TH // 2 if c else 0
                with dve.Fori(0, pairs - adds) as i:
                    for p in range(2):
                        step(2 * i + peeled + p, p)
                if adds:
                    for g in range(TB):
                        dve.wait_ge(s_yg[g], 16 * 2 * TB * q)
                    with dve.Fori(0, adds) as i:
                        for p in range(2):
                            step(2 * (i + pairs - adds) + peeled + p, p)
                        moe_add(m, 0, 2 * i, i)
                step(NB - 1, 0)
                result(NB - 1, 0)

            def moe_finish(m):
                for r in range(TH // 2):
                    if r % 2 == 0:
                        dve.wait_ge(s_yg[r // 2], 16 * 2 * TB * (2 * m + 2))
                    moe_add(m, 1, 2 * r, r)

            def att_inputs(b, p):
                dve.wait_ge(a_qk, b + 1)
                if not (isinstance(b, int) and b == 0):
                    dve.wait_ge(a_sp, 2 * b)
                vec.tensor_scalar(qk_f[:, 0, :], bank[6][:, :], bqk_sb[:, 0:1], DH ** -0.5, ALU.add, ALU.mult)
                vec.tensor_scalar(qk_f[:, 1, :], bank[7][:, :], bqk_sb[:, 1:2], None, ALU.add).then_inc(a_qf, 1)
                dve.wait_ge(a_v, b + 1)
                if not (isinstance(b, int) and b < 2):
                    dve.wait_ge(a_pv, NH * (b - 1))
                vec.tensor_tensor(va[:, p, :, :, 0:DH], bank[2][:, :].rearrange("p (t h d) -> p t h d", t=TB, h=NH),
                                  bv_all[:, None, :, :].to_broadcast([P, TB, NH, DH]), ALU.add)
                for r in range(R):
                    rows = slice(32 * r, 32 * r + KS_N)
                    vi = vec.tensor_tensor(vs_[rows, p, :, 0:DH], bank[4][rows, 0:G * DH].rearrange("p (g d) -> p g d", g=G),
                                           bv_str[rows, :, :], ALU.add)
                vi.then_inc(a_va, 1)

            def att_maxima(b):
                if not (isinstance(b, int) and b == 0):
                    dve.wait_ge(a_mn, b)
                for z in range(2):
                    dve.wait_ge(a_ss, 2 * b + z + 1)
                    vec.tensor_reduce(mxs[:, :, z, :], bank[z][:, :].rearrange("p (q m k) -> p q m k", q=TB, k=KS_N),
                                      AX.X, ALU.max).then_inc(a_ms, 1)
                for qt in range(TB):
                    lo, hi = reach[qt]
                    for g in range(G):
                        dve.wait_ge(a_s, NH * b + G * qt + g + 1)
                        vec.tensor_reduce(mxw[:, qt, :, 2 * g:2 * g + 2],
                                          score[(G * qt + g) % 2][:, :, lo:hi].rearrange("p (z m) k -> p z m k", z=2),
                                          AX.X, ALU.max).then_inc(a_mx, 1)
                dve.wait_ge(a_mx, NH * (b + 1))
                dve.wait_ge(a_ms, 2 * (b + 1))
                if not (isinstance(b, int) and b == 0):
                    dve.wait_ge(a_mt, b)
                vec.tensor_tensor(mxs[:, :, :, :], mxw[:, :, :, :], mxs[:, :, :, :], ALU.max).then_inc(a_mm, 1)
                dve.wait_ge(a_mm, b + 1)
                vec.tensor_scalar(mxn[:, :, :, :], mxs[:, :, :, :], -1.0, None, ALU.mult).then_inc(a_mn, 1)

            def att_normalise(b, g):
                dve.wait_ge(a_dn, G * b + g + 1)
                if not (isinstance(b, int) and b == 0 and g == 0):
                    dve.wait_ge(a_on, G * b + g)
                vec.reciprocal(rden[:, :], bank[0][:, :]).then_inc(a_rd, 1)
                dve.wait_ge(a_rd, G * b + g + 1)
                vec.tensor_tensor(otn[:, g, :], ots[:, g % 2, :], rden[:, :], ALU.mult).then_inc(a_on, 1)

            def att_residual(b):
                dve.wait_ge(a_op, b + 1)
                xs = X[:, ts(b, TB), :]
                vec.tensor_tensor(xs, xs, bank[0][:, :].rearrange("p (t d) -> p t d", t=TB), ALU.add).then_inc(a_res, 1)

            def att_step(b, p, inputs=True, follow=None):
                for g in range(G - 1):
                    att_normalise(b, g)
                    if follow:
                        (statistics, variances, normalise)[g](follow, 0)
                att_maxima(b + 1)
                att_normalise(b, G - 1)
                if inputs:
                    att_inputs(b + 2, p)
                att_residual(b)

            def att_begin():
                if stages[0] != "att":
                    for p in range(2):
                        dve.wait_ge(s_ys[p], 16 * OF_PARITY[p] * 2)
                vec.memset(wo_sb[:, :, :], 0.0).then_inc(a_cst, 1)
                vec.memset(va[:, :, :, :, :], 0.0).then_inc(a_cst, 1)
                vec.memset(vs_[:, :, :, :], 0.0).then_inc(a_cst, 1)
                vec.memset(ks[:, :, :, :], 1.0).then_inc(a_cst, 1)
                dve.wait_ge(a_cst, 4)
                vec.memset(va[:, :, :, :, DH:DH + 1], 1.0).then_inc(a_cst, 1)
                for r in range(R):
                    vec.memset(vs_[32 * r:32 * r + KS_N, :, :, DH:DH + 1], 1.0).then_inc(a_cst, 1)
                dve.wait_ge(a_w, 16 * 10)
                vec.tensor_copy(consts_b[:, :], consts_f).then_inc(a_cst, 1)
                dve.wait_ge(a_cst, 10)
                att_inputs(0, 0)

            def begin(k):
                layer_norm(k, 0)
                if stages[k] == "att":
                    att_begin()

            begin(0)
            for k, stage in enumerate(stages):
                if not early(k):
                    layer_norm(k, 1)
                if stage == "ssm":
                    dve.wait_ge(s_w, 16 * 18)
                    dve.wait_ge(s_cst, 3)
                    for j in range(J):
                        for t in range(KC):
                            vec.tensor_scalar(conv_diag[:, j, t, :], ident[:, :], conv_w_sb[:, j, t:t + 1], None,
                                              ALU.mult).then_inc(s_diag, 1)
                    ssm_dt(0, 0)
                    ssm_parts(0, 0)
                    ssm_batch(0, 0, True, False)
                    with dve.Fori(0, (B - 2) // 2) as i:
                        ssm_batch(2 * i + 1, 1, False, False)
                        ssm_batch(2 * i + 2, 0, False, False)

                    def first_half(pause):
                        statistics(k + 1, 0)
                        variances(k + 1, 0)
                        pause()
                        normalise(k + 1, 0)
                        for _ in range(4):
                            pause()
                        moe_route(0, 0, pause, (2, 4, 6))

                    ssm_batch(B - 1, 1, False, True, first_half if early(k + 1) else None)
                    if k + 1 < len(stages) and not early(k + 1):
                        begin(k + 1)
                elif stage == "moe":
                    m = stages[:k].count("moe")

                    def second_half(pause):
                        statistics(k, 1)
                        pause()
                        variances(k, 1)
                        pause()
                        normalise(k, 1)
                        for _ in range(6):
                            pause()
                        moe_route(m, 1, pause, range(1, 8))

                    moe_blocks(m, 0, second_half if early(k) else None)
                    moe_blocks(m, 1)
                    if k + 1 < len(stages):
                        begin(k + 1)
                    moe_finish(m)
                else:
                    att_maxima(0)
                    att_inputs(1, 1)
                    att_step(0, 0)
                    with dve.Fori(0, (B - 4) // 2) as i:
                        att_step(2 * i + 1, 1)
                        att_step(2 * i + 2, 0)
                    att_step(B - 3, 1)
                    follow = k + 1 if k + 1 < len(stages) else None
                    att_step(B - 2, 0, False, follow)
                    if follow:
                        moe_route(stages[:k].count("moe"), 0)
                    for g in range(G):
                        att_normalise(B - 1, g)
                    att_residual(B - 1)


_INS = ["L0_attn_a_x", "L0_attn_a_W_in", "L0_attn_a_b_in", "L0_attn_a_W_gate", "L0_attn_a_b_gate",
        "L0_attn_a_conv_w", "L0_attn_a_conv_b", "L0_attn_a_A_log", "L0_attn_a_D_skip", "L0_attn_a_W_delta",
        "L0_attn_a_b_delta", "L0_attn_a_W_B", "L0_attn_a_W_C", "L0_attn_a_W_out", "L0_attn_a_b_out",
        "L0_attn_b_w_qkv", "L0_attn_b_b_qkv", "L0_attn_b_w_out", "L0_attn_b_b_out", "L0_ffn_wg", "L0_ffn_bg",
        "L0_ffn_Wgate", "L0_ffn_Wup", "L0_ffn_Wdown"]


def kernel(**inputs):
    import numpy as _np
    import concourse.bacc as _bacc
    from concourse import mybir as _mybir
    from concourse.bass_utils import run_bass_kernel_spmd as _run

    nc = _bacc.Bacc("TRN2", target_bir_lowering=False, num_devices=1)
    arrays, args = {}, []
    for name in _INS:
        a = _np.asarray(inputs[name])
        if name in ("L0_ffn_Wgate", "L0_ffn_Wup"):
            a = a.transpose(2, 0, 1)
        elif name == "L0_ffn_Wdown":
            a = a.reshape(a.shape[0], a.shape[1], -1, 128).transpose(3, 0, 2, 1)
        a = _np.ascontiguousarray(a)
        arrays[f"in_{name}_dram"] = a
        args.append(nc.dram_tensor(f"in_{name}_dram", a.shape, _mybir.dt.from_np(a.dtype), kind="ExternalInput").ap())
    p, c, q = _np.arange(128)[:, None], _np.arange(256)[None, :], _np.arange(512)[None, :]
    near = (c - p >= 0) & (c - p <= 128)
    tile = (p % 32) // 4
    covered = (q >= 128 * tile - 64) & (q < 128 * tile + 192) & (p % 32 < 16)
    neg = lambda seen: _np.where(seen, 0.0, -1.0e30)
    spread = (p == 32 * (_np.arange(128)[None, :] // 32) + 8) * 1.0
    consts = _np.concatenate([neg(near | (c % 32 == 0)), neg(near | (p % 32 == 0)), neg(~covered), spread], axis=1)
    arrays["att_consts"] = _np.ascontiguousarray(consts.astype(_np.float32))
    args.append(nc.dram_tensor("att_consts", consts.shape, _mybir.dt.float32, kind="ExternalInput").ap())
    full = lambda a: _np.broadcast_to(_np.asarray(a, _np.float32)[None, :], (128, len(a)))
    routing = _np.concatenate([(p < _np.arange(128)[None, :]) * 1.0, _np.ones((128, 128)),
                               full((_np.arange(8 * 16) % 16 > 0) * 1.0), full(128 * _np.arange(16)),
                               full(_np.arange(39)), full(8 - _np.arange(8)), full(_np.ones(8))], axis=1)
    arrays["moe_consts"] = _np.ascontiguousarray(routing.astype(_np.float32))
    args.append(nc.dram_tensor("moe_consts", routing.shape, _mybir.dt.float32, kind="ExternalInput").ap())
    shape = inputs["L0_attn_a_x"].shape
    args.append(nc.dram_tensor("out_0_dram", shape, _mybir.dt.float32, kind="ExternalOutput").ap())
    hybrid_layer_kernel(nc, *args)
    r = _run(nc, [arrays], core_ids=[0])
    return r.results[0]["out_0_dram"]
```
